# Optimizing a Trainium2 kernel written in Bass

```python
import numpy as np
import jax
import jax.numpy as jnp

def _softmax(x, axis=-1):
    return jax.nn.softmax(x, axis=axis)

def _gelu(x):
    return jax.nn.gelu(x, approximate=True)

def _silu(x):
    return jax.nn.silu(x)

def _sigmoid(x):
    return jax.nn.sigmoid(x)

def _layernorm(x, axis=-1, eps=1e-05):
    m = jnp.mean(x, axis=axis, keepdims=True)
    v = jnp.var(x, axis=axis, keepdims=True)
    return (x - m) / jnp.sqrt(v + eps)

def _scatter_add(tgt, idx, src, axis=0):
    return tgt.at[idx].add(src)

def _segment_sum(src, seg, n):
    return jax.ops.segment_sum(src, seg, n)
kernel_name = 'mk_decoder_postln_d2_seqx_r4_038e91'

def setup_inputs(seed: int=0):
    np.random.seed(seed)
    _w = jnp.asarray

    def _rec_inputs():
        import jax
        import jax.numpy as jnp
        _rk = jax.random.key(seed)
        x = -0.0005207 + 1.001 * jax.random.normal(jax.random.fold_in(_rk, 1), (32, 256, 256), jnp.float32)
        _lenS = 256 - jax.random.randint(jax.random.fold_in(_rk, 7), (32,), 0, max(1, 256 // 4) + 1, jnp.int32)
        _lenS2 = 77 - jax.random.randint(jax.random.fold_in(_rk, 8), (32,), 0, max(1, 77 // 4) + 1, jnp.int32)
        _ctx_1024P = jax.random.normal(jax.random.fold_in(_rk, 11), (32, 16, 256), jnp.float32)
        _ctx_1024c = jax.random.dirichlet(jax.random.fold_in(_rk, 511), 0.3 * jnp.ones((16,), jnp.float32), (32, 77))
        _ctx_1024t = jnp.einsum('bsk,bkd->bsd', _ctx_1024c, _ctx_1024P)
        _ctx_1024t = _ctx_1024t * jax.lax.rsqrt(jnp.mean(jnp.square(_ctx_1024t)) + 1e-12) * 0.953939
        ctx_1024 = -1.52775e-05 + 0.999936 * (_ctx_1024t + 0.3 * jax.random.normal(jax.random.fold_in(_rk, 611), (32, 77, 256), jnp.float32))
        _validS = jnp.arange(256)[None, :] < _lenS[:, None]
        _validS2 = jnp.arange(77)[None, :] < _lenS2[:, None]
        _causal = jnp.tril(jnp.ones((256, 256), dtype=bool))
        mask_BxS2_ik0 = jnp.where(jnp.broadcast_to(_validS2[:, :], (32, 77)), 0, 1).astype(jnp.int32)
        return (x, ctx_1024, mask_BxS2_ik0)
    x, ctx_1024, mask_BxS2_ik0 = _rec_inputs()

    def _L0_attn_setup():
        import jax, jax.numpy as jnp
        import numpy as np
        EMBED_DIM = 256
        NUM_HEADS = 16
        BATCH = 4
        SEQ = 1024
        key = jax.random.key(seed)
        ks = jax.random.split(key, 5)
        scale = 0.02
        E = EMBED_DIM
        x = jax.random.normal(ks[0], (BATCH, SEQ, E), dtype=jnp.float32)
        Wq = jax.random.normal(ks[1], (E, E), dtype=jnp.float32) * scale
        Wk = jax.random.normal(ks[2], (E, E), dtype=jnp.float32) * scale
        Wv = jax.random.normal(ks[3], (E, E), dtype=jnp.float32) * scale
        Wo = jax.random.normal(ks[4], (E, E), dtype=jnp.float32) * scale
        z = jnp.zeros((E,), dtype=jnp.float32)
        return {'x': x, 'Wq': Wq, 'bq': z, 'Wk': Wk, 'bk': z, 'Wv': Wv, 'bv': z, 'Wo': Wo, 'bo': z}
    _L0_attn_all = _L0_attn_setup()
    _L0_attn_in = {k: v for k, v in _L0_attn_all.items() if k in ('Wq', 'bq', 'Wk', 'bk', 'Wv', 'bv', 'Wo', 'bo')}
    del _L0_attn_all

    def _L0_xattn_setup():
        import jax, jax.numpy as jnp
        import numpy as np
        DIM = 256
        HEADS = 16
        HEAD_DIM = DIM // HEADS
        SCALE = HEAD_DIM ** (-0.5)
        MASK_FILL = -1000000000.0

        def layer_norm(x, gamma, beta, eps=1e-05):
            mu = jnp.mean(x, axis=-1, keepdims=True)
            var = jnp.var(x, axis=-1, keepdims=True)
            return (x - mu) * jax.lax.rsqrt(var + eps) * gamma + beta
        key = jax.random.key(seed)
        ks = jax.random.split(key, 10)
        B, N1, N2, C = (8, 64, 1024, DIM)
        s = C ** (-0.5)
        return {'x': jax.random.normal(ks[0], (B, N1, C), jnp.float32), 'kv': jax.random.normal(ks[1], (B, N2, C), jnp.float32), 'padding_mask': jax.random.randint(ks[2], (B, N2), 0, 2, jnp.int32), 'w_q': jax.random.normal(ks[3], (C, C), jnp.float32) * s, 'w_kv': jax.random.normal(ks[4], (C, 2 * C), jnp.float32) * s, 'w_proj': jax.random.normal(ks[5], (C, C), jnp.float32) * s, 'b_proj': jnp.zeros((C,), jnp.float32), 'g_x': jnp.ones((C,), jnp.float32), 'b_x': jnp.zeros((C,), jnp.float32), 'g_kv': jnp.ones((C,), jnp.float32), 'b_kv': jnp.zeros((C,), jnp.float32)}
    _L0_xattn_all = _L0_xattn_setup()
    _L0_xattn_in = {k: v for k, v in _L0_xattn_all.items() if k in ('w_q', 'w_kv', 'w_proj', 'b_proj', 'g_x', 'b_x', 'g_kv', 'b_kv')}
    del _L0_xattn_all

    def _L0_ffn_setup():
        import jax, jax.numpy as jnp
        import numpy as np
        S, B, D, H, DH = (1024, 8, 256, 16, 64)

        def _forward(x, Wg, Wq, bq, Wkv, bkv, Wo, bo, ln_g, ln_b):
            s_len, bsz, d_model = x.shape
            n_head, _, d_head = Wq.shape
            cap = s_len // n_head
            scale = 1.0 / d_head ** 0.5
            h = jnp.transpose(x, (1, 0, 2))
            t = h
            probs = jax.nn.softmax(h @ Wg, axis=-1)
            scores = jnp.transpose(probs, (0, 2, 1))
            _, idx = jax.lax.top_k(scores, cap)
            idx = jnp.sort(idx, axis=-1)
            hg = jnp.take_along_axis(h[:, None, :, :], idx[..., None], axis=2)
            hg = jnp.transpose(hg, (1, 0, 2, 3))
            q = jnp.einsum('hbcd,hde->hbce', hg, Wq) + bq[:, None, None, :]
            kv = jnp.einsum('hbcd,hde->hbce', hg, Wkv) + bkv[:, None, None, :]
            k, v = jnp.split(kv, 2, axis=-1)
            att = jnp.einsum('hbid,hbjd->hbij', q, k) * scale
            p = jax.nn.softmax(att, axis=1)
            av = jnp.einsum('hbij,hbjd->hbid', p, v)
            ao = jnp.einsum('hbid,hde->hbie', av, Wo) + bo
            tok = jnp.transpose(idx, (1, 0, 2))
            b_ids = jnp.arange(bsz)[None, :, None]
            outs = jnp.zeros_like(t).at[b_ids, tok].add(ao)
            y = t + outs
            mu = jnp.mean(y, axis=-1, keepdims=True)
            var = jnp.var(y, axis=-1, keepdims=True)
            yn = (y - mu) * jax.lax.rsqrt(var + 1e-05) * ln_g + ln_b
            return jnp.transpose(yn, (1, 0, 2))
        key = jax.random.key(seed)
        ks = jax.random.split(key, 6)
        s = 0.02
        return {'x': jax.random.normal(ks[0], (S, B, D), jnp.float32), 'attn_mask': jnp.zeros((S, S), jnp.bool_), 'Wg': jax.random.normal(ks[1], (D, H), jnp.float32) * s, 'Wq': jax.random.normal(ks[2], (H, D, DH), jnp.float32) * s, 'bq': jnp.zeros((H, DH), jnp.float32), 'Wkv': jax.random.normal(ks[3], (H, D, 2 * DH), jnp.float32) * s, 'bkv': jnp.zeros((H, 2 * DH), jnp.float32), 'Wo': jax.random.normal(ks[4], (H, DH, D), jnp.float32) * s, 'bo': jnp.zeros((D,), jnp.float32), 'ln_g': jnp.ones((D,), jnp.float32), 'ln_b': jnp.zeros((D,), jnp.float32)}
    _L0_ffn_all = _L0_ffn_setup()
    _L0_ffn_in = {k: v for k, v in _L0_ffn_all.items() if k in ('attn_mask', 'Wg', 'Wq', 'bq', 'Wkv', 'bkv', 'Wo', 'bo', 'ln_g', 'ln_b')}
    del _L0_ffn_all

    def _L1_attn_setup():
        import jax, jax.numpy as jnp
        import numpy as np
        import math
        D_MODEL = 256
        D_STATE = 16
        D_CONV = 4
        EXPAND = 2
        D_INNER = D_MODEL * EXPAND
        EPS = 1e-06
        key = jax.random.key(seed)
        ks = jax.random.split(key, 7)
        B, T = (2, 256)
        x = jax.random.normal(ks[0], (B, T, D_MODEL), jnp.float32)
        g = jnp.ones((D_MODEL,), jnp.float32)
        W_in = jax.random.normal(ks[1], (2 * D_INNER, D_MODEL), jnp.float32) * 0.02
        W_out = jax.random.normal(ks[2], (D_MODEL, D_INNER), jnp.float32) * 0.02
        conv_w = jax.random.normal(ks[3], (D_INNER, D_CONV), jnp.float32) * 0.1
        conv_b = jnp.zeros((D_INNER,), jnp.float32)
        W_x = jax.random.normal(ks[4], (2 * D_STATE + 1, D_INNER), jnp.float32) * 0.02
        W_dt = jax.random.normal(ks[5], (D_INNER, 1), jnp.float32) * 0.1
        b_dt = jnp.full((D_INNER,), math.log(0.001), jnp.float32)
        A_log = jnp.broadcast_to(jnp.log(jnp.arange(1, D_STATE + 1, dtype=jnp.float32))[None, :], (D_INNER, D_STATE)) + jnp.zeros((D_INNER, D_STATE), jnp.float32)
        D = jnp.ones((D_INNER,), jnp.float32)
        return dict(x=x, g=g, W_in=W_in, W_out=W_out, conv_w=conv_w, conv_b=conv_b, W_x=W_x, W_dt=W_dt, b_dt=b_dt, A_log=A_log, D=D)
    _L1_attn_all = _L1_attn_setup()
    _L1_attn_in = {k: v for k, v in _L1_attn_all.items() if k in ('g', 'W_in', 'W_out', 'conv_w', 'conv_b', 'W_x', 'W_dt', 'b_dt', 'A_log', 'D')}
    del _L1_attn_all

    def _L1_xattn_setup():
        import jax, jax.numpy as jnp
        import numpy as np
        D_MODEL = 256
        NUM_HEADS = 16
        HEAD_DIM = D_MODEL // NUM_HEADS

        def _split_heads(x):
            B, S, _ = x.shape
            return x.reshape(B, S, NUM_HEADS, HEAD_DIM).transpose(0, 2, 1, 3)
        key = jax.random.key(seed)
        ks = jax.random.split(key, 11)
        B, S = (2, 512)
        sc = 1.0 / np.sqrt(D_MODEL)
        inp = {'query': jax.random.normal(ks[0], (B, S, D_MODEL), jnp.float32), 'key': jax.random.normal(ks[1], (B, S, D_MODEL), jnp.float32), 'value': jax.random.normal(ks[2], (B, S, D_MODEL), jnp.float32), 'Wq': jax.random.normal(ks[3], (D_MODEL, D_MODEL), jnp.float32) * sc, 'bq': jnp.zeros((D_MODEL,), jnp.float32), 'Wk': jax.random.normal(ks[4], (D_MODEL, D_MODEL), jnp.float32) * sc, 'bk': jnp.zeros((D_MODEL,), jnp.float32), 'Wv': jax.random.normal(ks[5], (D_MODEL, D_MODEL), jnp.float32) * sc, 'bv': jnp.zeros((D_MODEL,), jnp.float32), 'Wo': jax.random.normal(ks[6], (D_MODEL, D_MODEL), jnp.float32) * sc, 'bo': jnp.zeros((D_MODEL,), jnp.float32)}
        return inp
    _L1_xattn_all = _L1_xattn_setup()
    _L1_xattn_in = {k: v for k, v in _L1_xattn_all.items() if k in ('Wq', 'bq', 'Wk', 'bk', 'Wv', 'bv', 'Wo', 'bo')}
    del _L1_xattn_all

    def _L1_ffn_setup():
        import jax, jax.numpy as jnp
        import numpy as np
        HIDDEN = 256
        INNER = 1024

        def _weight_quant(w):
            scale = 1.0 / jnp.clip(jnp.mean(jnp.abs(w)), 1e-05)
            wq = jnp.clip(jnp.round(w * scale), -1.0, 1.0) / scale
            return w + jax.lax.stop_gradient(wq - w)

        def _act_quant(x):
            scale = 127.0 / jnp.clip(jnp.max(jnp.abs(x), axis=-1, keepdims=True), 1e-05)
            xq = jnp.clip(jnp.round(x * scale), -128.0, 127.0) / scale
            return x + jax.lax.stop_gradient(xq - x)

        def _bitlinear(x, w):
            return jnp.einsum('bsi,oi->bso', _act_quant(x), _weight_quant(w))
        key = jax.random.key(seed)
        k0, k1, k2, k3 = jax.random.split(key, 4)
        x = jax.random.normal(k0, (4, 512, HIDDEN), dtype=jnp.float32)
        w_gate = jax.random.normal(k1, (INNER, HIDDEN), dtype=jnp.float32) / np.sqrt(HIDDEN)
        w_up = jax.random.normal(k2, (INNER, HIDDEN), dtype=jnp.float32) / np.sqrt(HIDDEN)
        w_down = jax.random.normal(k3, (HIDDEN, INNER), dtype=jnp.float32) / np.sqrt(INNER)
        return {'x': x, 'w_gate': w_gate, 'w_up': w_up, 'w_down': w_down}
    _L1_ffn_all = _L1_ffn_setup()
    _L1_ffn_in = {k: v for k, v in _L1_ffn_all.items() if k in ('w_gate', 'w_up', 'w_down')}
    del _L1_ffn_all
    return {'x': x, 'ctx_1024': ctx_1024, 'mask_BxS2_ik0': mask_BxS2_ik0, 'L0_attn_Wq': _L0_attn_in['Wq'], 'L0_attn_bq': _L0_attn_in['bq'], 'L0_attn_Wk': _L0_attn_in['Wk'], 'L0_attn_bk': _L0_attn_in['bk'], 'L0_attn_Wv': _L0_attn_in['Wv'], 'L0_attn_bv': _L0_attn_in['bv'], 'L0_attn_Wo': _L0_attn_in['Wo'], 'L0_attn_bo': _L0_attn_in['bo'], 'L0_xattn_w_q': _L0_xattn_in['w_q'], 'L0_xattn_w_kv': _L0_xattn_in['w_kv'], 'L0_xattn_w_proj': _L0_xattn_in['w_proj'], 'L0_xattn_b_proj': _L0_xattn_in['b_proj'], 'L0_xattn_g_x': _L0_xattn_in['g_x'], 'L0_xattn_b_x': _L0_xattn_in['b_x'], 'L0_xattn_g_kv': _L0_xattn_in['g_kv'], 'L0_xattn_b_kv': _L0_xattn_in['b_kv'], 'L0_ffn_attn_mask': _L0_ffn_in['attn_mask'], 'L0_ffn_Wg': _L0_ffn_in['Wg'], 'L0_ffn_Wq': _L0_ffn_in['Wq'], 'L0_ffn_bq': _L0_ffn_in['bq'], 'L0_ffn_Wkv': _L0_ffn_in['Wkv'], 'L0_ffn_bkv': _L0_ffn_in['bkv'], 'L0_ffn_Wo': _L0_ffn_in['Wo'], 'L0_ffn_bo': _L0_ffn_in['bo'], 'L0_ffn_ln_g': _L0_ffn_in['ln_g'], 'L0_ffn_ln_b': _L0_ffn_in['ln_b'], 'L1_attn_g': _L1_attn_in['g'], 'L1_attn_W_in': _L1_attn_in['W_in'], 'L1_attn_W_out': _L1_attn_in['W_out'], 'L1_attn_conv_w': _L1_attn_in['conv_w'], 'L1_attn_conv_b': _L1_attn_in['conv_b'], 'L1_attn_W_x': _L1_attn_in['W_x'], 'L1_attn_W_dt': _L1_attn_in['W_dt'], 'L1_attn_b_dt': _L1_attn_in['b_dt'], 'L1_attn_A_log': _L1_attn_in['A_log'], 'L1_attn_D': _L1_attn_in['D'], 'L1_xattn_Wq': _L1_xattn_in['Wq'], 'L1_xattn_bq': _L1_xattn_in['bq'], 'L1_xattn_Wk': _L1_xattn_in['Wk'], 'L1_xattn_bk': _L1_xattn_in['bk'], 'L1_xattn_Wv': _L1_xattn_in['Wv'], 'L1_xattn_bv': _L1_xattn_in['bv'], 'L1_xattn_Wo': _L1_xattn_in['Wo'], 'L1_xattn_bo': _L1_xattn_in['bo'], 'L1_ffn_w_gate': _L1_ffn_in['w_gate'], 'L1_ffn_w_up': _L1_ffn_in['w_up'], 'L1_ffn_w_down': _L1_ffn_in['w_down']}

def reference(x, ctx_1024, mask_BxS2_ik0, L0_attn_Wq, L0_attn_bq, L0_attn_Wk, L0_attn_bk, L0_attn_Wv, L0_attn_bv, L0_attn_Wo, L0_attn_bo, L0_xattn_w_q, L0_xattn_w_kv, L0_xattn_w_proj, L0_xattn_b_proj, L0_xattn_g_x, L0_xattn_b_x, L0_xattn_g_kv, L0_xattn_b_kv, L0_ffn_attn_mask, L0_ffn_Wg, L0_ffn_Wq, L0_ffn_bq, L0_ffn_Wkv, L0_ffn_bkv, L0_ffn_Wo, L0_ffn_bo, L0_ffn_ln_g, L0_ffn_ln_b, L1_attn_g, L1_attn_W_in, L1_attn_W_out, L1_attn_conv_w, L1_attn_conv_b, L1_attn_W_x, L1_attn_W_dt, L1_attn_b_dt, L1_attn_A_log, L1_attn_D, L1_xattn_Wq, L1_xattn_bq, L1_xattn_Wk, L1_xattn_bk, L1_xattn_Wv, L1_xattn_bv, L1_xattn_Wo, L1_xattn_bo, L1_ffn_w_gate, L1_ffn_w_up, L1_ffn_w_down):
    import jax
    import jax.numpy as jnp

    def _L0_attn_ref(x, Wq, bq, Wk, bk, Wv, bv, Wo, bo):
        import jax, jax.numpy as jnp
        import numpy as np
        EMBED_DIM = 256
        NUM_HEADS = 16
        BATCH = 4
        SEQ = 1024
        B, S, E = x.shape
        H = NUM_HEADS
        D = E // H

        def proj(W, b):
            return (jnp.einsum('bse,fe->bsf', x, W) + b).reshape(B, S, H, D)
        q = jax.nn.elu(proj(Wq, bq)) + 1.0
        k = jax.nn.elu(proj(Wk, bk)) + 1.0
        v = proj(Wv, bv)
        kv = jnp.einsum('bshd,bshe->bhde', k, v)
        out = jnp.einsum('bshd,bhde->bshe', q, kv).reshape(B, S, E)
        out = jnp.einsum('bse,fe->bsf', out, Wo) + bo
        return out

    def _L0_xattn_ref(x, kv, padding_mask, w_q, w_kv, w_proj, b_proj, g_x, b_x, g_kv, b_kv):
        import jax, jax.numpy as jnp
        import numpy as np
        DIM = 256
        HEADS = 16
        HEAD_DIM = DIM // HEADS
        SCALE = HEAD_DIM ** (-0.5)
        MASK_FILL = -1000000000.0

        def layer_norm(x, gamma, beta, eps=1e-05):
            mu = jnp.mean(x, axis=-1, keepdims=True)
            var = jnp.var(x, axis=-1, keepdims=True)
            return (x - mu) * jax.lax.rsqrt(var + eps) * gamma + beta
        B, N1, C = x.shape
        N2 = kv.shape[1]
        xn = layer_norm(x, g_x, b_x)
        kvn = layer_norm(kv, g_kv, b_kv)
        q = (xn @ w_q).reshape(B, N1, HEADS, HEAD_DIM).transpose(0, 2, 1, 3)
        kv_proj = (kvn @ w_kv).reshape(B, N2, 2, HEADS, HEAD_DIM).transpose(2, 0, 3, 1, 4)
        k, v = (kv_proj[0], kv_proj[1])
        attn = jnp.einsum('bhqd,bhkd->bhqk', q, k) * SCALE
        mask = padding_mask[:, None, None, :]
        attn = jnp.where(mask == 0, MASK_FILL, attn)
        attn = jax.nn.softmax(attn, axis=-1)
        out = jnp.einsum('bhqk,bhkd->bhqd', attn, v)
        out = out.transpose(0, 2, 1, 3).reshape(B, N1, C)
        return out @ w_proj + b_proj

    def _L0_ffn_ref(x, attn_mask, Wg, Wq, bq, Wkv, bkv, Wo, bo, ln_g, ln_b):
        import jax, jax.numpy as jnp
        import numpy as np
        S, B, D, H, DH = (1024, 8, 256, 16, 64)

        def _forward(x, Wg, Wq, bq, Wkv, bkv, Wo, bo, ln_g, ln_b):
            s_len, bsz, d_model = x.shape
            n_head, _, d_head = Wq.shape
            cap = s_len // n_head
            scale = 1.0 / d_head ** 0.5
            h = jnp.transpose(x, (1, 0, 2))
            t = h
            probs = jax.nn.softmax(h @ Wg, axis=-1)
            scores = jnp.transpose(probs, (0, 2, 1))
            _, idx = jax.lax.top_k(scores, cap)
            idx = jnp.sort(idx, axis=-1)
            hg = jnp.take_along_axis(h[:, None, :, :], idx[..., None], axis=2)
            hg = jnp.transpose(hg, (1, 0, 2, 3))
            q = jnp.einsum('hbcd,hde->hbce', hg, Wq) + bq[:, None, None, :]
            kv = jnp.einsum('hbcd,hde->hbce', hg, Wkv) + bkv[:, None, None, :]
            k, v = jnp.split(kv, 2, axis=-1)
            att = jnp.einsum('hbid,hbjd->hbij', q, k) * scale
            p = jax.nn.softmax(att, axis=1)
            av = jnp.einsum('hbij,hbjd->hbid', p, v)
            ao = jnp.einsum('hbid,hde->hbie', av, Wo) + bo
            tok = jnp.transpose(idx, (1, 0, 2))
            b_ids = jnp.arange(bsz)[None, :, None]
            outs = jnp.zeros_like(t).at[b_ids, tok].add(ao)
            y = t + outs
            mu = jnp.mean(y, axis=-1, keepdims=True)
            var = jnp.var(y, axis=-1, keepdims=True)
            yn = (y - mu) * jax.lax.rsqrt(var + 1e-05) * ln_g + ln_b
            return jnp.transpose(yn, (1, 0, 2))
        return _forward(x, Wg, Wq, bq, Wkv, bkv, Wo, bo, ln_g, ln_b)

    def _L1_attn_ref(x, g, W_in, W_out, conv_w, conv_b, W_x, W_dt, b_dt, A_log, D):
        import jax, jax.numpy as jnp
        import numpy as np
        import math
        D_MODEL = 256
        D_STATE = 16
        D_CONV = 4
        EXPAND = 2
        D_INNER = D_MODEL * EXPAND
        EPS = 1e-06
        residual = x
        xn = x * jax.lax.rsqrt(jnp.mean(x * x, axis=-1, keepdims=True) + EPS) * g
        xz = xn @ W_in.T
        x_s, z = jnp.split(xz, 2, axis=-1)
        xt = jnp.transpose(x_s, (0, 2, 1))
        kern = conv_w[:, None, :]
        xc = jax.lax.conv_general_dilated(xt, kern, window_strides=(1,), padding=[(D_CONV - 1, 0)], feature_group_count=D_INNER, dimension_numbers=('NCH', 'OIH', 'NCH'))
        xc = jax.nn.silu(jnp.transpose(xc + conv_b[None, :, None], (0, 2, 1)))
        params = xc @ W_x.T
        B_coef = params[..., :D_STATE]
        C_coef = params[..., D_STATE:2 * D_STATE]
        log_dt = params[..., -1:]
        dt = jax.nn.softplus(log_dt @ W_dt.T + b_dt)
        A = -jnp.exp(A_log)
        dt_e = dt[..., None]
        A_bar = jnp.exp(dt_e * A)
        Bu = dt_e * B_coef[:, :, None, :] * xc[..., None]

        def step(h, inp):
            Ab, bu, c = inp
            h = Ab * h + bu
            y = jnp.einsum('bds,bs->bd', h, c)
            return (h, y)
        h0 = jnp.zeros((x.shape[0], D_INNER, D_STATE), x.dtype)
        _, ys = jax.lax.scan(step, h0, (jnp.swapaxes(A_bar, 0, 1), jnp.swapaxes(Bu, 0, 1), jnp.swapaxes(C_coef, 0, 1)))
        y = jnp.swapaxes(ys, 0, 1)
        y = (y + xc * D) * jax.nn.silu(z)
        return residual + y @ W_out.T

    def _L1_xattn_ref(query, key, value, Wq, bq, Wk, bk, Wv, bv, Wo, bo):
        import jax, jax.numpy as jnp
        import numpy as np
        D_MODEL = 256
        NUM_HEADS = 16
        HEAD_DIM = D_MODEL // NUM_HEADS

        def _split_heads(x):
            B, S, _ = x.shape
            return x.reshape(B, S, NUM_HEADS, HEAD_DIM).transpose(0, 2, 1, 3)
        Q = _split_heads(query @ Wq.T + bq)
        K = _split_heads(key @ Wk.T + bk)
        V = _split_heads(value @ Wv.T + bv)
        scores = jnp.einsum('bhqd,bhkd->bhqk', Q, K) / jnp.sqrt(jnp.float32(HEAD_DIM))
        attn = jax.nn.softmax(scores, axis=-1)
        out = jnp.einsum('bhqk,bhkd->bhqd', attn, V)
        B, H, S, Dh = out.shape
        out = out.transpose(0, 2, 1, 3).reshape(B, S, H * Dh)
        return out @ Wo.T + bo

    def _L1_ffn_ref(x, w_gate, w_up, w_down):
        import jax, jax.numpy as jnp
        import numpy as np
        HIDDEN = 256
        INNER = 1024

        def _weight_quant(w):
            scale = 1.0 / jnp.clip(jnp.mean(jnp.abs(w)), 1e-05)
            wq = jnp.clip(jnp.round(w * scale), -1.0, 1.0) / scale
            return w + jax.lax.stop_gradient(wq - w)

        def _act_quant(x):
            scale = 127.0 / jnp.clip(jnp.max(jnp.abs(x), axis=-1, keepdims=True), 1e-05)
            xq = jnp.clip(jnp.round(x * scale), -128.0, 127.0) / scale
            return x + jax.lax.stop_gradient(xq - x)

        def _bitlinear(x, w):
            return jnp.einsum('bsi,oi->bso', _act_quant(x), _weight_quant(w))
        gate = jax.nn.silu(_bitlinear(x, w_gate))
        up = _bitlinear(x, w_up)
        return _bitlinear(gate * up, w_down)
    x = _layernorm(x + _L0_attn_ref(x, L0_attn_Wq, L0_attn_bq, L0_attn_Wk, L0_attn_bk, L0_attn_Wv, L0_attn_bv, L0_attn_Wo, L0_attn_bo), axis=-1)
    x = _layernorm(x + _L0_xattn_ref(x, ctx_1024, mask_BxS2_ik0, L0_xattn_w_q, L0_xattn_w_kv, L0_xattn_w_proj, L0_xattn_b_proj, L0_xattn_g_x, L0_xattn_b_x, L0_xattn_g_kv, L0_xattn_b_kv), axis=-1)
    x = _layernorm(x + _L0_ffn_ref(x, L0_ffn_attn_mask, L0_ffn_Wg, L0_ffn_Wq, L0_ffn_bq, L0_ffn_Wkv, L0_ffn_bkv, L0_ffn_Wo, L0_ffn_bo, L0_ffn_ln_g, L0_ffn_ln_b), axis=-1)
    x = _layernorm(x + _L1_attn_ref(x, L1_attn_g, L1_attn_W_in, L1_attn_W_out, L1_attn_conv_w, L1_attn_conv_b, L1_attn_W_x, L1_attn_W_dt, L1_attn_b_dt, L1_attn_A_log, L1_attn_D), axis=-1)
    x = _layernorm(x + _L1_xattn_ref(x, ctx_1024, ctx_1024, L1_xattn_Wq, L1_xattn_bq, L1_xattn_Wk, L1_xattn_bk, L1_xattn_Wv, L1_xattn_bv, L1_xattn_Wo, L1_xattn_bo), axis=-1)
    x = _layernorm(x + _L1_ffn_ref(x, L1_ffn_w_gate, L1_ffn_w_up, L1_ffn_w_down), axis=-1)
    return x

_drawn_inputs = setup_inputs


def setup_inputs(seed=0):
    import zlib

    import numpy as np

    out = dict(_drawn_inputs(seed))
    spreads = {'L0_attn_bq': (0.0, 0.412),
     'L0_attn_bk': (0.0, 0.526),
     'L0_attn_bv': (0.0, 0.1),
     'L0_attn_bo': (0.0, 0.8),
     'L0_xattn_b_proj': (0.0, 0.1),
     'L0_xattn_g_x': (1.0, 0.2),
     'L0_xattn_b_x': (0.0, 0.301),
     'L0_xattn_g_kv': (1.0, 0.2),
     'L0_xattn_b_kv': (0.0, 0.1),
     'L0_ffn_bq': (0.0, 0.8),
     'L0_ffn_bkv': (0.0, 0.8),
     'L0_ffn_bo': (0.0, 0.1),
     'L0_ffn_ln_g': (1.0, 0.2),
     'L0_ffn_ln_b': (0.0, 0.1),
     'L1_attn_g': (1.0, 0.6),
     'L1_attn_conv_b': (0.0, 0.8),
     'L1_attn_b_dt': (-6.907755374908447, 0.6),
     'L1_attn_D': (1.0, 0.6),
     'L1_xattn_bq': (0.0, 0.397),
     'L1_xattn_bk': (0.0, 0.8),
     'L1_xattn_bv': (0.0, 0.1),
     'L1_xattn_bo': (0.0, 0.1)}
    factors = {'L0_attn_Wk': 2.918,
     'L0_ffn_Wq': 8.0,
     'L0_ffn_Wkv': 8.0,
     'L0_ffn_Wo': 8.0,
     'L1_attn_W_in': 8.0,
     'L1_attn_W_out': 8.0,
     'L1_attn_conv_w': 8.0,
     'L1_attn_W_x': 8.0,
     'L1_attn_W_dt': 8.0,
     'L1_attn_A_log': 8.0}
    for name, (base, spread) in spreads.items():
        noise = np.random.default_rng([zlib.crc32(name.encode()), seed]).standard_normal(out[name].shape)
        drawn = base * np.exp(spread * noise) if base else spread * noise
        out[name] = jnp.asarray(drawn.astype(out[name].dtype))
    for name, factor in factors.items():
        out[name] = (out[name] * factor).astype(out[name].dtype)
    return out
```

```python
import concourse.bass as bass
from concourse import mybir
from contextlib import ExitStack

fp32 = mybir.dt.float32
bf16 = mybir.dt.bfloat16
i32 = mybir.dt.int32
ALU = mybir.AluOpType
ACT = mybir.ActivationFunctionType
AX = mybir.AxisListType

P = 128
B = 32
S = 256
D = 256
T = S // P
C = D // P
H = 16
DH = D // H
CTX = 77
PAIRS = B // 2
LN_EPS = 1e-5


class Stage:

    def __init__(self, nc, name):
        self.nc, self.name, self.ctx = nc, name, ExitStack()

    def __enter__(self):
        self.ctx.__enter__()
        self.ctx.enter_context(self.nc.cleanup_on_exit())
        return self

    def __exit__(self, *e):
        return self.ctx.__exit__(*e)

    def sb(self, name, shape, dt=fp32):
        return self.ctx.enter_context(self.nc.sbuf_tensor(f"{self.name}_{name}", shape, dt))

    def ps(self, name, shape, dt=fp32):
        return self.ctx.enter_context(self.nc.psum_tensor(f"{self.name}_{name}", shape, dt))

    def sem(self, name):
        return self.nc.alloc_semaphore(name=f"{self.name}_{name}")

    def block(self):
        return self.ctx.enter_context(self.nc.Block())


class Chain:

    def __init__(self, eng, sem, per_turn):
        self.eng, self.sem, self.per_turn, self.done, self.turn = eng, sem, per_turn, 0, None

    def begin(self, turn):
        assert self.turn is None
        self.base, self.turn, self.n = self.done, turn, 0

    def end(self, turns):
        assert self.n == self.per_turn, (self.n, self.per_turn)
        self.done, self.turn = self.base + turns * self.per_turn, None

    def __call__(self, ins):
        ins.then_inc(self.sem, 1)
        if self.turn is None:
            self.done += 1
            self.eng.wait_ge(self.sem, self.done)
        else:
            self.n += 1
            self.eng.wait_ge(self.sem, self.turn * self.per_turn + (self.base + self.n))


def batch_tiles(x, b):
    return x[b].rearrange("(t p) d -> p t d", p=P)


def split_in_three(link, row, rest, parts, ident, out):
    v = link.eng
    for k in range(3):
        link(v.tensor_copy(parts[:, k, :], row[:, :] if k == 0 else rest[:, :]))
        if k < 2:
            link(v.tensor_tensor(rest[:, :], row[:, :] if k == 0 else rest[:, :], parts[:, k, :], ALU.subtract))
    link(v.tensor_scalar(rest[:, :], parts[:, 0, :], ident[0:3, 0:1], None, ALU.mult))
    for k in (1, 2):
        link(v.scalar_tensor_tensor(out=rest[:, :] if k == 1 else out[:, :], in0=parts[:, k, :],
                                    scalar=ident[0:3, k:k + 1], in1=rest[:, :], op0=ALU.mult, op1=ALU.add))


def linear_attention(nc, x_in, x_out, wqT, bq, wkvT, bkv, woT, bo, ident_d, blocks_d):
    with Stage(nc, "la") as st:
        sb, ps, sem = st.sb, st.ps, st.sem
        ident = sb("ident", [P, P])
        blocks = sb("blocks", [P, P])
        wq = sb("wq", [P, C, D])
        wkv = sb("wkv", [P, C, 2 * D])
        wo = sb("wo", [P, C, D])
        bq_c = sb("bq_c", [P, C])
        bias3 = sb("bias3", [3, 3 * D])
        rest3 = sb("rest3", [3, 3 * D])
        parts3 = sb("parts3", [3, 3, 3 * D], bf16)
        biasr = sb("biasr", [3, 3 * D], bf16)
        ones3 = sb("ones3", [3, P], bf16)
        minus_half = sb("minus_half", [P, T])
        eps = sb("eps", [P, T])
        spacer = sb("spacer", [P, 1])
        x = sb("x", [P, 4, T, D])
        xT = sb("xT", [P, 2, C, S])
        eq = sb("eq", [P, 2, C, S])
        rq = sb("rq", [P, 2, C, S])
        qT = sb("qT", [P, 2, C, S])
        ek = sb("ek", [P, 2, T, D])
        rk = sb("rk", [P, 2, T, D])
        k = sb("k", [P, 2, T, D])
        v = sb("v", [P, 2, T, D])
        kv = sb("kv", [P, 2, C, P])
        oT = sb("oT", [P, 2, C, S])
        r = sb("r", [P, 2, T, D])
        stats = sb("stats", [P, 2, T, 6])
        mv = sb("mv", [P, 2, T, 2])
        veps = sb("veps", [P, 2, T])
        rstd = sb("rstd", [P, 2, T])
        y = sb("y", [P, 2, T, D])
        pA = [ps(f"pA{p}", [P, C, S]) for p in range(2)]
        pB = [ps(f"pB{p}", [P, C, S]) for p in range(2)]
        pC = [ps(f"pC{p}", [P, T, 2 * D]) for p in range(2)]

        w_loaded, setup_done = sem("w_loaded"), sem("setup_done")
        x_loaded = [sem(f"x_loaded{b}") for b in range(4)]
        y_stored = [sem(f"y_stored{p}") for p in range(2)]
        xT_made, xT_copied = sem("xT_made"), sem("xT_copied")
        q_made, kv_made = sem("q_made"), sem("kv_made")
        exp_done, v_copied, qk_ready = sem("exp_done"), sem("v_copied"), sem("qk_ready")
        outer_made, outer_masked = sem("outer_made"), sem("outer_masked")
        oT_made, oT_copied = sem("oT_made"), sem("oT_copied")
        proj_made, pB_free = sem("proj_made"), sem("pB_free")
        var_ready, rstd_ready, y_ready = sem("var_ready"), sem("rstd_ready"), sem("y_ready")
        dve_chain, pool_chain = sem("dve_chain"), sem("pool_chain")
        block = st.block()

        @block.sync
        def _(sp):
            for dst, src in ((ident[:, :], ident_d), (blocks[:, :], blocks_d),
                             (wq[:, :, :], wqT.rearrange("(c p) f -> p c f", p=P)),
                             (wkv[:, :, :], wkvT.rearrange("(c p) f -> p c f", p=P)),
                             (wo[:, :, :], woT.rearrange("(c p) f -> p c f", p=P)),
                             (bq_c[:, :], bq),
                             (bias3[:, 0:2 * D], bkv.partition_broadcast(3)),
                             (bias3[:, 2 * D:3 * D], bo.partition_broadcast(3))):
                sp.dma_start(dst, src).then_inc(w_loaded, 16)
            for b in range(4):
                sp.dma_start(x[:, b], batch_tiles(x_in, b)).then_inc(x_loaded[b], 16)
            for p in range(2):
                sp.sem_inc(y_stored[p], 16)

            def store(j, q, p):
                sp.wait_ge(y_ready, 4 * j + (2 * q + p + 1))
                sp.dma_start(batch_tiles(x_out, 4 * j + (2 * q + p)), y[:, p]).then_inc(y_stored[p], 16)

            with sp.Fori(0, B // 4 - 1) as j:
                for q in range(2):
                    for p in range(2):
                        store(j, q, p)
                        sp.dma_start(x[:, 2 * q + p], batch_tiles(x_in, 4 * j + (2 * q + p + 4))).then_inc(x_loaded[2 * q + p], 16)
            for q in range(2):
                for p in range(2):
                    store(B // 4 - 1, q, p)
            for p in range(2):
                sp.wait_ge(y_stored[p], 16 * (B // 2 + 1))

        @block.tensor
        def _(pe):
            def pair(j, q):
                for p in range(2):
                    pe.wait_ge(x_loaded[2 * q + p], 16 * j + 16)
                    for c in range(C):
                        for t in range(T):
                            last = pe.transpose(pA[p][:, c, t * P:(t + 1) * P],
                                                x[:, 2 * q + p, t, c * P:(c + 1) * P], ident[:, :])
                    last.then_inc(xT_made, 1)
                for p in range(2):
                    n = 4 * j + (2 * q + p + 1)
                    pe.wait_ge(xT_copied, n)
                    pe.wait_ge(pB_free, n)
                    for f in range(C):
                        for c in range(C):
                            last = pe.matmul(pB[p][:, f, :], wq[:, c, f * P:(f + 1) * P], xT[:, p, c, :],
                                             start=(c == 0), stop=(c == C - 1))
                    last.then_inc(q_made, 1)
                    for t in range(T):
                        pe.matmul(pC[p][:, t, :], ones3[:, :], biasr[:, 0:2 * D], start=True, stop=False)
                        for c in range(C):
                            last = pe.matmul(pC[p][:, t, :], xT[:, p, c, t * P:(t + 1) * P], wkv[:, c, :],
                                             start=False, stop=(c == C - 1))
                    last.then_inc(kv_made, 1)
                for p in range(2):
                    n = 4 * j + (2 * q + p + 1)
                    pe.wait_ge(v_copied, n)
                    pe.wait_ge(qk_ready, n)
                    for c in range(C):
                        for t in range(T):
                            last = pe.matmul(pA[p][:, c, 0:P], k[:, p, t, c * P:(c + 1) * P],
                                             v[:, p, t, c * P:(c + 1) * P], start=(t == 0), stop=(t == T - 1))
                    last.then_inc(outer_made, 1)
                for p in range(2):
                    pe.wait_ge(outer_masked, 4 * j + (2 * q + p + 1))
                    for c in range(C):
                        last = pe.matmul(pC[p][:, 0, c * S:(c + 1) * S], kv[:, p, c, :], qT[:, p, c, :],
                                         start=True, stop=True)
                    last.then_inc(oT_made, 1)
                for p in range(2):
                    pe.wait_ge(oT_copied, 4 * j + (2 * q + p + 1))
                    for t in range(T):
                        pe.matmul(pB[p][:, t, :], ones3[:, :], biasr[:, 2 * D:3 * D], start=True, stop=False)
                        for c in range(C):
                            last = pe.matmul(pB[p][:, t, :], oT[:, p, c, t * P:(t + 1) * P], wo[:, c, :],
                                             start=False, stop=(c == C - 1))
                    last.then_inc(proj_made, 1)

            pe.wait_ge(w_loaded, 16 * 8)
            pe.wait_ge(setup_done, 1)
            with pe.Fori(0, B // 4) as j:
                for q in range(2):
                    pair(j, q)

        @block.scalar
        def _(act):
            def pair(j, q):
                for p in range(2):
                    act.wait_ge(xT_made, 4 * j + (2 * q + p + 1))
                    act.activation(xT[:, p], pA[p][:, :, :], ACT.Copy).then_inc(xT_copied, 1)
                for p in range(2):
                    n = 4 * j + (2 * q + p + 1)
                    act.wait_ge(q_made, n)
                    for f in range(C):
                        last = act.activation(eq[:, p, f, :], pB[p][:, f, :], ACT.Exp, bias=bq_c[:, f:f + 1])
                    last.then_inc(exp_done, 1)
                    act.wait_ge(kv_made, n)
                    act.activation(ek[:, p], pC[p][:, :, 0:D], ACT.Exp)
                    act.activation(v[:, p], pC[p][:, :, D:2 * D], ACT.Copy).then_inc(v_copied, 1)
                for p in range(2):
                    act.wait_ge(oT_made, 4 * j + (2 * q + p + 1))
                    act.activation(oT[:, p], pC[p][:, 0, :].rearrange("p (c s) -> p c s", c=C),
                                   ACT.Copy).then_inc(oT_copied, 1)

            act.wait_ge(w_loaded, 16 * 8)
            with act.Fori(0, B // 4) as j:
                for q in range(2):
                    pair(j, q)

        @block.gpsimd
        def _(pool):
            link = Chain(pool, pool_chain, 4)
            pool.memset(eps[:, :], LN_EPS)
            link(pool.memset(minus_half[:, :], -0.5))
            link.begin(0)
            with pool.Fori(0, B // 4) as j:
                link.turn = j
                for b in range(4):
                    pool.wait_ge(var_ready, 4 * j + (b + 1))
                    link(pool.tensor_tensor(veps[:, b % 2], mv[:, b % 2, :, 1], eps[:, :], ALU.add))
                    pool.tensor_tensor(rstd[:, b % 2], veps[:, b % 2], minus_half[:, :], ALU.pow).then_inc(rstd_ready, 1)
            link.end(B // 4)

        @block.vector
        def _(dve):
            def pair(j, q):
                for p in range(2):
                    n = 4 * j + (2 * q + p + 1)
                    dve.wait_ge(exp_done, n)
                    for f in range(C):
                        dve.tensor_scalar(rq[:, p, f, :], pB[p][:, f, :], bq_c[:, f:f + 1], 0.0, ALU.add, ALU.max)
                    dve.wait_ge(v_copied, n)
                    link(dve.tensor_scalar(rk[:, p], pC[p][:, :, 0:D], 0.0, None, ALU.max))
                    dve.scalar_tensor_tensor(out=qT[:, p], in0=eq[:, p], scalar=1.0, in1=rq[:, p],
                                             op0=ALU.min, op1=ALU.add)
                    dve.scalar_tensor_tensor(out=k[:, p], in0=ek[:, p], scalar=1.0, in1=rk[:, p],
                                             op0=ALU.min, op1=ALU.add).then_inc(qk_ready, 1)
                for p in range(2):
                    dve.wait_ge(outer_made, 4 * j + (2 * q + p + 1))
                    dve.tensor_tensor(kv[:, p], pA[p][:, :, 0:P], blocks[:, :].unsqueeze(1).broadcast_to([P, C, P]),
                                      ALU.mult).then_inc(outer_masked, 1)
                for p in range(2):
                    dve.wait_ge(proj_made, 4 * j + (2 * q + p + 1))
                    link(dve.tensor_tensor(r[:, p], pB[p][:, :, :], x[:, 2 * q + p], ALU.add))
                    dve.sem_inc(pB_free, 1)
                    for t in range(T):
                        last = dve.bn_stats(stats[:, p, t, :], r[:, p, t, :])
                    link(last)
                    dve.memset(spacer[:, :], 0.0)
                    for t in range(T):
                        last = dve.bn_aggr(mv[:, p, t, :], stats[:, p, t, :])
                    last.then_inc(var_ready, 1)
                for p in range(2):
                    dve.wait_ge(rstd_ready, 4 * j + (2 * q + p + 1))
                    dve.wait_ge(y_stored[p], 32 * j + 16 * (q + 1))
                    for t in range(T):
                        last = dve.tensor_scalar(y[:, p, t, :], r[:, p, t, :], mv[:, p, t, 0:1], rstd[:, p, t:t + 1],
                                                 ALU.subtract, ALU.mult)
                    last.then_inc(y_ready, 1)

            link = Chain(dve, dve_chain, 3 * 4)
            dve.wait_ge(w_loaded, 16 * 8)
            dve.memset(ones3[:, :], 1.0)
            split_in_three(link, bias3, rest3, parts3, ident, biasr)
            dve.sem_inc(setup_done, 1)
            dve.sem_inc(pB_free, 2)
            link.begin(0)
            with dve.Fori(0, B // 4) as j:
                link.turn = j
                for q in range(2):
                    pair(j, q)
            link.end(B // 4)


def cross_attention(nc, name, x_in, x_out, ctx_d, wq_d, wkv_d, wo_d, bo_d, ident_d, heads_d,
                    bq_d=None, bk_d=None, bv_d=None, mask_d=None, norms_d=None):
    normed, masked = norms_d is not None, mask_d is not None
    HC = H // C
    HB = HC // 2
    W = DH + 1
    with Stage(nc, name) as st:
        sb, ps, sem = st.sb, st.ps, st.sem
        ident = sb("ident", [P, P])
        head_of = sb("head_of", [P, HC])
        wq = sb("wq", [P, C, D])
        wkv = sb("wkv", [P, C, 2 * D])
        wo = sb("wo", [P, C, D])
        bqk = sb("bqk", [P, 2, C])
        bq4 = sb("bq4", [P, C])
        norms = sb("norms", [P, 4, C])
        bias3 = sb("bias3", [3, 2 * D])
        rest3 = sb("rest3", [3, 2 * D])
        parts3 = sb("parts3", [3, 3, 2 * D], bf16)
        biasr = sb("biasr", [3, 2 * D], bf16)
        fill3 = sb("fill3", [3, 1])
        fill_rest = sb("fill_rest", [3, 1])
        fill_parts = sb("fill_parts", [3, 3, 1], bf16)
        fillr = sb("fillr", [3, 1])
        ones3 = sb("ones3", [3, P], bf16)
        spacer = sb("spacer", [P, 1])
        eps = sb("eps", [P, 3])
        minus_half = sb("minus_half", [P, 3])
        x = sb("x", [P, 4, T, D])
        cx = sb("cx", [CTX, 2, D])
        mask_i = sb("mask_i", [P, 2, CTX], i32)
        seen = sb("seen", [P, 2, CTX])
        fill_row = sb("fill_row", [3, 2, CTX], bf16)
        n_stats = sb("n_stats", [P, 2, 3, 6])
        n_mv = sb("n_mv", [P, 2, 3, 2])
        n_veps = sb("n_veps", [P, 2, 3])
        n_rstd = sb("n_rstd", [P, 2, 3])
        xn = sb("xn", [P, 2, T, D])
        cn = sb("cn", [CTX, 2, D])
        xT = sb("xT", [P, 2, C, S])
        cT = sb("cT", [P, 2, C, CTX])
        qT = sb("qT", [P, 2, C, S])
        kT = sb("kT", [P, 2, C, CTX])
        kheads = sb("kheads", [P, 2, C, HC * CTX])
        v = sb("v", [CTX, 2, H, W])
        top = sb("top", [P, 2, HC])
        low = sb("low", [P, 2, HC * CTX])
        e = sb("e", [P, 2, HC * CTX])
        eT = sb("eT", [CTX, 2, C, HC, P])
        rec = sb("rec", [P, 2, H])
        on = sb("on", [P, 2, T, D])
        oT = sb("oT", [P, 2, C, S])
        r = sb("r", [P, 2, T, D])
        stats = sb("stats", [P, 2, T, 6])
        mv = sb("mv", [P, 2, T, 2])
        veps = sb("veps", [P, 2, T])
        rstd = sb("rstd", [P, 2, T])
        y = sb("y", [P, 2, T, D])
        pS = [ps(f"pS{c}", [P, 2, 512]) for c in range(C)]
        pE = [ps(f"pE{h}", [CTX, HB, P]) for h in range(2)]
        pG = [ps(f"pG{g}", [P, 512]) for g in range(2)]

        w_loaded, setup_done = sem("w_loaded"), sem("setup_done")
        x_loaded = [sem(f"x_loaded{b}") for b in range(4)]
        c_loaded = [sem(f"c_loaded{p}") for p in range(2)]
        y_stored = [sem(f"y_stored{p}") for p in range(2)]
        n_var, n_rstd_ready, n_ready = sem("n_var"), sem("n_rstd_ready"), sem("n_ready")
        xT_made, xT_copied, cT_made, cT_copied = sem("xT_made"), sem("xT_copied"), sem("cT_made"), sem("cT_copied")
        q_made, q_copied, k_made, k_copied = sem("q_made"), sem("q_copied"), sem("k_made"), sem("k_copied")
        v_made, v_copied, kheads_ready = sem("v_made"), sem("v_copied"), sem("kheads_ready")
        scores_made, low_ready = sem("scores_made"), sem("low_ready")
        e_ready, eT_made, eT_copied = sem("e_ready"), sem("eT_made"), sem("eT_copied")
        o_made, o_normed = sem("o_made"), sem("o_normed")
        oT_made, oT_copied, proj_made, res_added = sem("oT_made"), sem("oT_copied"), sem("proj_made"), sem("res_added")
        var_ready, rstd_ready, y_ready = sem("var_ready"), sem("rstd_ready"), sem("y_ready")
        dve_chain, pool_chain = sem("dve_chain"), sem("pool_chain")
        bq4_ready = sem("bq4_ready")
        block = st.block()
        ctx_used = n_ready if normed else cT_made
        U = T * C

        loads = [(ident[:, :], ident_d), (head_of[:, :], heads_d),
                 (wq[:, :, :], wq_d.rearrange("(c p) f -> p c f", p=P)),
                 (wkv[:, :, :], wkv_d.rearrange("(c p) f -> p c f", p=P)),
                 (wo[:, :, :], wo_d.rearrange("(c p) f -> p c f", p=P)),
                 (bias3[:, D:2 * D], bo_d.partition_broadcast(3))]
        if bq_d is not None:
            loads += [(bqk[:, 0, :], bq_d), (bqk[:, 1, :], bk_d), (bias3[:, 0:D], bv_d.partition_broadcast(3))]
        if normed:
            loads += [(norms[:, n, :], d) for n, d in enumerate(norms_d)]

        @block.sync
        def _(sp):
            for dst, src in loads:
                sp.dma_start(dst, src).then_inc(w_loaded, 16)

            def load_x(b, at):
                sp.dma_start(x[:, b], batch_tiles(x_in, at)).then_inc(x_loaded[b], 16)

            def load_ctx(p, at):
                sp.dma_start(cx[:, p], ctx_d[at]).then_inc(c_loaded[p], 16)
                if masked:
                    sp.dma_start(mask_i[:, p], mask_d[at].partition_broadcast(P)).then_inc(c_loaded[p], 16)

            for b in range(4):
                load_x(b, b)
            for p in range(2):
                load_ctx(p, p)
                sp.sem_inc(y_stored[p], 16)

            def store(j, b):
                p = b % 2
                sp.wait_ge(y_ready, 4 * j + (b + 1))
                sp.dma_start(batch_tiles(x_out, 4 * j + b), y[:, p]).then_inc(y_stored[p], 16)

            with sp.Fori(0, B // 4 - 1) as j:
                for b in range(4):
                    sp.wait_ge(ctx_used, 4 * j + (b + 1))
                    load_ctx(b % 2, 4 * j + (b + 2))
                    store(j, b)
                    load_x(b, 4 * j + (b + 4))
            for b in range(4):
                if b < 2:
                    sp.wait_ge(ctx_used, B - 3 + b)
                    load_ctx(b % 2, B - 2 + b)
                store(B // 4 - 1, b)
            for p in range(2):
                sp.wait_ge(y_stored[p], 16 * (B // 2 + 1))

        @block.tensor
        def _(pe):
            def front(j, b):
                p, n = b % 2, 4 * j + (b + 1)
                if normed:
                    pe.wait_ge(n_ready, n)
                else:
                    pe.wait_ge(x_loaded[b], 16 * j + 16)
                for c in range(C):
                    for t in range(T):
                        src = xn[:, p, t, c * P:(c + 1) * P] if normed else x[:, b, t, c * P:(c + 1) * P]
                        last = pe.transpose(pG[0][:, (c * T + t) * P:(c * T + t + 1) * P], src, ident[:, :])
                last.then_inc(xT_made, 1)
                if not normed:
                    pe.wait_ge(c_loaded[p], 32 * j + 16 * (b // 2 + 1))
                for c in range(C):
                    src = cn[:, p, c * P:(c + 1) * P] if normed else cx[:, p, c * P:(c + 1) * P]
                    last = pe.transpose(pG[1][:, c * CTX:(c + 1) * CTX], src, ident[0:CTX, 0:CTX])
                last.then_inc(cT_made, 1)
                pe.wait_ge(xT_copied, n)
                for f in range(C):
                    for c in range(C):
                        last = pe.matmul(pG[0][:, f * S:(f + 1) * S], wq[:, c, f * P:(f + 1) * P], xT[:, p, c, :],
                                         start=(c == 0), stop=(c == C - 1))
                last.then_inc(q_made, 1)
                pe.wait_ge(cT_copied, n)
                for f in range(C):
                    for c in range(C):
                        last = pe.matmul(pG[1][:, f * CTX:(f + 1) * CTX], wkv[:, c, f * P:(f + 1) * P], cT[:, p, c, :],
                                         start=(c == 0), stop=(c == C - 1))
                last.then_inc(k_made, 1)
                pe.wait_ge(q_copied, n)
                if bv_d is not None:
                    pe.matmul(pG[0][0:CTX, 0:D], ones3[:, 0:CTX], biasr[:, 0:D], start=True, stop=False)
                for c in range(C):
                    last = pe.matmul(pG[0][0:CTX, 0:D], cT[:, p, c, :], wkv[:, c, D:2 * D],
                                     start=(c == 0 and bv_d is None), stop=(c == C - 1))
                last.then_inc(v_made, 1)

            def scores(j, b, u):
                p, c, t = b % 2, u % C, u // C
                pe.wait_ge(low_ready, (4 * U) * j + (U * b + u + 1))
                for h in range(2):
                    cols = slice(h * HB * CTX, (h + 1) * HB * CTX)
                    if masked:
                        pe.matmul(pS[c][:, h, 0:HB * CTX], ones3[:, :],
                                  fill_row[:, p, :].unsqueeze(1).broadcast_to([3, HB, CTX]), start=True, stop=False)
                    last = pe.matmul(pS[c][:, h, 0:HB * CTX], qT[:, p, c, t * P:(t + 1) * P], kheads[:, p, c, cols],
                                     start=not masked, stop=True)
                last.then_inc(scores_made, 1)

            def turn(j, b, u):
                pe.wait_ge(e_ready, (4 * U) * j + (U * b + u + 1))
                for h in range(2):
                    pe.wait_ge(eT_copied, (8 * U) * j + (2 * (U * b + u) + h + 1))
                    for i in range(HB):
                        at = (h * HB + i) * CTX
                        last = pe.transpose(pE[h][:, i, :], e[:, u % 2, at:at + CTX], ident[:, :])
                    last.then_inc(eT_made, 1)

            def values(j, b, t):
                p = b % 2
                pe.wait_ge(eT_copied, (8 * U) * j + (2 * U * b + 4 * (t + 1) + 2))
                if t == 0:
                    pe.wait_ge(v_copied, 4 * j + (b + 1))
                for h in range(H):
                    last = pe.matmul(pG[t][:, h * W:(h + 1) * W], eT[:, t, h // HC, h % HC, :], v[:, p, h, :],
                                     start=True, stop=True)
                last.then_inc(o_made, 1)

            def back(j, b):
                p, n = b % 2, 4 * j + (b + 1)
                pe.wait_ge(o_normed, 8 * j + 2 * (b + 1))
                for c in range(C):
                    for t in range(T):
                        last = pe.transpose(pG[0][:, (c * T + t) * P:(c * T + t + 1) * P],
                                            on[:, p, t, c * P:(c + 1) * P], ident[:, :])
                last.then_inc(oT_made, 1)
                pe.wait_ge(oT_copied, n)
                for t in range(T):
                    pe.matmul(pG[1][:, t * D:(t + 1) * D], ones3[:, :], biasr[:, D:2 * D], start=True, stop=False)
                    for c in range(C):
                        last = pe.matmul(pG[1][:, t * D:(t + 1) * D], oT[:, p, c, t * P:(t + 1) * P], wo[:, c, :],
                                         start=False, stop=(c == C - 1))
                last.then_inc(proj_made, 1)

            def batch(j, b, nxt):
                n = 4 * j + (b + 1)
                pe.wait_ge(kheads_ready, n)
                scores(j, b, 0)
                scores(j, b, 1)
                turn(j, b, 0)
                scores(j, b, 2)
                if nxt is not None:
                    pe.wait_ge(v_copied, n)
                    pe.wait_ge(res_added, n)
                    front(*nxt)
                turn(j, b, 1)
                scores(j, b, 3)
                turn(j, b, 2)
                if nxt is not None:
                    pe.wait_ge(v_copied, n + 1)
                    pe.wait_ge(k_copied, n + 1)
                values(j, b, 0)
                turn(j, b, 3)
                values(j, b, 1)
                back(j, b)

            pe.wait_ge(w_loaded, 16 * len(loads))
            pe.wait_ge(setup_done, 1)
            front(0, 0)
            with pe.Fori(0, B // 4 - 1) as j:
                for b in range(4):
                    batch(j, b, (j, b + 1) if b < 3 else (j + 1, 0))
            for b in range(4):
                batch(B // 4 - 1, b, (B // 4 - 1, b + 1) if b < 3 else None)

        @block.scalar
        def _(act):
            def front(j, b):
                p, n = b % 2, 4 * j + (b + 1)
                act.wait_ge(xT_made, n)
                for c in range(C):
                    last = act.activation(xT[:, p, c, :], pG[0][:, c * S:(c + 1) * S], ACT.Identity,
                                          **(dict(bias=norms[:, 1, c:c + 1], scale=norms[:, 0, c:c + 1]) if normed else {}))
                last.then_inc(xT_copied, 1)
                act.wait_ge(cT_made, n)
                for c in range(C):
                    last = act.activation(cT[:, p, c, :], pG[1][:, c * CTX:(c + 1) * CTX], ACT.Identity,
                                          **(dict(bias=norms[:, 3, c:c + 1], scale=norms[:, 2, c:c + 1]) if normed else {}))
                last.then_inc(cT_copied, 1)
                act.wait_ge(q_made, n)
                for f in range(C):
                    last = act.activation(qT[:, p, f, :], pG[0][:, f * S:(f + 1) * S], ACT.Identity, scale=0.25,
                                          **(dict(bias=bq4[:, f:f + 1]) if bq_d is not None else {}))
                last.then_inc(q_copied, 1)
                act.wait_ge(k_made, n)
                for f in range(C):
                    last = act.activation(kT[:, p, f, :], pG[1][:, f * CTX:(f + 1) * CTX], ACT.Identity,
                                          **(dict(bias=bqk[:, 1, f:f + 1]) if bk_d is not None else {}))
                last.then_inc(k_copied, 1)
                act.wait_ge(v_made, n)
                act.activation(v[:, p, :, 0:DH], pG[0][0:CTX, 0:D].rearrange("p (h e) -> p h e", h=H),
                               ACT.Copy).then_inc(v_copied, 1)

            def expo(j, b, u):
                act.wait_ge(low_ready, (4 * U) * j + (U * b + u + 3))
                act.activation(e[:, u % 2], low[:, u % 2], ACT.Exp).then_inc(e_ready, 1)

            def turned(j, b, u):
                for h in range(2):
                    act.wait_ge(eT_made, (8 * U) * j + (2 * (U * b + u) + h + 1))
                    act.activation(eT[:, u // C, u % C, h * HB:(h + 1) * HB, :], pE[h][:, :, :],
                                   ACT.Copy).then_inc(eT_copied, 1)

            def batch(j, b, nxt):
                expo(j, b, 0)
                turned(j, b, 0)
                expo(j, b, 1)
                if nxt is not None:
                    front(*nxt)
                turned(j, b, 1)
                expo(j, b, 2)
                turned(j, b, 2)
                expo(j, b, 3)
                turned(j, b, 3)
                act.wait_ge(oT_made, 4 * j + (b + 1))
                act.activation(oT[:, b % 2], pG[0][:, :].rearrange("p (c s) -> p c s", c=C), ACT.Copy).then_inc(oT_copied, 1)

            act.wait_ge(w_loaded, 16 * len(loads))
            act.wait_ge(setup_done, 1)
            act.sem_inc(eT_copied, 2)
            if bq_d is not None:
                act.activation(bq4[:, :], bqk[:, 0, :], ACT.Copy, scale=0.25).then_inc(bq4_ready, 1)
                act.wait_ge(bq4_ready, 1)
            front(0, 0)
            with act.Fori(0, B // 4 - 1) as j:
                for b in range(4):
                    batch(j, b, (j, b + 1) if b < 3 else (j + 1, 0))
            for b in range(4):
                batch(B // 4 - 1, b, (B // 4 - 1, b + 1) if b < 3 else None)

        @block.gpsimd
        def _(pool):
            def norm_scale(j, b):
                p = b % 2
                pool.wait_ge(n_var, 4 * j + (b + 1))
                link(pool.tensor_tensor(n_veps[:, p], n_mv[:, p, :, 1], eps[:, :], ALU.add))
                pool.tensor_tensor(n_rstd[:, p], n_veps[:, p], minus_half[:, :], ALU.pow).then_inc(n_rstd_ready, 1)

            def spread_k(j, b):
                p, n = b % 2, 4 * j + (b + 1)
                pool.wait_ge(k_copied, n)
                if masked:
                    link(pool.tensor_tensor(kT[:, p], kT[:, p], seen[:, p].unsqueeze(1).broadcast_to([P, C, CTX]), ALU.mult))
                for c in range(C):
                    last = pool.tensor_tensor(kheads[:, p, c, :].rearrange("p (h s) -> p h s", h=HC),
                                              kT[:, p, c, :].unsqueeze(1).broadcast_to([P, HC, CTX]),
                                              head_of[:, :].unsqueeze(2).broadcast_to([P, HC, CTX]), ALU.mult)
                last.then_inc(kheads_ready, 1)

            def batch(j, b, nxt):
                if nxt is not None:
                    if normed:
                        norm_scale(*nxt)
                    spread_k(*nxt)
                p = b % 2
                pool.wait_ge(var_ready, 4 * j + (b + 1))
                link(pool.tensor_tensor(veps[:, p], mv[:, p, :, 1], eps[:, 0:T], ALU.add))
                pool.tensor_tensor(rstd[:, p], veps[:, p], minus_half[:, 0:T], ALU.pow).then_inc(rstd_ready, 1)

            link = Chain(pool, pool_chain, 4 * (1 + normed + masked))
            pool.memset(eps[:, :], LN_EPS)
            link(pool.memset(minus_half[:, :], -0.5))
            pool.wait_ge(w_loaded, 16 * len(loads))
            if normed:
                norm_scale(0, 0)
            spread_k(0, 0)
            link.begin(0)
            with pool.Fori(0, B // 4 - 1) as j:
                link.turn = j
                for b in range(4):
                    batch(j, b, (j, b + 1) if b < 3 else (j + 1, 0))
            link.end(B // 4 - 1)
            for b in range(4):
                batch(B // 4 - 1, b, (B // 4 - 1, b + 1) if b < 3 else None)

        @block.vector
        def _(dve):
            def norm_stats(j, b):
                p = b % 2
                dve.wait_ge(x_loaded[b], 16 * j + 16)
                for t in range(T):
                    dve.bn_stats(n_stats[:, p, t, :], x[:, b, t, :])
                dve.wait_ge(c_loaded[p], (2 * L) * j + L * (b // 2 + 1))
                link(dve.bn_stats(n_stats[0:CTX, p, T, :], cx[:, p, :]))
                dve.memset(spacer[:, :], 0.0)
                for t in range(T):
                    dve.bn_aggr(n_mv[:, p, t, :], n_stats[:, p, t, :])
                dve.bn_aggr(n_mv[0:CTX, p, T, :], n_stats[0:CTX, p, T, :]).then_inc(n_var, 1)
                if masked:
                    dve.tensor_scalar(seen[:, p, :], mask_i[:, p, :], 0.0, None, ALU.not_equal)
                    dve.tensor_scalar(fill_row[:, p, :], mask_i[0:3, p, :], 0.0, fillr[:, 0:1], ALU.is_equal, ALU.mult)

            def norm_apply(j, b):
                p = b % 2
                dve.wait_ge(n_rstd_ready, 4 * j + (b + 1))
                for t in range(T):
                    dve.tensor_scalar(xn[:, p, t, :], x[:, b, t, :], n_mv[:, p, t, 0:1], n_rstd[:, p, t:t + 1],
                                      ALU.subtract, ALU.mult)
                dve.tensor_scalar(cn[:, p, :], cx[:, p, :], n_mv[0:CTX, p, T, 0:1], n_rstd[0:CTX, p, T:T + 1],
                                  ALU.subtract, ALU.mult).then_inc(n_ready, 1)

            def unit(j, b, u):
                c = u % C
                dve.wait_ge(scores_made, (4 * U) * j + (U * b + u + 1))
                s = pS[c][:, :, 0:HB * CTX].rearrange("p g (h s) -> p g h s", h=HB)
                m = top[:, c, :].rearrange("p (g h) -> p g h", g=2)
                link(dve.tensor_reduce(m, s, AX.X, ALU.max))
                dve.tensor_tensor(low[:, u % 2].rearrange("p (g h s) -> p g h s", g=2, h=HB), s,
                                  m.unsqueeze(3).broadcast_to([P, 2, HB, CTX]), ALU.subtract).then_inc(low_ready, 1)

            def normalize(j, b, t):
                p = b % 2
                dve.wait_ge(o_made, 8 * j + (2 * b + t + 1))
                o = pG[t][:, 0:H * W].rearrange("p (h w) -> p h w", h=H)
                link(dve.reciprocal(rec[:, t, :], o[:, :, DH]))
                dve.tensor_tensor(on[:, p, t, :].rearrange("p (h e) -> p h e", h=H), o[:, :, 0:DH],
                                  rec[:, t, :].unsqueeze(2).broadcast_to([P, H, DH]), ALU.mult).then_inc(o_normed, 1)

            def batch(j, b, nxt):
                p = b % 2
                if nxt is not None and normed:
                    norm_stats(*nxt)
                unit(j, b, 0)
                unit(j, b, 1)
                if nxt is not None and normed:
                    norm_apply(*nxt)
                unit(j, b, 2)
                unit(j, b, 3)
                normalize(j, b, 0)
                normalize(j, b, 1)
                dve.wait_ge(proj_made, 4 * j + (b + 1))
                link(dve.tensor_tensor(r[:, p], pG[1][:, :].rearrange("p (t d) -> p t d", t=T), x[:, b], ALU.add))
                dve.sem_inc(res_added, 1)
                for t in range(T):
                    last = dve.bn_stats(stats[:, p, t, :], r[:, p, t, :])
                link(last)
                dve.memset(spacer[:, :], 0.0)
                for t in range(T):
                    last = dve.bn_aggr(mv[:, p, t, :], stats[:, p, t, :])
                last.then_inc(var_ready, 1)
                dve.wait_ge(rstd_ready, 4 * j + (b + 1))
                dve.wait_ge(y_stored[p], 32 * j + 16 * (b // 2 + 1))
                for t in range(T):
                    last = dve.tensor_scalar(y[:, p, t, :], r[:, p, t, :], mv[:, p, t, 0:1], rstd[:, p, t:t + 1],
                                             ALU.subtract, ALU.mult)
                last.then_inc(y_ready, 1)

            L = 16 * (1 + masked)
            link = Chain(dve, dve_chain, 4 * (U + 4 + normed))
            dve.wait_ge(w_loaded, 16 * len(loads))
            dve.memset(ones3[:, :], 1.0)
            dve.memset(n_mv[:, :, :, :], 1.0)
            dve.memset(v[:, :, :, DH:W], 1.0)
            if bv_d is None:
                link(dve.memset(bias3[:, 0:D], 0.0))
            split_in_three(link, bias3, rest3, parts3, ident, biasr)
            link(dve.memset(fill3[:, :], -1e9))
            split_in_three(link, fill3, fill_rest, fill_parts, ident, fillr)
            dve.sem_inc(setup_done, 1)
            dve.sem_inc(low_ready, 2)
            dve.sem_inc(res_added, 1)
            if normed:
                norm_stats(0, 0)
                norm_apply(0, 0)
            link.begin(0)
            with dve.Fori(0, B // 4 - 1) as j:
                link.turn = j
                for b in range(4):
                    batch(j, b, (j, b + 1) if b < 3 else (j + 1, 0))
            link.end(B // 4 - 1)
            for b in range(4):
                batch(B // 4 - 1, b, (B // 4 - 1, b + 1) if b < 3 else None)


def expert_attention(nc, x_in, x_out, wg_d, wq_d, wkv_d, wo_d, bqkv_d, bo_d, ln_d, ident_d, iota_d, posmask_d,
                     sum4_d, pick4_d):
    E, F, SP, G8, NG = H, 64, 4, 8, 8
    NT = NG * G8
    SL = 2 * SP
    ES = NT * SL
    xg_in = x_in.rearrange("b (g t s) d -> g s b t d", g=NG, t=G8)
    xg_out = x_out.rearrange("b (g t s) d -> g s b t d", g=NG, t=G8)
    with Stage(nc, "ea") as outer:
        ident = outer.sb("ident", [P, P])
        xg = outer.sb("xg", [P, 2, G8, D])
        sel = outer.sb("sel", [P, NT, P])
        hg = outer.sb("hg", [P, C, E, ES])

        def load_group(sp, g, q, sem_):
            for s in range(SP):
                sp.dma_start(xg[s * B:(s + 1) * B, q], xg_in[g][s]).then_inc(sem_, 16)

        with Stage(nc, "route") as st:
            sb, ps, sem = st.sb, st.ps, st.sem
            wg = sb("wg", [P, C, E])
            iota = sb("iota", [P, B])
            iota64 = sb("iota64", [P, B])
            posmask = sb("posmask", [P, SP])
            hT = sb("hT", [P, 2, C, P])
            lg = sb("lg", [P, NT, E])
            pr = sb("pr", [P, NT, E])
            tmax = sb("tmax", [P, NT])
            tsum = sb("tsum", [P, NT])
            SG = NG * SP
            pT = sb("pT", [P, SG, B])
            eq = sb("eq", [P, SG, B])
            m = sb("m", [P, SG])
            i1 = sb("i1", [P, SG])
            i2 = sb("i2", [P, SG])
            lo_hi = sb("lo_hi", [P, 2, SG])
            hot = sb("hot", [P, 2, SG, B])
            ph = [ps(f"ph{q}", [P, C, P]) for q in range(2)]
            pl = [ps(f"pl{q}", [P, G8, E]) for q in range(2)]
            pt = [ps(f"pt{q}", [P, 4, P]) for q in range(4)]
            w_loaded = sem("w_loaded")
            x_loaded = [sem(f"x_loaded{q}") for q in range(2)]
            hT_made, hT_copied, lg_made, lg_copied = sem("hT_made"), sem("hT_copied"), sem("lg_made"), sem("lg_copied")
            low_ready, exp_done, pr_ready = sem("low_ready"), sem("exp_done"), sem("pr_ready")
            pT_made, hot_ready, hotT_made = sem("pT_made"), sem("hot_ready"), sem("hotT_made")
            chain, sel_ready = sem("chain"), sem("sel_ready")
            block = st.block()
            loads = [(ident[:, :], ident_d), (wg[:, :, :], wg_d.rearrange("(c p) e -> p c e", p=P)),
                     (iota[:, :], iota_d), (posmask[:, :], posmask_d)]

            @block.sync
            def _(sp):
                for dst, src in loads:
                    sp.dma_start(dst, src).then_inc(w_loaded, 16)
                for q in range(2):
                    load_group(sp, q, q, x_loaded[q])
                with sp.Fori(0, NG // 2 - 1) as j:
                    for q in range(2):
                        sp.wait_ge(lg_made, 2 * j + (q + 1))
                        load_group(sp, 2 * j + (q + 2), q, x_loaded[q])

            @block.tensor
            def _(pe):
                pe.wait_ge(w_loaded, 16 * len(loads))

                def turn(j, q, t):
                    if t == 0:
                        pe.wait_ge(x_loaded[q], 64 * j + 64)
                    pe.wait_ge(hT_copied, (2 * G8) * j + (G8 * q + t + 1))
                    for c in range(C):
                        last = pe.transpose(ph[t % 2][:, c, :], xg[:, q, t, c * P:(c + 1) * P], ident[:, :])
                    last.then_inc(hT_made, 1)

                def score(j, q, t):
                    if t == 0:
                        pe.wait_ge(lg_copied, 2 * j + (q + 1))
                    pe.wait_ge(hT_copied, (2 * G8) * j + (G8 * q + t + 3))
                    for c in range(C):
                        last = pe.matmul(pl[q][:, t, :], hT[:, t % 2, c, :], wg[:, c, :], start=(c == 0), stop=(c == C - 1))
                    if t == G8 - 1:
                        last.then_inc(lg_made, 1)

                with pe.Fori(0, NG // 2) as j:
                    for q in range(2):
                        turn(j, q, 0)
                        for t in range(G8):
                            if t + 1 < G8:
                                turn(j, q, t + 1)
                            score(j, q, t)
                pe.wait_ge(pr_ready, 1)
                for g in range(NG):
                    last = pe.transpose(pt[g // 4][:, g % 4, :], pr[:, g * G8:(g + 1) * G8, :].rearrange("p t e -> p (t e)"), ident[:, :])
                    if g % 4 == 3:
                        last.then_inc(pT_made, 1)
                pe.wait_ge(hot_ready, 1)
                for i in range(2):
                    for g in range(NG):
                        n = (i * NG + g) // 4
                        last = pe.transpose(pt[n][:, g % 4, :], hot[:, i, g * SP:(g + 1) * SP, :].rearrange("p s b -> p (s b)"), ident[:, :])
                        if g % 4 == 3:
                            last.then_inc(hotT_made, 1)

            @block.scalar
            def _(act):
                act.sem_inc(hT_copied, 2)
                with act.Fori(0, NG // 2) as j:
                    for q in range(2):
                        for t in range(G8):
                            act.wait_ge(hT_made, (2 * G8) * j + (G8 * q + t + 1))
                            act.activation(hT[:, t % 2], ph[t % 2][:, :, :], ACT.Copy).then_inc(hT_copied, 1)
                act.wait_ge(low_ready, 1)
                act.activation(pr[:, :, :], lg[:, :, :], ACT.Exp).then_inc(exp_done, 1)

            @block.vector
            def _(dve):
                link = Chain(dve, chain, 0)
                dve.wait_ge(w_loaded, 16 * len(loads))
                link(dve.tensor_scalar(iota64[:, :], iota[:, :], 64.0, None, ALU.add))
                dve.sem_inc(lg_copied, 2)
                with dve.Fori(0, NG // 2) as j:
                    for q in range(2):
                        dve.wait_ge(lg_made, 2 * j + (q + 1))
                        dve.tensor_copy(lg[:, bass.ds((2 * G8) * j + G8 * q, G8), :], pl[q][:, :, :]).then_inc(lg_copied, 1)
                dve.wait_ge(lg_copied, NG + 2)
                link(dve.tensor_reduce(tmax[:, :], lg[:, :, :], AX.X, ALU.max))
                dve.tensor_tensor(lg[:, :, :], lg[:, :, :], tmax[:, :].unsqueeze(2).broadcast_to([P, NT, E]),
                                  ALU.subtract).then_inc(low_ready, 1)
                dve.wait_ge(exp_done, 1)
                link(dve.tensor_reduce(tsum[:, :], pr[:, :, :], AX.X, ALU.add))
                link(dve.reciprocal(tsum[:, :], tsum[:, :]))
                dve.tensor_tensor(pr[:, :, :], pr[:, :, :], tsum[:, :].unsqueeze(2).broadcast_to([P, NT, E]),
                                  ALU.mult).then_inc(pr_ready, 1)
                for n in range(2):
                    dve.wait_ge(pT_made, n + 1)
                    last = dve.tensor_copy(pT[:, n * 16:(n + 1) * 16, :].rearrange("p s b -> p (s b)"),
                                           pt[n][:, :, :].rearrange("p g t -> p (g t)"))
                link(last)

                def wide(a):
                    return a.unsqueeze(2).broadcast_to([P, SG, B])

                def row(a):
                    return a[:, :].unsqueeze(1).broadcast_to([P, SG, B])

                def first_of_top(index):
                    link(dve.tensor_reduce(m[:, :], pT[:, :, :], AX.X, ALU.max))
                    link(dve.tensor_tensor(eq[:, :, :], pT[:, :, :], wide(m[:, :]), ALU.is_equal))
                    link(dve.scalar_tensor_tensor(out=eq[:, :, :], in0=eq[:, :, :], scalar=-64.0, in1=row(iota64),
                                                  op0=ALU.mult, op1=ALU.add))
                    link(dve.tensor_reduce(index[:, :], eq[:, :, :], AX.X, ALU.min))

                first_of_top(i1)
                link(dve.tensor_tensor(eq[:, :, :], row(iota), wide(i1[:, :]), ALU.is_equal))
                link(dve.scalar_tensor_tensor(out=pT[:, :, :], in0=eq[:, :, :], scalar=-4.0, in1=pT[:, :, :],
                                              op0=ALU.mult, op1=ALU.add))
                first_of_top(i2)
                dve.tensor_tensor(lo_hi[:, 0, :], i1[:, :], i2[:, :], ALU.min)
                link(dve.tensor_tensor(lo_hi[:, 1, :], i1[:, :], i2[:, :], ALU.max))
                for i in range(2):
                    last = dve.tensor_tensor(hot[:, i], row(iota), wide(lo_hi[:, i, :]), ALU.is_equal)
                last.then_inc(hot_ready, 1)
                for i in range(2):
                    for g in range(NG):
                        n = (i * NG + g) // 4
                        dve.wait_ge(hotT_made, n + 1)
                        slots = sel[:, g * G8:(g + 1) * G8, :].rearrange("p t (e s i) -> p (t e) s i", e=E, i=2)[:, :, :, i]
                        dve.tensor_tensor(slots, pt[n][:, g % 4, :].unsqueeze(2).broadcast_to([P, P, SP]),
                                          posmask[:, :].unsqueeze(1).broadcast_to([P, P, SP]), ALU.mult).then_inc(sel_ready, 1)

        with Stage(nc, "gather") as st:
            sem = st.sem
            pg = [st.ps(f"pg{q}", [P, C, P]) for q in range(4)]
            x_loaded = [sem(f"x_loaded{q}") for q in range(2)]
            made, copied = sem("made"), sem("copied")
            block = st.block()

            @block.sync
            def _(sp):
                for q in range(2):
                    load_group(sp, q, q, x_loaded[q])
                with sp.Fori(0, NG // 2 - 1) as j:
                    for q in range(2):
                        sp.wait_ge(made, (2 * G8) * j + G8 * (q + 1))
                        load_group(sp, 2 * j + (q + 2), q, x_loaded[q])

            @block.tensor
            def _(pe):
                with pe.Fori(0, NG // 2) as j:
                    for q in range(2):
                        pe.wait_ge(x_loaded[q], 64 * j + 64)
                        for t in range(G8):
                            pe.wait_ge(copied, (2 * G8) * j + (G8 * q + t + 1))
                            for c in range(C):
                                last = pe.matmul(pg[t % 4][:, c, :], xg[:, q, t, c * P:(c + 1) * P],
                                                 sel[:, bass.ds((2 * G8) * j + (G8 * q + t), 1), :].rearrange("p o s -> p (o s)"),
                                                 start=True, stop=True)
                            last.then_inc(made, 1)

            @block.scalar
            def _(act):
                act.sem_inc(copied, 4)
                with act.Fori(0, NG // 2) as j:
                    for q in range(2):
                        for t in range(G8):
                            act.wait_ge(made, (2 * G8) * j + (G8 * q + t + 1))
                            act.activation(hg[:, :, :, bass.ds((2 * G8 * SL) * j + SL * (G8 * q + t), SL)],
                                           pg[t % 4][:, :, :].rearrange("p c (e s) -> p c e s", e=E), ACT.Copy).then_inc(copied, 1)

        with Stage(nc, "expert") as st:
            sb, ps, sem = st.sb, st.ps, st.sem
            wq = sb("wq", [P, 2, C, F])
            wkv = sb("wkv", [P, 2, C, 2 * F])
            wo = sb("wo", [P, 2, D])
            bqkv = sb("bqkv", [P, 2, 2])
            bo = sb("bo", [P, C])
            sum4 = sb("sum4", [F, 4, P])
            pick4 = sb("pick4", [4, 4, P])
            q_sb = sb("q", [F, 2, ES])
            kv = sb("kv", [P, 2, ES])
            prod = sb("prod", [F, 2, 4, S])
            nmax = sb("nmax", [4, 2])
            rsum = sb("rsum", [4, 2])
            prob = sb("prob", [4, 2, S])
            pv = sb("pv", [P, 4, S])
            av = sb("av", [P, 2, ES])
            pq, pkv, pa = ps("pq", [F, 512]), ps("pkv", [P, 512]), ps("pa", [P, 512])
            pb = ps("pb", [P, 4, S])
            po = [ps(f"po{c}", [P, 512]) for c in range(C)]
            w_loaded = [sem(f"w_loaded{q}") for q in range(2)]
            c_loaded = sem("c_loaded")
            q_made, kv_made, q_ready, kv_ready = sem("q_made"), sem("kv_made"), sem("q_ready"), sem("kv_ready")
            prod_ready, att_made, max_ready, exp_done = sem("prod_ready"), sem("att_made"), sem("max_ready"), sem("exp_done")
            prob_ready, spread_made, av_ready = sem("prob_ready"), sem("spread_made"), sem("av_ready")
            out_made, out_copied, chain = sem("out_made"), sem("out_copied"), sem("chain")
            block = st.block()
            PER = 4

            @block.sync
            def _(sp):
                for dst, src in ((sum4[:, :, :], sum4_d), (pick4[:, :, :], pick4_d), (bo[:, :], bo_d)):
                    sp.dma_start(dst, src).then_inc(c_loaded, 16)

                def load(h, q):
                    sp.dma_start(wq[:, q], wq_d[h].rearrange("(c p) f -> p c f", p=P)).then_inc(w_loaded[q], 16)
                    sp.dma_start(wkv[:, q], wkv_d[h].rearrange("(c p) f -> p c f", p=P)).then_inc(w_loaded[q], 16)
                    sp.dma_start(wo[F:P, q], wo_d[h]).then_inc(w_loaded[q], 16)
                    sp.dma_start(bqkv[:, q], bqkv_d[h]).then_inc(w_loaded[q], 16)

                load(0, 0)
                load(1, 1)
                with sp.Fori(0, E // 2 - 1) as j:
                    for q in range(2):
                        sp.wait_ge(out_made, 2 * j + (q + 1))
                        load(2 * j + (q + 2), q)

            @block.tensor
            def _(pe):
                def project(j, q):
                    pe.wait_ge(w_loaded[q], (16 * PER) * j + 16 * PER)
                    pe.wait_ge(kv_ready, 2 * j + (q + 1))
                    pe.wait_ge(q_ready, 2 * j + (q + 1))
                    for c in range(C):
                        tok = hg[:, c, bass.ds(2 * j + q, 1), :].rearrange("p o s -> p (o s)")
                        last = pe.matmul(pq[:, :], wq[:, q, c, :], tok, start=(c == 0), stop=(c == C - 1))
                    last.then_inc(q_made, 1)
                    for c in range(C):
                        tok = hg[:, c, bass.ds(2 * j + q, 1), :].rearrange("p o s -> p (o s)")
                        last = pe.matmul(pkv[:, :], wkv[:, q, c, :], tok, start=(c == 0), stop=(c == C - 1))
                    last.then_inc(kv_made, 1)

                def attend(j, q):
                    pe.wait_ge(prod_ready, 2 * j + (q + 1))
                    for n in range(4):
                        last = pe.matmul(pa[:, 0:S], sum4[:, n, :], prod[:, q, n, :], start=(n == 0), stop=(n == 3))
                    last.then_inc(att_made, 1)

                def mix(j, q):
                    pe.wait_ge(prob_ready, 2 * j + (q + 1))
                    pe.wait_ge(av_ready, 2 * j + (q + 1))
                    for n in range(4):
                        last = pe.matmul(pb[:, n, :], pick4[:, n, :], prob[:, q, :], start=True, stop=True)
                    last.then_inc(spread_made, 1)
                    pe.wait_ge(av_ready, 2 * j + (q + 2))
                    pe.wait_ge(out_copied, 2 * j + (q + 1))
                    for c in range(C):
                        last = pe.matmul(po[c][:, :], wo[F:P, q, c * P:(c + 1) * P], av[F:P, q, :], start=True, stop=True)
                    last.then_inc(out_made, 1)

                pe.wait_ge(c_loaded, 48)
                project(0, 0)
                with pe.Fori(0, E // 2 - 1) as j:
                    for q in range(2):
                        attend(j, q)
                        project(*((j, 1) if q == 0 else (j + 1, 0)))
                        mix(j, q)
                attend(E // 2 - 1, 0)
                project(E // 2 - 1, 1)
                mix(E // 2 - 1, 0)
                attend(E // 2 - 1, 1)
                mix(E // 2 - 1, 1)

            @block.scalar
            def _(act):
                def keys(j, q):
                    act.wait_ge(kv_made, 2 * j + (q + 1))
                    act.activation(kv[:, q, :], pkv[:, :], ACT.Identity, bias=bqkv[:, q, 0:1]).then_inc(kv_ready, 1)

                def rest(j, q, nxt):
                    act.wait_ge(max_ready, 2 * j + (q + 1))
                    act.activation(prob[:, q, :], pa[0:4, 0:S], ACT.Exp, bias=nmax[:, q:q + 1],
                                   accum_out=rsum[:, q:q + 1]).then_inc(exp_done, 1)
                    if nxt is not None:
                        keys(*nxt)
                    act.wait_ge(out_made, 2 * j + (q + 1))
                    for c in range(C):
                        last = act.activation(hg[:, c, bass.ds(2 * j + q, 1), :].rearrange("p o s -> p (o s)"), po[c][:, :],
                                              ACT.Identity, bias=bo[:, c:c + 1])
                    last.then_inc(out_copied, 1)

                act.sem_inc(kv_ready, 1)
                act.sem_inc(out_copied, 1)
                act.wait_ge(c_loaded, 48)
                keys(0, 0)
                with act.Fori(0, E // 2 - 1) as j:
                    rest(j, 0, (j, 1))
                    rest(j, 1, (j + 1, 0))
                rest(E // 2 - 1, 0, (E // 2 - 1, 1))
                rest(E // 2 - 1, 1, None)

            @block.vector
            def _(dve):
                def pairs(j, q):
                    dve.wait_ge(q_made, 2 * j + (q + 1))
                    dve.tensor_scalar(q_sb[:, q, :], pq[:, :], bqkv[0:F, q, 1:2], 0.125, ALU.add, ALU.mult).then_inc(q_ready, 1)
                    dve.wait_ge(q_ready, 2 * j + (q + 2))
                    dve.wait_ge(kv_ready, 2 * j + (q + 2))
                    dve.tensor_tensor(prod[:, q].rearrange("p (i k) b -> p i k b", i=2),
                                      q_sb[:, q, :].rearrange("p (b i) -> p i b", i=2).unsqueeze(2).broadcast_to([F, 2, 2, S]),
                                      kv[0:F, q, :].rearrange("p (b k) -> p k b", k=2).unsqueeze(1).broadcast_to([F, 2, 2, S]),
                                      ALU.mult).then_inc(prod_ready, 1)

                def softmax(j, q):
                    dve.wait_ge(att_made, 2 * j + (q + 1))
                    dve.tensor_reduce(nmax[:, q:q + 1], pa[0:4, 0:S], AX.X, ALU.max, negate=True).then_inc(max_ready, 1)
                    dve.wait_ge(exp_done, 2 * j + (q + 1))
                    link(dve.reciprocal(rsum[:, q:q + 1], rsum[:, q:q + 1]))
                    dve.tensor_scalar(prob[:, q, :], prob[:, q, :], rsum[:, q:q + 1], None, ALU.mult).then_inc(prob_ready, 1)

                def weigh(j, q):
                    dve.wait_ge(spread_made, 2 * j + (q + 1))
                    v = kv[F:P, q, :].rearrange("p (b k) -> p k b", k=2).unsqueeze(1).broadcast_to([F, 2, 2, S])
                    link(dve.tensor_tensor(pv[F:P].rearrange("p (i k) b -> p i k b", i=2),
                                           pb[F:P].rearrange("p (i k) b -> p i k b", i=2), v, ALU.mult))
                    w = pv[F:P].rearrange("p (i k) b -> p i k b", i=2)
                    dve.tensor_tensor(av[F:P, q, :].rearrange("p (b i) -> p i b", i=2), w[:, :, 0, :], w[:, :, 1, :],
                                      ALU.add).then_inc(av_ready, 1)

                link = Chain(dve, chain, 4)
                dve.sem_inc(q_ready, 1)
                dve.sem_inc(av_ready, 1)
                pairs(0, 0)
                link.begin(0)
                with dve.Fori(0, E // 2 - 1) as j:
                    link.turn = j
                    for q in range(2):
                        softmax(j, q)
                        pairs(*((j, 1) if q == 0 else (j + 1, 0)))
                        weigh(j, q)
                link.end(E // 2 - 1)
                softmax(E // 2 - 1, 0)
                pairs(E // 2 - 1, 1)
                weigh(E // 2 - 1, 0)
                softmax(E // 2 - 1, 1)
                weigh(E // 2 - 1, 1)

        with Stage(nc, "scatter") as st:
            sb, ps, sem = st.sb, st.ps, st.sem
            NP = G8 // 2
            slots = sb("slots", [P, 2, 2, C + 1, P])
            turned = sb("turned", [P, 2, 2, C + 1, P])
            ln_gb = sb("ln_gb", [P, 2, D])
            spacer = sb("spacer", [P, 1])
            eps = sb("eps", [P, 2])
            minus_half = sb("minus_half", [P, 2])
            r = sb("r", [P, 2, 2, D])
            z = sb("z", [P, 2, 2, D])
            r2 = sb("r2", [P, 2, 2, D])
            stats = sb("stats", [P, 2, 2, 6])
            mv = sb("mv", [P, 2, 2, 2])
            stats2 = sb("stats2", [P, 2, 2, 6])
            mv2 = sb("mv2", [P, 2, 2, 2])
            veps = sb("veps", [P, 2, 2])
            rstd = sb("rstd", [P, 2, 2])
            rstd2 = sb("rstd2", [P, 2, 2])
            yg = sb("yg", [P, G8, D])
            pt = [ps(f"pt{k}", [P, C + 1, P]) for k in range(4)]
            py = [ps(f"py{k}", [P, 2, D]) for k in range(2)]
            w_loaded = sem("w_loaded")
            x_loaded = [sem(f"x_loaded{q}") for q in range(2)]
            y_stored = sem("y_stored")
            slots_free = sem("slots_free")
            slots_ready, turn_made, turn_copied = sem("slots_ready"), sem("turn_made"), sem("turn_copied")
            y_made, res_added, var_ready, rstd_ready = sem("y_made"), sem("res_added"), sem("var_ready"), sem("rstd_ready")
            z_ready, r2_ready, var2_ready, rstd2_ready = sem("z_ready"), sem("r2_ready"), sem("var2_ready"), sem("rstd2_ready")
            y_ready, chain, pool_chain = sem("y_ready"), sem("chain"), sem("pool_chain")
            block = st.block()

            @block.sync
            def _(sp):
                for n in range(2):
                    sp.dma_start(ln_gb[:, n, :], ln_d[n].partition_broadcast(P)).then_inc(w_loaded, 16)
                for q in range(2):
                    load_group(sp, q, q, x_loaded[q])
                sp.sem_inc(y_stored, 64)

                def store(j, q):
                    sp.wait_ge(y_ready, (2 * NP) * j + NP * (q + 1))
                    for s in range(SP):
                        sp.dma_start(xg_out[2 * j + q][s], yg[s * B:(s + 1) * B]).then_inc(y_stored, 16)

                with sp.Fori(0, NG // 2 - 1) as j:
                    for q in range(2):
                        store(j, q)
                        load_group(sp, 2 * j + (q + 2), q, x_loaded[q])
                store(NG // 2 - 1, 0)
                store(NG // 2 - 1, 1)
                sp.wait_ge(y_stored, 64 * (NG + 1))

            @block.tensor
            def _(pe):
                def turn(n, k):
                    p = k % 2
                    pe.wait_ge(slots_ready, n)
                    pe.wait_ge(turn_copied, n)
                    for t in range(2):
                        for c in range(C + 1):
                            last = pe.transpose(pt[2 * p + t][:, c, :], slots[:, p, t, c, :], ident[:, :])
                    last.then_inc(turn_made, 1)

                def scatter(n, k):
                    p = k % 2
                    pe.wait_ge(turn_copied, n + 2)
                    pe.wait_ge(res_added, n)
                    for t in range(2):
                        last = pe.matmul(py[p][:, t, :], turned[:, p, t, C, :],
                                         turned[:, p, t, 0:C, :].rearrange("p c d -> p (c d)"), start=True, stop=True)
                    last.then_inc(y_made, 1)

                with pe.Fori(0, NG) as j:
                    turn(NP * j + 1, 0)
                    for k in range(NP):
                        if k + 1 < NP:
                            turn(NP * j + (k + 2), k + 1)
                        scatter(NP * j + (k + 1), k)

            @block.scalar
            def _(act):
                act.sem_inc(turn_copied, 2)
                with act.Fori(0, NG) as j:
                    for k in range(NP):
                        act.wait_ge(turn_made, NP * j + (k + 1))
                        for t in range(2):
                            last = act.activation(turned[:, k % 2, t], pt[2 * (k % 2) + t][:, :, :], ACT.Copy)
                        last.then_inc(turn_copied, 1)
                        act.sem_inc(slots_free, 1)

            @block.gpsimd
            def _(pool):
                def stage(n, g, k):
                    pool.wait_ge(slots_free, n)
                    for t in range(2):
                        tile = G8 * g + (2 * k + t)
                        pool.tensor_copy(slots[:, k % 2, t, 0:C, :].rearrange("p c (e s) -> p c e s", e=E),
                                         hg[:, :, :, bass.ds(tile * SL, SL)])
                        last = pool.tensor_copy(slots[:, k % 2, t, C, :], sel[:, bass.ds(tile, 1), :].rearrange("p o s -> p (o s)"))
                    last.then_inc(slots_ready, 1)

                def rstd_of(out, m, ready, done, n):
                    pool.wait_ge(ready, n)
                    link(pool.tensor_tensor(veps[:, 0], m, eps[:, :], ALU.add))
                    pool.tensor_tensor(out, veps[:, 0], minus_half[:, :], ALU.pow).then_inc(done, 1)

                def affine(n, k, q):
                    p = k % 2
                    pool.wait_ge(z_ready, n)
                    for a, b_, op in ((z[:, p], ln_gb[:, 0, :], ALU.mult), (z[:, p], ln_gb[:, 1, :], ALU.add)):
                        link(pool.tensor_tensor(z[:, p], a, b_.unsqueeze(1).broadcast_to([P, 2, D]), op))
                    pool.tensor_tensor(r2[:, p], z[:, p], xg[:, q, 2 * k:2 * k + 2, :], ALU.add).then_inc(r2_ready, 1)

                link = Chain(pool, pool_chain, 2 * NP * 4)
                pool.memset(eps[:, :], LN_EPS)
                link(pool.memset(minus_half[:, :], -0.5))
                pool.sem_inc(slots_free, 2)
                pool.wait_ge(w_loaded, 32)
                link.begin(0)
                with pool.Fori(0, NG // 2) as j:
                    link.turn = j
                    for q in range(2):
                        for k in range(NP):
                            n = (2 * NP) * j + (NP * q + k + 1)
                            if k == 0:
                                stage(n, 2 * j + q, 0)
                            if k + 1 < NP:
                                stage((2 * NP) * j + (NP * q + k + 2), 2 * j + q, k + 1)
                            rstd_of(rstd[:, k % 2], mv[:, k % 2, :, 1], var_ready, rstd_ready, n)
                            affine(n, k, q)
                            rstd_of(rstd2[:, k % 2], mv2[:, k % 2, :, 1], var2_ready, rstd2_ready, n)
                link.end(NG // 2)

            @block.vector
            def _(dve):
                def moments(st_, mv_, src, ready):
                    for t in range(2):
                        last = dve.bn_stats(st_[:, t, :], src[:, t, :])
                    link(last)
                    dve.memset(spacer[:, :], 0.0)
                    for t in range(2):
                        last = dve.bn_aggr(mv_[:, t, :], st_[:, t, :])
                    last.then_inc(ready, 1)

                def apply(out, src, mv_, rs):
                    for t in range(2):
                        last = dve.tensor_scalar(out[:, t, :], src[:, t, :], mv_[:, t, 0:1], rs[:, t:t + 1],
                                                 ALU.subtract, ALU.mult)
                    return last

                link = Chain(dve, chain, 2 * NP * 3)
                dve.sem_inc(res_added, 2)
                link.begin(0)
                with dve.Fori(0, NG // 2) as j:
                    link.turn = j
                    for q in range(2):
                        for k in range(NP):
                            p = k % 2
                            n = (2 * NP) * j + (NP * q + k + 1)
                            if k == 0:
                                dve.wait_ge(x_loaded[q], 64 * j + 64)
                                dve.wait_ge(y_stored, 128 * j + 64 * (q + 1))
                            dve.wait_ge(y_made, n)
                            link(dve.tensor_tensor(r[:, p], py[p][:, :, :], xg[:, q, 2 * k:2 * k + 2, :], ALU.add))
                            dve.sem_inc(res_added, 1)
                            moments(stats[:, p], mv[:, p], r[:, p], var_ready)
                            dve.wait_ge(rstd_ready, n)
                            apply(z[:, p], r[:, p], mv[:, p], rstd[:, p]).then_inc(z_ready, 1)
                            dve.wait_ge(r2_ready, n)
                            moments(stats2[:, p], mv2[:, p], r2[:, p], var2_ready)
                            dve.wait_ge(rstd2_ready, n)
                            apply(yg[:, 2 * k:2 * k + 2], r2[:, p], mv2[:, p], rstd2[:, p]).then_inc(y_ready, 1)
                link.end(NG // 2)


def mamba(nc, x_in, x_out, ct_dram, g_d, win_d, wout_d, conv_d, wx_d, dtp_d, alog_d, ident_d):
    DI = wout_d.shape[0]
    IC = DI // P
    N = alog_d.shape[2]
    GB = 2
    NG = B // GB
    TT = GB * T
    GS = GB * S
    xf_in = x_in.rearrange("(g b) (t p) d -> g p (b t) d", b=GB, p=P)
    xf_out = x_out.rearrange("(g b) (t p) d -> g p (b t) d", b=GB, p=P)
    with Stage(nc, "ma") as st:
        sb, ps, sem = st.sb, st.ps, st.sem
        ident = sb("ident", [P, P])
        gain = sb("gain", [P, C])
        win = sb("win", [P, C, 2 * DI])
        wout = sb("wout", [P, IC, D])
        wx = sb("wx", [P, IC, 2 * N + 1])
        conv = sb("conv", [P, IC, 5])
        dtp = sb("dtp", [P, 3, IC])
        A = sb("A", [P, IC, N])
        k256 = sb("k256", [P, TT])
        eps6 = sb("eps6", [P, TT])
        eps5 = sb("eps5", [P, TT])
        minus_half = sb("minus_half", [P, TT])
        spacer = sb("spacer", [P, 1])
        x = sb("x", [P, TT, D])
        xr = sb("xr", [P, TT, D])
        square = sb("square", [P, TT, D])
        ssq = sb("ssq", [P, TT])
        ms = sb("ms", [P, TT])
        rms = sb("rms", [P, TT])
        xn = sb("xn", [P, TT, D])
        xnT = sb("xnT", [P, C, GS])
        xc = sb("xc", [P, 2, IC, GS])
        sz = sb("sz", [P, 2, IC, GS])
        dt = sb("dt", [P, 2, IC, GS])
        par_t = sb("par_t", [P, 2, TT, 2 * N + 1])
        ct = sb("ct", [N + 1, GS])
        lrep = sb("lrep", [P, GS])
        av = sb("av", [P, IC, GS])
        ln1 = sb("ln1", [P, IC, GS])
        w1 = sb("w1", [P, IC, GS])
        uT = sb("uT", [P, 2, TT, DI])
        bu = sb("bu", [P, 2, TT, DI])
        a = sb("a", [P, 2, IC, GS])
        h = sb("h", [P, 2, IC, GS])
        crep = sb("crep", [P, 4, GS])
        ch = sb("ch", [P, 2, IC, GS])
        yv = w1
        r = sb("r", [P, TT, D])
        stats = sb("stats", [P, TT, 6])
        mv = sb("mv", [P, TT, 2])
        veps = sb("veps", [P, TT])
        rstd = sb("rstd", [P, TT])
        y = sb("y", [P, TT, D])
        u = av
        py = [ps(f"py{c}", [P, GS]) for c in range(IC)]
        pbu = [ps(f"pbu{k}", [P, GS]) for k in range(2)]
        pm = [ps(f"pm{k}", [P, GS]) for k in range(2)]

        w_loaded, x_loaded, xr_loaded, y_stored = sem("w_loaded"), sem("x_loaded"), sem("xr_loaded"), sem("y_stored")
        ct_stored, lrep_loaded = sem("ct_stored"), sem("lrep_loaded")
        crep_loaded = [sem(f"crep_loaded{k}") for k in range(4)]
        setup_done, ssq_ready, rms_ready, xn_ready = sem("setup_done"), sem("ssq_ready"), sem("rms_ready"), sem("xn_ready")
        xT_made, xT_copied, in_made = sem("xT_made"), sem("xT_copied"), sem("in_made")
        conv_done, z_copied, silu_done = sem("conv_done"), sem("z_copied"), sem("silu_done")
        par_made, par_copied, ct_made, ct_copied = sem("par_made"), sem("par_copied"), sem("ct_made"), sem("ct_copied")
        ln_ready, dt_ready, u_ready, uT_made, uT_copied = sem("ln_ready"), sem("dt_ready"), sem("u_ready"), sem("uT_made"), sem("uT_copied")
        bu_ready, bu_turned, a_ready, scanned = sem("bu_ready"), sem("bu_turned"), sem("a_ready"), sem("scanned")
        multiplied, summed, gated, yv_ready = sem("multiplied"), sem("summed"), sem("gated"), sem("yv_ready")
        out_made, res_added, var_ready, rstd_ready, y_ready = sem("out_made"), sem("res_added"), sem("var_ready"), sem("rstd_ready"), sem("y_ready")
        act_chain, dve_chain, pool_chain = sem("act_chain"), sem("dve_chain"), sem("pool_chain")
        block = st.block()
        loads = [(ident[:, :], ident_d), (gain[:, :], g_d), (win[:, :, :], win_d.rearrange("(c p) f -> p c f", p=P)),
                 (wout[:, :, :], wout_d.rearrange("(c p) f -> p c f", p=P)),
                 (wx[:, :, :], wx_d.rearrange("(c p) f -> p c f", p=P)),
                 (conv[:, :, :], conv_d), (dtp[:, :, :], dtp_d), (A[:, :, :], alog_d)]

        def groups(eng, group, link=None, turns=NG // 2 - 1):
            if link:
                link.turn = None
            group(0, 0, True, False)
            if link:
                link.begin(0)
            with eng.Fori(0, turns) as j:
                if link:
                    link.turn = j
                group(2 * j + 1, 1, False, False)
                group(2 * j + 2, 0, False, False)
            if link:
                link.end(turns)
            for g in range(2 * turns + 1, NG):
                group(g, g % 2, False, g == NG - 1)

        @block.sync
        def _(sp):
            def load_x(g):
                sp.dma_start(x[:, :, :], xf_in[g]).then_inc(x_loaded, 16)

            def load_c(g, par, s):
                sp.dma_start(crep[:, s % 4, :], ct_dram[par, s, :].partition_broadcast(P)).then_inc(crep_loaded[s % 4], 16)

            def spread(g, par):
                sp.wait_ge(ct_copied, g + 1)
                sp.dma_start(ct_dram[par], ct[:, :]).then_inc(ct_stored, 16)
                sp.wait_ge(ct_stored, 16 * g + 32)
                sp.dma_start(lrep[:, :], ct_dram[par, N, :].partition_broadcast(P)).then_inc(lrep_loaded, 16)

            def group(g, par, first, last):
                for s in range(N):
                    if s == 2 and not last:
                        if not (type(g) is int and g + 2 >= NG):
                            sp.wait_ge(xn_ready, g + 2)
                            load_x(g + 2)
                    if s == 5:
                        if not first:
                            sp.wait_ge(y_ready, g)
                            sp.dma_start(xf_out[g - 1], y[:, :, :]).then_inc(y_stored, 16)
                        sp.dma_start(xr[:, :, :], xf_in[g]).then_inc(xr_loaded, 16)
                    if s == 9 and not last:
                        spread(g + 1, 1 - par)
                    sp.wait_ge(multiplied, N * g + (s + 3))
                    if s + 4 < N:
                        load_c(g, par, s + 4)
                    elif not last:
                        load_c(g + 1, 1 - par, s + 4 - N)

            for dst, src in loads:
                sp.dma_start(dst, src).then_inc(w_loaded, 16)
            sp.sem_inc(y_stored, 16)
            sp.sem_inc(ct_stored, 16)
            load_x(0)
            sp.wait_ge(xn_ready, 1)
            load_x(1)
            spread(0, 0)
            for s in range(4):
                load_c(0, 0, s)
            groups(sp, group, turns=NG // 2 - 2)
            sp.wait_ge(y_ready, NG)
            sp.dma_start(xf_out[NG - 1], y[:, :, :]).then_inc(y_stored, 16)
            sp.wait_ge(y_stored, 16 * (NG + 1))

        @block.tensor
        def _(pe):
            def turn_x(n, c):
                if c == 0:
                    pe.wait_ge(xn_ready, n + 1)
                    if not (type(n) is int and n == 0):
                        pe.wait_ge(uT_copied, 4 * n)
                for t in range(TT):
                    last = pe.transpose(pm[c][:, t * P:(t + 1) * P], xn[:, t, c * P:(c + 1) * P], ident[:, :])
                last.then_inc(xT_made, 1)

            def project_in(n, f, after_out):
                if f == 0:
                    pe.wait_ge(xT_copied, 2 * n + 2)
                    if after_out:
                        pe.wait_ge(res_added, 2 * n - 2)
                elif f >= 2:
                    pe.wait_ge(conv_done if f < 6 else z_copied, 4 * n + (f - 1 if f < 6 else f - 5))
                for c in range(C):
                    last = pe.matmul(pm[f % 2][:, :], win[:, c, f * P:(f + 1) * P], xnT[:, c, :],
                                     start=(c == 0), stop=(c == C - 1))
                last.then_inc(in_made, 1)

            def parameters(n, par):
                pe.wait_ge(silu_done, n + 1)
                pe.wait_ge(z_copied, 4 * n + 4)
                for t in range(TT):
                    for c in range(IC):
                        last = pe.matmul(pm[0][:, t * 64:t * 64 + 2 * N + 1], xc[:, par, c, t * P:(t + 1) * P], wx[:, c, :],
                                         start=(c == 0), stop=(c == IC - 1))
                last.then_inc(par_made, 1)
                for c in range(IC):
                    last = pe.matmul(pm[1][0:N + 1, :], wx[:, c, N:2 * N + 1], xc[:, par, c, :],
                                     start=(c == 0), stop=(c == IC - 1))
                last.then_inc(ct_made, 1)

            def turn_u(n, t):
                if t == 0:
                    pe.wait_ge(u_ready, n + 1)
                    pe.wait_ge(par_copied, n + 1)
                elif t == 1:
                    pe.wait_ge(ct_copied, n + 1)
                else:
                    pe.wait_ge(uT_copied, 4 * n + (t - 1))
                for c in range(IC):
                    last = pe.transpose(pm[t % 2][:, c * P:(c + 1) * P], u[:, c, t * P:(t + 1) * P], ident[:, :])
                last.then_inc(uT_made, 1)

            def inputs(g, s):
                pe.wait_ge(bu_ready, N * g + (s + 1))
                for c in range(IC):
                    pe.wait_ge(scanned, (N * IC) * g + (IC * s + c + 7))
                    for t in range(TT):
                        last = pe.transpose(pbu[c % 2][:, t * P:(t + 1) * P], bu[:, s % 2, t, c * P:(c + 1) * P], ident[:, :])
                    last.then_inc(bu_turned, 1)

            def sum_states(g, s):
                pe.wait_ge(multiplied, N * g + (s + 3))
                if s == 0:
                    pe.wait_ge(gated, g + 1)
                for c in range(IC):
                    last = pe.matmul(py[c][:, :], ident[:, :], ch[:, s % 2, c, :], start=(s == 0), stop=(s == N - 1))
                last.then_inc(summed, 1)

            def project_out(g, k, prep):
                if k == 0:
                    pe.wait_ge(yv_ready, g + 1)
                    if prep:
                        pe.wait_ge(xT_copied, 2 * g + 6)
                    else:
                        pe.wait_ge(uT_copied, 4 * g + 8)
                for t in range(2):
                    for c in range(IC):
                        last = pe.matmul(pm[k][:, t * D:(t + 1) * D], yv[:, c, (2 * k + t) * P:(2 * k + t + 1) * P],
                                         wout[:, c, :], start=(c == 0), stop=(c == IC - 1))
                last.then_inc(out_made, 1)

            def group(g, par, first, last):
                n, prep = g + 1, not last
                for s in range(N):
                    inputs(g, s)
                    if s == 2 and prep:
                        turn_x(n, 0)
                        turn_x(n, 1)
                    if s == 3 and not first:
                        project_out(g - 1, 0, prep)
                        project_out(g - 1, 1, prep)
                    if 4 <= s < 8 and prep:
                        project_in(n, 2 * (s - 4), not first)
                        project_in(n, 2 * (s - 4) + 1, not first)
                    if s == 9 and prep:
                        parameters(n, 1 - par)
                    if s in (13, 14) and prep:
                        turn_u(n, 2 * (s - 13))
                        turn_u(n, 2 * (s - 13) + 1)
                    if s >= 2:
                        sum_states(g, s - 2)
                    elif not first:
                        sum_states(g - 1, N + s - 2)

            pe.wait_ge(w_loaded, 16 * len(loads))
            turn_x(0, 0)
            turn_x(0, 1)
            for f in range(2 * IC):
                project_in(0, f, False)
            parameters(0, 0)
            for t in range(TT):
                turn_u(0, t)
            groups(pe, group)
            sum_states(NG - 1, N - 2)
            sum_states(NG - 1, N - 1)
            pe.wait_ge(yv_ready, NG)
            pe.wait_ge(res_added, 2 * NG - 2)
            for k in range(2):
                for t in range(2):
                    for c in range(IC):
                        last = pe.matmul(pm[k][:, t * D:(t + 1) * D], yv[:, c, (2 * k + t) * P:(2 * k + t + 1) * P],
                                         wout[:, c, :], start=(c == 0), stop=(c == IC - 1))
                last.then_inc(out_made, 1)

        @block.scalar
        def _(act):
            link = Chain(act, act_chain, 2 * 2)

            def squares(n):
                act.wait_ge(x_loaded, 16 * n + 16)
                for t in range(TT):
                    last = act.activation(square[:, t, :], x[:, t, :], ACT.Square, accum_out=ssq[:, t:t + 1])
                last.then_inc(ssq_ready, 1)

            def copy_xT(n, c):
                act.wait_ge(xT_made, 2 * n + (c + 1))
                act.activation(xnT[:, c, :], pm[c][:, :], ACT.Copy, scale=gain[:, c:c + 1]).then_inc(xT_copied, 1)

            def copy_z(n, par, f):
                act.wait_ge(in_made, 8 * n + (IC + f + 1))
                act.activation(sz[:, par, f, :], pm[f % 2][:, :], ACT.Copy).then_inc(z_copied, 1)

            def silu(n, par):
                act.wait_ge(z_copied, 4 * n + 4)
                act.activation(sz[:, par], sz[:, par], ACT.Silu)
                act.wait_ge(conv_done, 4 * n + 4)
                act.activation(xc[:, par], xc[:, par], ACT.Silu).then_inc(silu_done, 1)

            def copy_parameters(n, par):
                act.wait_ge(par_made, n + 1)
                act.activation(par_t[:, par], pm[0][:, 0:TT * 64].rearrange("p (t k) -> p t k", k=64)[:, :, 0:2 * N + 1],
                               ACT.Copy).then_inc(par_copied, 1)
                act.wait_ge(ct_made, n + 1)
                act.wait_ge(ct_stored, 16 * n + 16)
                act.activation(ct[:, :], pm[1][0:N + 1, :], ACT.Copy).then_inc(ct_copied, 1)

            def step_size(n, par):
                act.wait_ge(lrep_loaded, 16 * n + 16)
                for c in range(IC):
                    act.activation(dt[:, par, c, :], lrep[:, :], ACT.Relu, bias=dtp[:, 1, c:c + 1], scale=dtp[:, 0, c:c + 1])
                    last = act.activation(av[:, c, :], lrep[:, :], ACT.Abs, bias=dtp[:, 1, c:c + 1], scale=dtp[:, 0, c:c + 1])
                link(last)
                link(act.activation(av[:, :, :], av[:, :, :], ACT.Exp, scale=-1.0))
                act.activation(ln1[:, :, :], av[:, :, :], ACT.Ln, bias=1.0).then_inc(ln_ready, 1)

            def copy_uT(n, par, t):
                act.wait_ge(uT_made, 4 * n + (t + 1))
                act.activation(uT[:, par, t, :], pm[t % 2][:, :], ACT.Copy).then_inc(uT_copied, 1)

            def scale_b(g, par, s):
                if s == 0:
                    act.wait_ge(uT_copied, 4 * g + 4)
                    act.wait_ge(par_copied, g + 1)
                act.wait_ge(bu_turned, (N * IC) * g + (IC * s + 4))
                for t in range(TT):
                    last = act.activation(bu[:, s % 2, t, :], uT[:, par, t, :], ACT.Copy, scale=par_t[:, par, t, s:s + 1])
                last.then_inc(bu_ready, 1)

            def decay(g, par, s):
                if s == 0:
                    act.wait_ge(dt_ready, g + 1)
                for c in range(IC):
                    act.wait_ge(scanned, (N * IC) * g + (IC * s + c + 1))
                    act.activation(a[:, s % 2, c, :].rearrange("p (b t) -> p b t", b=GB)[:, :, 1:S],
                                   dt[:, par, c, :].rearrange("p (b t) -> p b t", b=GB)[:, :, 1:S],
                                   ACT.Exp, scale=A[:, c, s:s + 1]).then_inc(a_ready, 1)

            def group(g, par, first, last):
                n, prep, np_ = g + 1, not last, 1 - par
                for s in range(N):
                    decay(g, par, s)
                    if s == 0 and prep:
                        squares(n)
                    if s == 2 and prep:
                        copy_xT(n, 0)
                        copy_xT(n, 1)
                    if s in (6, 7) and prep:
                        copy_z(n, np_, 2 * (s - 6))
                        copy_z(n, np_, 2 * (s - 6) + 1)
                    if s == 8 and prep:
                        silu(n, np_)
                    if s == 9 and prep:
                        copy_parameters(n, np_)
                    if s == 11 and prep:
                        step_size(n, np_)
                    if s in (13, 14) and prep:
                        copy_uT(n, np_, 2 * (s - 13))
                        copy_uT(n, np_, 2 * (s - 13) + 1)
                    if s + 1 < N:
                        scale_b(g, par, s + 1)
                    elif prep:
                        scale_b(n, np_, 0)

            act.wait_ge(w_loaded, 16 * len(loads))
            link(act.activation(A[:, :, :], A[:, :, :], ACT.Exp))
            link(act.activation(A[:, :, :], A[:, :, :], ACT.Copy, scale=-1.0))
            act.wait_ge(setup_done, 1)
            squares(0)
            copy_xT(0, 0)
            copy_xT(0, 1)
            for f in range(IC):
                copy_z(0, 0, f)
            silu(0, 0)
            copy_parameters(0, 0)
            step_size(0, 0)
            for t in range(TT):
                copy_uT(0, 0, t)
            scale_b(0, 0, 0)
            groups(act, group, link)

        @block.gpsimd
        def _(pool):
            link = Chain(pool, pool_chain, 2 * 3)

            def rms_scale(n):
                pool.wait_ge(ssq_ready, n + 1)
                link(pool.tensor_tensor(ms[:, :], ssq[:, :], k256[:, :], ALU.mult))
                link(pool.tensor_tensor(ms[:, :], ms[:, :], eps6[:, :], ALU.add))
                pool.tensor_tensor(rms[:, :], ms[:, :], minus_half[:, :], ALU.pow).then_inc(rms_ready, 1)

            def times_c(g, s):
                pool.wait_ge(scanned, (N * IC) * g + (IC * s + IC + 8))
                pool.wait_ge(crep_loaded[s % 4], (4 * 16) * g + 16 * (s // 4 + 1))
                pool.wait_ge(summed, N * g + (s + 1))
                pool.tensor_tensor(ch[:, s % 2], h[:, s % 2], crep[:, s % 4, :].unsqueeze(1).broadcast_to([P, IC, GS]),
                                   ALU.mult).then_inc(multiplied, 1)

            def rstd_of(g):
                pool.wait_ge(var_ready, g + 1)
                link(pool.tensor_tensor(veps[:, :], mv[:, :, 1], eps5[:, :], ALU.add))
                pool.tensor_tensor(rstd[:, :], veps[:, :], minus_half[:, :], ALU.pow).then_inc(rstd_ready, 1)

            def group(g, par, first, last):
                for s in range(N):
                    if s == 1 and not last:
                        rms_scale(g + 1)
                    if s == 4 and not first:
                        rstd_of(g - 1)
                    times_c(g, s)

            pool.memset(k256[:, :], 1.0 / D)
            pool.memset(eps6[:, :], 1e-6)
            pool.memset(eps5[:, :], LN_EPS)
            link(pool.memset(minus_half[:, :], -0.5))
            pool.sem_inc(multiplied, 2)
            pool.sem_inc(summed, 2)
            rms_scale(0)
            groups(pool, group, link)
            rstd_of(NG - 1)

        @block.vector
        def _(dve):
            link = Chain(dve, dve_chain, 2 * (4 * 4 + 3 + 1 + 1))

            def normalize(n):
                dve.wait_ge(rms_ready, n + 1)
                for t in range(TT):
                    last = dve.tensor_scalar(xn[:, t, :], x[:, t, :], rms[:, t:t + 1], None, ALU.mult)
                last.then_inc(xn_ready, 1)

            def convolve(n, par, f):
                dve.wait_ge(in_made, 8 * n + (f + 1))
                out = xc[:, par, f, :].rearrange("p (b t) -> p b t", b=GB)
                src = pm[f % 2][:, :].rearrange("p (b t) -> p b t", b=GB)
                link(dve.tensor_scalar(out, src, conv[:, f, 3:4], conv[:, f, 4:5], ALU.mult, ALU.add))
                for k in range(1, 4):
                    link(dve.scalar_tensor_tensor(out=out[:, :, k:S], in0=src[:, :, 0:S - k], scalar=conv[:, f, 3 - k:4 - k],
                                                  in1=out[:, :, k:S], op0=ALU.mult, op1=ALU.add))
                dve.sem_inc(conv_done, 1)

            def step_size(n, par):
                dve.wait_ge(ln_ready, n + 1)
                link(dve.tensor_scalar(w1[:, :, :], av[:, :, :], 1.0, 1.0, ALU.add, ALU.subtract))
                dve.tensor_tensor(dt[:, par], dt[:, par], ln1[:, :, :], ALU.add)
                link(dve.tensor_tensor(w1[:, :, :], av[:, :, :], w1[:, :, :], ALU.subtract))
                link(dve.tensor_tensor(dt[:, par], dt[:, par], w1[:, :, :], ALU.add))
                dve.sem_inc(dt_ready, 1)
                dve.tensor_tensor(u[:, :, :], dt[:, par], xc[:, par], ALU.mult).then_inc(u_ready, 1)

            def scans(g, s):
                dve.wait_ge(multiplied, N * g + (s + 1))
                for c in range(IC):
                    m = (N * IC) * g + (IC * s + c + 1)
                    dve.wait_ge(a_ready, m)
                    dve.wait_ge(bu_turned, m + 8)
                    dve.tensor_tensor_scan(out=h[:, s % 2, c, :], data0=a[:, s % 2, c, :], data1=pbu[c % 2][:, :],
                                           initial=0.0, op0=ALU.mult, op1=ALU.add).then_inc(scanned, 1)

            def gate(g, par):
                dve.wait_ge(summed, N * g + (N + 2))
                for c in range(IC):
                    last = dve.scalar_tensor_tensor(out=yv[:, c, :], in0=xc[:, par, c, :], scalar=dtp[:, 2, c:c + 1],
                                                    in1=py[c][:, :], op0=ALU.mult, op1=ALU.add)
                link(last)
                dve.sem_inc(gated, 1)
                dve.tensor_tensor(yv[:, :, :], yv[:, :, :], sz[:, par], ALU.mult).then_inc(yv_ready, 1)

            def residual(g, k):
                dve.wait_ge(out_made, 2 * g + (k + 1))
                if k == 0:
                    dve.wait_ge(xr_loaded, 16 * g + 16)
                dve.scalar_tensor_tensor(out=r[:, 2 * k:2 * k + 2, :], in0=xr[:, 2 * k:2 * k + 2, :], scalar=2.0,
                                         in1=pm[k][:, :].rearrange("p (t d) -> p t d", t=2),
                                         op0=ALU.mult, op1=ALU.add).then_inc(res_added, 1)
                if k == 1:
                    dve.wait_ge(res_added, 2 * g + 2)
                    for t in range(TT):
                        last = dve.bn_stats(stats[:, t, :], r[:, t, :])
                    link(last)
                    dve.memset(spacer[:, :], 0.0)
                    for t in range(TT):
                        last = dve.bn_aggr(mv[:, t, :], stats[:, t, :])
                    last.then_inc(var_ready, 1)

            def finish(g):
                dve.wait_ge(rstd_ready, g + 1)
                dve.wait_ge(y_stored, 16 * g + 16)
                for t in range(TT):
                    last = dve.tensor_scalar(y[:, t, :], r[:, t, :], mv[:, t, 0:1], rstd[:, t:t + 1], ALU.subtract, ALU.mult)
                last.then_inc(y_ready, 1)

            def group(g, par, first, last):
                n, prep, np_ = g + 1, not last, 1 - par
                for s in range(N):
                    if s == 2 and not first:
                        gate(g - 1, 1 - par)
                    scans(g, s)
                    if s == 1 and prep:
                        normalize(n)
                    if s == 3 and not first:
                        residual(g - 1, 0)
                        residual(g - 1, 1)
                    if s == 4 and not first:
                        finish(g - 1)
                    if s in (4, 5) and prep:
                        convolve(n, np_, 2 * (s - 4))
                        convolve(n, np_, 2 * (s - 4) + 1)
                    if s == 12 and prep:
                        step_size(n, np_)

            for p in range(2):
                dve.memset(a[:, p], 0.0)
            link(dve.memset(spacer[:, :], 0.0))
            dve.sem_inc(setup_done, 1)
            dve.sem_inc(bu_turned, 8)
            dve.sem_inc(scanned, 8)
            dve.sem_inc(gated, 1)
            dve.wait_ge(w_loaded, 16 * len(loads))
            normalize(0)
            for f in range(IC):
                convolve(0, 0, f)
            step_size(0, 0)
            groups(dve, group, link)
            gate(NG - 1, 1)
            residual(NG - 1, 0)
            residual(NG - 1, 1)
            finish(NG - 1)


def bit_ffn(nc, x_in, x_out, wgu_d, wd_d, ident_d):
    I = wd_d.shape[0]
    IC = I // P
    ROUND = 12582912.0
    FLOOR = 1e-5
    NT = 2 * B
    BT = 8
    with Stage(nc, "ff") as st:
        sb, ps, sem = st.sb, st.ps, st.sem
        ident = sb("ident", [P, P])
        identb = sb("identb", [P, P], bf16)
        ones = sb("ones", [P, P])
        wgu_f = sb("wgu_f", [P, 2, C, I])
        wd_f = sb("wd_f", [P, IC, D])
        wgu = sb("wgu", [P, 2, C, I], bf16)
        wd = sb("wd", [P, IC, D], bf16)
        wsum = sb("wsum", [P, 3])
        wmean = sb("wmean", [P, 3])
        wscale = sb("wscale", [P, 3])
        wm127 = sb("wm127", [P, 3])
        eps = sb("eps", [P, 1])
        minus_half = sb("minus_half", [P, 1])
        spacer = sb("spacer", [P, 1])
        x = sb("x", [P, 4, T, D])
        xmax = sb("xmax", [P, 2])
        xs = sb("xs", [P, 1])
        fgu = sb("fgu", [P, 2, 2])
        xr = sb("xr", [P, D])
        xq = sb("xq", [P, D], bf16)
        xT = sb("xT", [P, C, P], bf16)
        g = sb("g", [P, I])
        h = sb("h", [P, I])
        hmax = sb("hmax", [P, 2])
        hs = sb("hs", [P, 1])
        fd = sb("fd", [P, 2])
        hr = sb("hr", [P, I])
        hq = sb("hq", [P, I], bf16)
        hT = sb("hT", [P, IC, P], bf16)
        r = sb("r", [P, 2, D])
        stats = sb("stats", [P, 2, 6])
        mv = sb("mv", [P, 2, 2])
        veps = sb("veps", [P, 1])
        rstd = sb("rstd", [P, 2])
        y = sb("y", [P, 2, T, D])
        pgate, pup = ps("pgate", [P, I]), ps("pup", [P, I])
        px, ph, pd = ps("px", [P, C, P], bf16), ps("ph", [P, IC, P], bf16), ps("pd", [P, 512])

        w_loaded, wsum_ready, wtotal_made, setup_done = sem("w_loaded"), sem("wsum_ready"), sem("wtotal_made"), sem("setup_done")
        x_loaded = [sem(f"x_loaded{b}") for b in range(4)]
        y_stored = [sem(f"y_stored{p}") for p in range(2)]
        xq_ready, xT_made, xT_copied = sem("xq_ready"), sem("xT_made"), sem("xT_copied")
        gate_made, up_made, g_ready, h_ready, hs_ready = sem("gate_made"), sem("up_made"), sem("g_ready"), sem("h_ready"), sem("hs_ready")
        hr_ready, hq_ready, hT_made, hT_copied = sem("hr_ready"), sem("hq_ready"), sem("hT_made"), sem("hT_copied")
        down_made, var_ready, rstd_ready, y_ready = sem("down_made"), sem("var_ready"), sem("rstd_ready"), sem("y_ready")
        chain, pool_chain = sem("chain"), sem("pool_chain")
        block = st.block()

        @block.sync
        def _(sp):
            for dst, src in ((ident[:, :], ident_d), (wgu_f[:, 0], wgu_d[0].rearrange("(c p) i -> p c i", p=P)),
                             (wgu_f[:, 1], wgu_d[1].rearrange("(c p) i -> p c i", p=P)),
                             (wd_f[:, :, :], wd_d.rearrange("(c p) f -> p c f", p=P))):
                sp.dma_start(dst, src).then_inc(w_loaded, 16)
            for b in range(4):
                sp.dma_start(x[:, b], batch_tiles(x_in, b)).then_inc(x_loaded[b], 16)
            for p in range(2):
                sp.sem_inc(y_stored[p], 16)

            def store(j, b):
                sp.wait_ge(y_ready, BT * j + 2 * (b + 1))
                sp.dma_start(batch_tiles(x_out, 4 * j + b), y[:, b % 2]).then_inc(y_stored[b % 2], 16)

            with sp.Fori(0, B // 4 - 1) as j:
                for b in range(4):
                    store(j, b)
                    sp.dma_start(x[:, b], batch_tiles(x_in, 4 * j + (b + 4))).then_inc(x_loaded[b], 16)
            for b in range(4):
                store(B // 4 - 1, b)
            for p in range(2):
                sp.wait_ge(y_stored[p], 16 * (B // 2 + 1))

        @block.tensor
        def _(pe):
            def turn_x(j, k):
                pe.wait_ge(xq_ready, BT * j + (k + 1))
                for c in range(C):
                    last = pe.transpose(px[:, c, :], xq[:, c * P:(c + 1) * P], identb[:, :])
                last.then_inc(xT_made, 1)

            def gate_up(j, k):
                pe.wait_ge(xT_copied, BT * j + (k + 1))
                pe.wait_ge(h_ready, BT * j + (k + 1))
                for m, out, done in ((0, pgate, gate_made), (1, pup, up_made)):
                    for half in range(2):
                        for c in range(C):
                            last = pe.matmul(out[:, half * 512:(half + 1) * 512], xT[:, c, :],
                                             wgu[:, m, c, half * 512:(half + 1) * 512], start=(c == 0), stop=(c == C - 1))
                    last.then_inc(done, 1)

            def down(j, k):
                pe.wait_ge(hq_ready, BT * j + (k + 1))
                for c in range(IC):
                    last = pe.transpose(ph[:, c, :], hq[:, c * P:(c + 1) * P], identb[:, :])
                last.then_inc(hT_made, 1)
                pe.wait_ge(hT_copied, BT * j + (k + 1))
                for c in range(IC):
                    last = pe.matmul(pd[:, 0:D], hT[:, c, :], wd[:, c, :], start=(c == 0), stop=(c == IC - 1))
                last.then_inc(down_made, 1)

            pe.wait_ge(wsum_ready, 1)
            pe.matmul(pd[:, 0:3], ones[:, :], wsum[:, :], start=True, stop=True).then_inc(wtotal_made, 1)
            pe.wait_ge(setup_done, 1)
            with pe.Fori(0, NT // BT) as j:
                turn_x(j, 0)
                gate_up(j, 0)
                for k in range(BT):
                    if k + 1 < BT:
                        turn_x(j, k + 1)
                        gate_up(j, k + 1)
                    down(j, k)

        @block.scalar
        def _(act):
            def copy_x(j, k):
                act.wait_ge(xT_made, BT * j + (k + 1))
                act.activation(xT[:, :, :], px[:, :, :], ACT.Copy).then_inc(xT_copied, 1)

            act.wait_ge(setup_done, 1)
            with act.Fori(0, NT // BT) as j:
                copy_x(j, 0)
                for k in range(BT):
                    n = BT * j + (k + 1)
                    act.wait_ge(gate_made, n)
                    act.activation(g[:, :], pgate[:, :], ACT.Silu, scale=fgu[:, k % 2, 0:1]).then_inc(g_ready, 1)
                    if k + 1 < BT:
                        copy_x(j, k + 1)
                    act.wait_ge(hs_ready, n)
                    act.activation(hr[:, :], h[:, :], ACT.Copy, scale=hs[:, 0:1], bias=ROUND).then_inc(hr_ready, 1)
                    act.wait_ge(hT_made, n)
                    act.activation(hT[:, :, :], ph[:, :, :], ACT.Copy).then_inc(hT_copied, 1)

        @block.gpsimd
        def _(pool):
            link = Chain(pool, pool_chain, BT)
            pool.memset(eps[:, :], LN_EPS)
            link(pool.memset(minus_half[:, :], -0.5))
            link.begin(0)
            with pool.Fori(0, NT // BT) as j:
                link.turn = j
                for k in range(BT):
                    pool.wait_ge(var_ready, BT * j + (k + 1))
                    link(pool.tensor_tensor(veps[:, :], mv[:, k % 2, 1:2], eps[:, :], ALU.add))
                    pool.tensor_tensor(rstd[:, k % 2:k % 2 + 1], veps[:, :], minus_half[:, :], ALU.pow).then_inc(rstd_ready, 1)
            link.end(NT // BT)

        @block.vector
        def _(dve):
            def quantize_x(j, k):
                xt, p = x[:, k // 2, k % 2, :], k % 2
                if p == 0:
                    dve.wait_ge(x_loaded[k // 2], 16 * j + 16)
                link(dve.tensor_reduce(xmax[:, p:p + 1], xt, AX.X, ALU.max, apply_absolute_value=True))
                link(dve.tensor_scalar(xmax[:, p:p + 1], xmax[:, p:p + 1], FLOOR, None, ALU.max))
                dve.tensor_scalar(fgu[:, p, :], wm127[:, 0:2], xmax[:, p:p + 1], None, ALU.mult)
                link(dve.reciprocal(xs[:, :], xmax[:, p:p + 1]))
                link(dve.tensor_scalar(xs[:, :], xs[:, :], 127.0, None, ALU.mult))
                link(dve.tensor_scalar(xr[:, :], xt, xs[:, 0:1], ROUND, ALU.mult, ALU.add))
                dve.tensor_scalar(xq[:, :], xr[:, :], ROUND, 127.0, ALU.subtract, ALU.min).then_inc(xq_ready, 1)

            def hidden(j, k):
                n, p = BT * j + (k + 1), k % 2
                dve.wait_ge(g_ready, n)
                dve.wait_ge(up_made, n)
                link(dve.scalar_tensor_tensor(out=h[:, :], in0=pup[:, :], scalar=fgu[:, p, 1:2], in1=g[:, :],
                                              op0=ALU.mult, op1=ALU.mult))
                dve.sem_inc(h_ready, 1)
                link(dve.tensor_reduce(hmax[:, p:p + 1], h[:, :], AX.X, ALU.max, apply_absolute_value=True))
                link(dve.tensor_scalar(hmax[:, p:p + 1], hmax[:, p:p + 1], FLOOR, None, ALU.max))
                dve.tensor_tensor(fd[:, p:p + 1], wm127[:, 2:3], hmax[:, p:p + 1], ALU.mult)
                link(dve.reciprocal(hs[:, :], hmax[:, p:p + 1]))
                dve.tensor_scalar(hs[:, :], hs[:, :], 127.0, None, ALU.mult).then_inc(hs_ready, 1)

            def quantize_h(j, k):
                dve.wait_ge(hr_ready, BT * j + (k + 1))
                dve.tensor_scalar(hq[:, :], hr[:, :], ROUND, 127.0, ALU.subtract, ALU.min).then_inc(hq_ready, 1)

            def residual(j, k):
                p = k % 2
                dve.wait_ge(down_made, BT * j + (k + 1))
                link(dve.scalar_tensor_tensor(out=r[:, p, :], in0=pd[:, 0:D], scalar=fd[:, p:p + 1],
                                              in1=x[:, k // 2, k % 2, :], op0=ALU.mult, op1=ALU.add))
                link(dve.bn_stats(stats[:, p, :], r[:, p, :]))
                dve.memset(spacer[:, :], 0.0)
                dve.bn_aggr(mv[:, p, :], stats[:, p, :]).then_inc(var_ready, 1)

            def finish(j, k):
                p, b = k % 2, k // 2
                dve.wait_ge(rstd_ready, BT * j + (k + 1))
                if p == 0:
                    dve.wait_ge(y_stored[b % 2], 32 * j + 16 * (b // 2 + 1))
                dve.tensor_scalar(y[:, b % 2, p, :], r[:, p, :], mv[:, p, 0:1], rstd[:, p:p + 1],
                                  ALU.subtract, ALU.mult).then_inc(y_ready, 1)

            link = Chain(dve, chain, BT * (5 + 4 + 2))
            dve.memset(ones[:, :], 1.0)
            dve.wait_ge(w_loaded, 64)
            dve.tensor_copy(identb[:, :], ident[:, :])
            weights = ((wgu_f[:, 0].rearrange("p c i -> p (c i)"), wgu[:, 0].rearrange("p c i -> p (c i)")),
                       (wgu_f[:, 1].rearrange("p c i -> p (c i)"), wgu[:, 1].rearrange("p c i -> p (c i)")),
                       (wd_f[:, :, :].rearrange("p c i -> p (c i)"), wd[:, :, :].rearrange("p c i -> p (c i)")))
            for m, (w, _) in enumerate(weights):
                last = dve.tensor_reduce(wsum[:, m:m + 1], w, AX.X, ALU.add, apply_absolute_value=True)
            last.then_inc(wsum_ready, 1)
            dve.wait_ge(wtotal_made, 1)
            link(dve.tensor_scalar(wmean[:, :], pd[:, 0:3], 1.0 / (I * D), FLOOR, ALU.mult, ALU.max))
            dve.tensor_scalar(wm127[:, :], wmean[:, :], 1.0 / 127.0, None, ALU.mult)
            link(dve.reciprocal(wscale[:, :], wmean[:, :]))
            for m, (w, _) in enumerate(weights):
                last = dve.tensor_scalar(w, w, wscale[:, m:m + 1], ROUND, ALU.mult, ALU.add)
            link(last)
            for m, (w, _) in enumerate(weights):
                last = dve.tensor_scalar(w, w, ROUND, 1.0, ALU.subtract, ALU.min)
            link(last)
            for w, q in weights:
                last = dve.tensor_scalar(q, w, -1.0, None, ALU.max)
            link(last)
            dve.sem_inc(setup_done, 2)
            dve.sem_inc(h_ready, 1)
            link.begin(0)
            with dve.Fori(0, NT // BT) as j:
                link.turn = j
                quantize_x(j, 0)
                for k in range(BT):
                    hidden(j, k)
                    if k > 0:
                        residual(j, k - 1)
                    if k + 1 < BT:
                        quantize_x(j, k + 1)
                    quantize_h(j, k)
                    if k > 0:
                        finish(j, k - 1)
                residual(j, BT - 1)
                finish(j, BT - 1)
            link.end(NT // BT)


STAGES = 6


def decoder(nc, a, out):
    scratch = [nc.dram_tensor(f"act{n}", [B, S, D], fp32, kind="Internal").ap() for n in range(6)]
    acts = [a["x"], *scratch][:STAGES] + [out]
    linear_attention(nc, acts[0], acts[1], a["L0_attn_WqT"], a["L0_attn_bq"], a["L0_attn_WkvT"], a["L0_attn_bkv"],
                     a["L0_attn_WoT"], a["L0_attn_bo"], a["ident"], a["head_blocks"])
    if STAGES > 1:
        cross_attention(nc, "xa0", acts[1], acts[2], a["ctx"], a["L0_xattn_wq"], a["L0_xattn_wkv"], a["L0_xattn_wproj"],
                        a["L0_xattn_bproj"], a["ident"], a["head_columns"], mask_d=a["mask"],
                        norms_d=[a["L0_xattn_" + n] for n in ("g_x", "b_x", "g_kv", "b_kv")])
    if STAGES > 2:
        expert_attention(nc, acts[2], acts[3], a["L0_ffn_Wg"], a["L0_ffn_Wq"], a["L0_ffn_Wkv"], a["L0_ffn_Wo"], a["L0_ffn_bqkv"],
                         a["L0_ffn_bo"], a["L0_ffn_ln"], a["ident"], a["batch_iota"], a["position_mask"], a["sum4"], a["pick4"])
    if STAGES > 3:
        ct_dram = nc.dram_tensor("ma_ct_dram", [2, 17, 2 * S], fp32, kind="Internal").ap()
        mamba(nc, acts[3], acts[4], ct_dram, a["L1_attn_g"], a["L1_attn_WinT"], a["L1_attn_WoutT"], a["L1_attn_conv"],
              a["L1_attn_WxT"], a["L1_attn_dtp"], a["L1_attn_Alog"], a["ident"])
    if STAGES > 4:
        cross_attention(nc, "xa1", acts[4], acts[5], a["ctx"], a["L1_xattn_WqT"], a["L1_xattn_WkvT"], a["L1_xattn_WoT"],
                        a["L1_xattn_bo"], a["ident"], a["head_columns"],
                        bq_d=a["L1_xattn_bq"], bk_d=a["L1_xattn_bk"], bv_d=a["L1_xattn_bv"])
    if STAGES > 5:
        bit_ffn(nc, acts[5], acts[6], a["L1_ffn_wguT"], a["L1_ffn_wdT"], a["ident"])


def kernel(**inputs):
    import numpy as _np
    import concourse.bacc as _bacc
    from concourse import mybir as _mybir
    from concourse.bass_utils import run_bass_kernel_spmd as _run

    def columns(v):
        return v.reshape(-1, P).T

    src = {name: _np.asarray(a) for name, a in inputs.items()}
    lay = {"x": src["x"]}
    lay["L0_attn_WqT"] = src["L0_attn_Wq"].T
    lay["L0_attn_bq"] = columns(src["L0_attn_bq"])
    lay["L0_attn_WkvT"] = _np.concatenate([src["L0_attn_Wk"].T, src["L0_attn_Wv"].T], axis=1)
    lay["L0_attn_bkv"] = _np.concatenate([src["L0_attn_bk"], src["L0_attn_bv"]])
    lay["L0_attn_WoT"] = src["L0_attn_Wo"].T
    lay["L0_attn_bo"] = src["L0_attn_bo"]
    lay["ctx"] = src["ctx_1024"]
    lay["mask"] = src["mask_BxS2_ik0"]
    lay["L0_xattn_wq"], lay["L0_xattn_wkv"], lay["L0_xattn_wproj"] = src["L0_xattn_w_q"], src["L0_xattn_w_kv"], src["L0_xattn_w_proj"]
    lay["L0_xattn_bproj"] = src["L0_xattn_b_proj"]
    for n in ("g_x", "b_x", "g_kv", "b_kv"):
        lay["L0_xattn_" + n] = columns(src["L0_xattn_" + n])
    lay["L1_xattn_WqT"] = src["L1_xattn_Wq"].T
    lay["L1_xattn_WkvT"] = _np.concatenate([src["L1_xattn_Wk"].T, src["L1_xattn_Wv"].T], axis=1)
    lay["L1_xattn_WoT"] = src["L1_xattn_Wo"].T
    lay["L1_xattn_bq"], lay["L1_xattn_bk"] = columns(src["L1_xattn_bq"]), columns(src["L1_xattn_bk"])
    lay["L1_xattn_bv"], lay["L1_xattn_bo"] = src["L1_xattn_bv"], src["L1_xattn_bo"]
    for n in ("Wg", "Wq", "Wkv", "Wo"):
        lay["L0_ffn_" + n] = src["L0_ffn_" + n]
    bqkv = _np.zeros((H, P, 2), _np.float32)
    bqkv[:, :, 0] = src["L0_ffn_bkv"]
    bqkv[:, 0:64, 1] = src["L0_ffn_bq"]
    lay["L0_ffn_bqkv"] = bqkv
    lay["L0_ffn_bo"] = columns(src["L0_ffn_bo"])
    lay["L0_ffn_ln"] = _np.stack([src["L0_ffn_ln_g"], src["L0_ffn_ln_b"]])
    lay["L1_attn_g"] = columns(src["L1_attn_g"])
    lay["L1_attn_WinT"], lay["L1_attn_WoutT"], lay["L1_attn_WxT"] = src["L1_attn_W_in"].T, src["L1_attn_W_out"].T, src["L1_attn_W_x"].T
    lay["L1_attn_conv"] = _np.concatenate([src["L1_attn_conv_w"], src["L1_attn_conv_b"][:, None]], 1).reshape(-1, P, 5).transpose(1, 0, 2)
    lay["L1_attn_dtp"] = _np.stack([columns(v) for v in (src["L1_attn_W_dt"][:, 0], src["L1_attn_b_dt"], src["L1_attn_D"])], axis=1)
    lay["L1_attn_Alog"] = src["L1_attn_A_log"].reshape(-1, P, src["L1_attn_A_log"].shape[1]).transpose(1, 0, 2)
    lay["L1_ffn_wguT"] = _np.stack([src["L1_ffn_w_gate"].T, src["L1_ffn_w_up"].T])
    lay["L1_ffn_wdT"] = src["L1_ffn_w_down"].T
    lay["ident"] = _np.eye(P, dtype=_np.float32)
    lay["batch_iota"] = _np.tile(_np.arange(B, dtype=_np.float32), (P, 1))
    lay["position_mask"] = _np.kron(_np.eye(P // B), _np.ones((B, 1))).astype(_np.float32)
    lay["sum4"] = _np.tile(_np.eye(4, P, dtype=_np.float32), (64, 1, 1))
    lay["pick4"] = _np.repeat(_np.eye(4, dtype=_np.float32)[:, :, None], P, axis=2)
    lay["head_columns"] = _np.kron(_np.eye(P // DH), _np.ones((DH, 1))).astype(_np.float32)
    lay["head_blocks"] = _np.kron(_np.eye(P // DH), _np.ones((DH, DH))).astype(_np.float32)

    nc = _bacc.Bacc("TRN2", target_bir_lowering=False, num_devices=1)
    arrays, args = {}, {}
    for name, a in lay.items():
        arrays[f"in_{name}"] = a = _np.ascontiguousarray(a)
        args[name] = nc.dram_tensor(f"in_{name}", a.shape, _mybir.dt.from_np(a.dtype), kind="ExternalInput").ap()
    out = nc.dram_tensor("out_0_dram", (B, S, D), _mybir.dt.float32, kind="ExternalOutput").ap()
    decoder(nc, args, out)
    r = _run(nc, [arrays], core_ids=[0])
    return r.results[0]["out_0_dram"]
```

```python
import concourse.bass as bass
from concourse import mybir
from contextlib import ExitStack

fp32 = mybir.dt.float32
bf16 = mybir.dt.bfloat16
i32 = mybir.dt.int32
ALU = mybir.AluOpType
ACT = mybir.ActivationFunctionType
AX = mybir.AxisListType

P = 128
B = 32
S = 256
D = 256
T = S // P
C = D // P
H = 16
DH = D // H
CTX = 77
PAIRS = B // 2
LN_EPS = 1e-5


class Stage:

    def __init__(self, nc, name):
        self.nc, self.name, self.ctx = nc, name, ExitStack()

    def __enter__(self):
        self.ctx.__enter__()
        self.ctx.enter_context(self.nc.cleanup_on_exit())
        return self

    def __exit__(self, *e):
        return self.ctx.__exit__(*e)

    def sb(self, name, shape, dt=fp32):
        return self.ctx.enter_context(self.nc.sbuf_tensor(f"{self.name}_{name}", shape, dt))

    def ps(self, name, shape, dt=fp32):
        return self.ctx.enter_context(self.nc.psum_tensor(f"{self.name}_{name}", shape, dt))

    def sem(self, name):
        return self.nc.alloc_semaphore(name=f"{self.name}_{name}")

    def block(self):
        return self.ctx.enter_context(self.nc.Block())


class Chain:

    def __init__(self, eng, sem, per_turn):
        self.eng, self.sem, self.per_turn, self.done, self.turn = eng, sem, per_turn, 0, None

    def begin(self, turn):
        assert self.turn is None
        self.base, self.turn, self.n = self.done, turn, 0

    def end(self, turns):
        assert self.n == self.per_turn, (self.n, self.per_turn)
        self.done, self.turn = self.base + turns * self.per_turn, None

    def __call__(self, ins):
        ins.then_inc(self.sem, 1)
        if self.turn is None:
            self.done += 1
            self.eng.wait_ge(self.sem, self.done)
        else:
            self.n += 1
            self.eng.wait_ge(self.sem, self.turn * self.per_turn + (self.base + self.n))


def in_turns(eng, step, turns, per, around, link=None):

    def peeled(turn, k):
        places = [per * turn + k + d for d in around]
        return [divmod(n, per) if 0 <= n < per * turns else None for n in places]

    for k in range(per):
        step(*peeled(0, k))
    if link:
        link.begin(0)
    with eng.Fori(0, turns - 2) as j:
        if link:
            link.turn = j
        for k in range(per):
            step(*((j, k + d + per) if k + d < 0 else (j + 1, k + d) if k + d < per else (j + 2, k + d - per) for d in around))
    if link:
        link.end(turns - 2)
    for k in range(per):
        step(*peeled(turns - 1, k))


def batch_tiles(x, b):
    return x[b].rearrange("(t p) d -> p t d", p=P)


def split_in_three(link, row, rest, parts, ident, out):
    v = link.eng
    for k in range(3):
        link(v.tensor_copy(parts[:, k, :], row[:, :] if k == 0 else rest[:, :]))
        if k < 2:
            link(v.tensor_tensor(rest[:, :], row[:, :] if k == 0 else rest[:, :], parts[:, k, :], ALU.subtract))
    link(v.tensor_scalar(rest[:, :], parts[:, 0, :], ident[0:3, 0:1], None, ALU.mult))
    for k in (1, 2):
        link(v.scalar_tensor_tensor(out=rest[:, :] if k == 1 else out[:, :], in0=parts[:, k, :],
                                    scalar=ident[0:3, k:k + 1], in1=rest[:, :], op0=ALU.mult, op1=ALU.add))


def linear_attention(nc, x_in, x_out, wqT, bq, wkvT, bkv, woT, bo, ident_d, blocks_d):
    with Stage(nc, "la") as st:
        sb, ps, sem = st.sb, st.ps, st.sem
        ident = sb("ident", [P, P])
        blocks = sb("blocks", [P, P])
        wq = sb("wq", [P, C, D])
        wkv = sb("wkv", [P, C, 2 * D])
        wo = sb("wo", [P, C, D])
        bq_c = sb("bq_c", [P, C])
        bias3 = sb("bias3", [3, 3 * D])
        rest3 = sb("rest3", [3, 3 * D])
        parts3 = sb("parts3", [3, 3, 3 * D], bf16)
        biasr = sb("biasr", [3, 3 * D], bf16)
        ones3 = sb("ones3", [3, P], bf16)
        minus_half = sb("minus_half", [P, T])
        eps = sb("eps", [P, T])
        spacer = sb("spacer", [P, 1])
        x = sb("x", [P, 4, T, D])
        xT = sb("xT", [P, 2, C, S])
        eq = sb("eq", [P, 2, C, S])
        rq = sb("rq", [P, 2, C, S])
        qT = sb("qT", [P, 2, C, S])
        ek = sb("ek", [P, 2, T, D])
        rk = sb("rk", [P, 2, T, D])
        k = sb("k", [P, 2, T, D])
        v = sb("v", [P, 2, T, D])
        kv = sb("kv", [P, 2, C, P])
        oT = sb("oT", [P, 2, C, S])
        r = sb("r", [P, 2, T, D])
        stats = sb("stats", [P, 2, T, 6])
        mv = sb("mv", [P, 2, T, 2])
        veps = sb("veps", [P, 2, T])
        rstd = sb("rstd", [P, 2, T])
        y = sb("y", [P, 2, T, D])
        pA = [ps(f"pA{p}", [P, C, S]) for p in range(2)]
        pB = [ps(f"pB{p}", [P, C, S]) for p in range(2)]
        pC = [ps(f"pC{p}", [P, T, 2 * D]) for p in range(2)]

        w_loaded, setup_done = sem("w_loaded"), sem("setup_done")
        x_loaded = [sem(f"x_loaded{b}") for b in range(4)]
        y_stored = [sem(f"y_stored{p}") for p in range(2)]
        xT_made, xT_copied = sem("xT_made"), sem("xT_copied")
        q_made, kv_made = sem("q_made"), sem("kv_made")
        exp_done, v_copied, qk_ready = sem("exp_done"), sem("v_copied"), sem("qk_ready")
        outer_made, outer_masked = sem("outer_made"), sem("outer_masked")
        oT_made, oT_copied = sem("oT_made"), sem("oT_copied")
        proj_made, pB_free = sem("proj_made"), sem("pB_free")
        var_ready, rstd_ready, y_ready = sem("var_ready"), sem("rstd_ready"), sem("y_ready")
        dve_chain, pool_chain = sem("dve_chain"), sem("pool_chain")
        block = st.block()

        @block.sync
        def _(sp):
            for dst, src in ((ident[:, :], ident_d), (blocks[:, :], blocks_d),
                             (wq[:, :, :], wqT.rearrange("(c p) f -> p c f", p=P)),
                             (wkv[:, :, :], wkvT.rearrange("(c p) f -> p c f", p=P)),
                             (wo[:, :, :], woT.rearrange("(c p) f -> p c f", p=P)),
                             (bq_c[:, :], bq),
                             (bias3[:, 0:2 * D], bkv.partition_broadcast(3)),
                             (bias3[:, 2 * D:3 * D], bo.partition_broadcast(3))):
                sp.dma_start(dst, src).then_inc(w_loaded, 16)
            for b in range(4):
                sp.dma_start(x[:, b], batch_tiles(x_in, b)).then_inc(x_loaded[b], 16)
            for p in range(2):
                sp.sem_inc(y_stored[p], 16)

            def store(j, q, p):
                sp.wait_ge(y_ready, 4 * j + (2 * q + p + 1))
                sp.dma_start(batch_tiles(x_out, 4 * j + (2 * q + p)), y[:, p]).then_inc(y_stored[p], 16)

            with sp.Fori(0, B // 4 - 1) as j:
                for q in range(2):
                    for p in range(2):
                        store(j, q, p)
                        sp.dma_start(x[:, 2 * q + p], batch_tiles(x_in, 4 * j + (2 * q + p + 4))).then_inc(x_loaded[2 * q + p], 16)
            for q in range(2):
                for p in range(2):
                    store(B // 4 - 1, q, p)
            for p in range(2):
                sp.wait_ge(y_stored[p], 16 * (B // 2 + 1))

        @block.tensor
        def _(pe):
            def pair(j, q):
                for p in range(2):
                    pe.wait_ge(x_loaded[2 * q + p], 16 * j + 16)
                    for c in range(C):
                        for t in range(T):
                            last = pe.transpose(pA[p][:, c, t * P:(t + 1) * P],
                                                x[:, 2 * q + p, t, c * P:(c + 1) * P], ident[:, :])
                    last.then_inc(xT_made, 1)
                for p in range(2):
                    n = 4 * j + (2 * q + p + 1)
                    pe.wait_ge(xT_copied, n)
                    pe.wait_ge(pB_free, n)
                    for f in range(C):
                        for c in range(C):
                            last = pe.matmul(pB[p][:, f, :], wq[:, c, f * P:(f + 1) * P], xT[:, p, c, :],
                                             start=(c == 0), stop=(c == C - 1))
                    last.then_inc(q_made, 1)
                    for t in range(T):
                        pe.matmul(pC[p][:, t, :], ones3[:, :], biasr[:, 0:2 * D], start=True, stop=False)
                        for c in range(C):
                            last = pe.matmul(pC[p][:, t, :], xT[:, p, c, t * P:(t + 1) * P], wkv[:, c, :],
                                             start=False, stop=(c == C - 1))
                    last.then_inc(kv_made, 1)
                for p in range(2):
                    n = 4 * j + (2 * q + p + 1)
                    pe.wait_ge(v_copied, n)
                    pe.wait_ge(qk_ready, n)
                    for c in range(C):
                        for t in range(T):
                            last = pe.matmul(pA[p][:, c, 0:P], k[:, p, t, c * P:(c + 1) * P],
                                             v[:, p, t, c * P:(c + 1) * P], start=(t == 0), stop=(t == T - 1))
                    last.then_inc(outer_made, 1)
                for p in range(2):
                    pe.wait_ge(outer_masked, 4 * j + (2 * q + p + 1))
                    for c in range(C):
                        last = pe.matmul(pC[p][:, 0, c * S:(c + 1) * S], kv[:, p, c, :], qT[:, p, c, :],
                                         start=True, stop=True)
                    last.then_inc(oT_made, 1)
                for p in range(2):
                    pe.wait_ge(oT_copied, 4 * j + (2 * q + p + 1))
                    for t in range(T):
                        pe.matmul(pB[p][:, t, :], ones3[:, :], biasr[:, 2 * D:3 * D], start=True, stop=False)
                        for c in range(C):
                            last = pe.matmul(pB[p][:, t, :], oT[:, p, c, t * P:(t + 1) * P], wo[:, c, :],
                                             start=False, stop=(c == C - 1))
                    last.then_inc(proj_made, 1)

            pe.wait_ge(w_loaded, 16 * 8)
            pe.wait_ge(setup_done, 1)
            with pe.Fori(0, B // 4) as j:
                for q in range(2):
                    pair(j, q)

        @block.scalar
        def _(act):
            def pair(j, q):
                for p in range(2):
                    act.wait_ge(xT_made, 4 * j + (2 * q + p + 1))
                    act.activation(xT[:, p], pA[p][:, :, :], ACT.Copy).then_inc(xT_copied, 1)
                for p in range(2):
                    n = 4 * j + (2 * q + p + 1)
                    act.wait_ge(q_made, n)
                    for f in range(C):
                        last = act.activation(eq[:, p, f, :], pB[p][:, f, :], ACT.Exp, bias=bq_c[:, f:f + 1])
                    last.then_inc(exp_done, 1)
                    act.wait_ge(kv_made, n)
                    act.activation(ek[:, p], pC[p][:, :, 0:D], ACT.Exp)
                    act.activation(v[:, p], pC[p][:, :, D:2 * D], ACT.Copy).then_inc(v_copied, 1)
                for p in range(2):
                    act.wait_ge(oT_made, 4 * j + (2 * q + p + 1))
                    act.activation(oT[:, p], pC[p][:, 0, :].rearrange("p (c s) -> p c s", c=C),
                                   ACT.Copy).then_inc(oT_copied, 1)

            act.wait_ge(w_loaded, 16 * 8)
            with act.Fori(0, B // 4) as j:
                for q in range(2):
                    pair(j, q)

        @block.gpsimd
        def _(pool):
            link = Chain(pool, pool_chain, 4)
            pool.memset(eps[:, :], LN_EPS)
            link(pool.memset(minus_half[:, :], -0.5))
            link.begin(0)
            with pool.Fori(0, B // 4) as j:
                link.turn = j
                for b in range(4):
                    pool.wait_ge(var_ready, 4 * j + (b + 1))
                    link(pool.tensor_tensor(veps[:, b % 2], mv[:, b % 2, :, 1], eps[:, :], ALU.add))
                    pool.tensor_tensor(rstd[:, b % 2], veps[:, b % 2], minus_half[:, :], ALU.pow).then_inc(rstd_ready, 1)
            link.end(B // 4)

        @block.vector
        def _(dve):
            def pair(j, q):
                for p in range(2):
                    n = 4 * j + (2 * q + p + 1)
                    dve.wait_ge(exp_done, n)
                    for f in range(C):
                        dve.tensor_scalar(rq[:, p, f, :], pB[p][:, f, :], bq_c[:, f:f + 1], 0.0, ALU.add, ALU.max)
                    dve.wait_ge(v_copied, n)
                    link(dve.tensor_scalar(rk[:, p], pC[p][:, :, 0:D], 0.0, None, ALU.max))
                    dve.scalar_tensor_tensor(out=qT[:, p], in0=eq[:, p], scalar=1.0, in1=rq[:, p],
                                             op0=ALU.min, op1=ALU.add)
                    dve.scalar_tensor_tensor(out=k[:, p], in0=ek[:, p], scalar=1.0, in1=rk[:, p],
                                             op0=ALU.min, op1=ALU.add).then_inc(qk_ready, 1)
                for p in range(2):
                    dve.wait_ge(outer_made, 4 * j + (2 * q + p + 1))
                    dve.tensor_tensor(kv[:, p], pA[p][:, :, 0:P], blocks[:, :].unsqueeze(1).broadcast_to([P, C, P]),
                                      ALU.mult).then_inc(outer_masked, 1)
                for p in range(2):
                    dve.wait_ge(proj_made, 4 * j + (2 * q + p + 1))
                    link(dve.tensor_tensor(r[:, p], pB[p][:, :, :], x[:, 2 * q + p], ALU.add))
                    dve.sem_inc(pB_free, 1)
                    for t in range(T):
                        last = dve.bn_stats(stats[:, p, t, :], r[:, p, t, :])
                    link(last)
                    dve.memset(spacer[:, :], 0.0)
                    for t in range(T):
                        last = dve.bn_aggr(mv[:, p, t, :], stats[:, p, t, :])
                    last.then_inc(var_ready, 1)
                for p in range(2):
                    dve.wait_ge(rstd_ready, 4 * j + (2 * q + p + 1))
                    dve.wait_ge(y_stored[p], 32 * j + 16 * (q + 1))
                    for t in range(T):
                        last = dve.tensor_scalar(y[:, p, t, :], r[:, p, t, :], mv[:, p, t, 0:1], rstd[:, p, t:t + 1],
                                                 ALU.subtract, ALU.mult)
                    last.then_inc(y_ready, 1)

            link = Chain(dve, dve_chain, 3 * 4)
            dve.wait_ge(w_loaded, 16 * 8)
            dve.memset(ones3[:, :], 1.0)
            split_in_three(link, bias3, rest3, parts3, ident, biasr)
            dve.sem_inc(setup_done, 1)
            dve.sem_inc(pB_free, 2)
            link.begin(0)
            with dve.Fori(0, B // 4) as j:
                link.turn = j
                for q in range(2):
                    pair(j, q)
            link.end(B // 4)


def cross_attention(nc, name, x_in, x_out, ctx_d, wq_d, wkv_d, wo_d, bo_d, ident_d, heads_d,
                    bq_d=None, bk_d=None, bv_d=None, mask_d=None, norms_d=None):
    normed, masked = norms_d is not None, mask_d is not None
    HC = H // C
    HB = HC // 2
    W = DH + 1
    with Stage(nc, name) as st:
        sb, ps, sem = st.sb, st.ps, st.sem
        ident = sb("ident", [P, P])
        head_of = sb("head_of", [P, HC])
        wq = sb("wq", [P, C, D])
        wkv = sb("wkv", [P, C, 2 * D])
        wo = sb("wo", [P, C, D])
        bqk = sb("bqk", [P, 2, C])
        bq4 = sb("bq4", [P, C])
        norms = sb("norms", [P, 4, C])
        bias3 = sb("bias3", [3, 2 * D])
        rest3 = sb("rest3", [3, 2 * D])
        parts3 = sb("parts3", [3, 3, 2 * D], bf16)
        biasr = sb("biasr", [3, 2 * D], bf16)
        fill3 = sb("fill3", [3, 1])
        fill_rest = sb("fill_rest", [3, 1])
        fill_parts = sb("fill_parts", [3, 3, 1], bf16)
        fillr = sb("fillr", [3, 1])
        ones3 = sb("ones3", [3, P], bf16)
        spacer = sb("spacer", [P, 1])
        eps = sb("eps", [P, 3])
        minus_half = sb("minus_half", [P, 3])
        x = sb("x", [P, 4, T, D])
        cx = sb("cx", [CTX, 2, D])
        mask_i = sb("mask_i", [P, 2, CTX], i32)
        seen = sb("seen", [P, 2, CTX])
        fill_row = sb("fill_row", [3, 2, CTX], bf16)
        n_stats = sb("n_stats", [P, 2, 3, 6])
        n_mv = sb("n_mv", [P, 2, 3, 2])
        n_veps = sb("n_veps", [P, 2, 3])
        n_rstd = sb("n_rstd", [P, 2, 3])
        xn = sb("xn", [P, 2, T, D])
        cn = sb("cn", [CTX, 2, D])
        xT = sb("xT", [P, 2, C, S])
        cT = sb("cT", [P, 2, C, CTX])
        qT = sb("qT", [P, 2, C, S])
        kT = sb("kT", [P, 2, C, CTX])
        kheads = sb("kheads", [P, 2, C, HC * CTX])
        v = sb("v", [CTX, 2, H, W])
        top = sb("top", [P, 2, HC])
        low = sb("low", [P, 2, HC * CTX])
        e = sb("e", [P, 2, HC * CTX])
        eT = sb("eT", [CTX, 2, C, HC, P])
        rec = sb("rec", [P, 2, H])
        on = sb("on", [P, 2, T, D])
        oT = sb("oT", [P, 2, C, S])
        r = sb("r", [P, 2, T, D])
        stats = sb("stats", [P, 2, T, 6])
        mv = sb("mv", [P, 2, T, 2])
        veps = sb("veps", [P, 2, T])
        rstd = sb("rstd", [P, 2, T])
        y = sb("y", [P, 2, T, D])
        pS = [ps(f"pS{c}", [P, 2, 512]) for c in range(C)]
        pE = [ps(f"pE{h}", [CTX, HB, P]) for h in range(2)]
        pG = [ps(f"pG{g}", [P, 512]) for g in range(2)]

        w_loaded, setup_done = sem("w_loaded"), sem("setup_done")
        x_loaded = [sem(f"x_loaded{b}") for b in range(4)]
        c_loaded = [sem(f"c_loaded{p}") for p in range(2)]
        y_stored = [sem(f"y_stored{p}") for p in range(2)]
        n_var, n_rstd_ready, n_ready = sem("n_var"), sem("n_rstd_ready"), sem("n_ready")
        xT_made, xT_copied, cT_made, cT_copied = sem("xT_made"), sem("xT_copied"), sem("cT_made"), sem("cT_copied")
        q_made, q_copied, k_made, k_copied = sem("q_made"), sem("q_copied"), sem("k_made"), sem("k_copied")
        v_made, v_copied, kheads_ready = sem("v_made"), sem("v_copied"), sem("kheads_ready")
        scores_made, low_ready = sem("scores_made"), sem("low_ready")
        e_ready, eT_made, eT_copied = sem("e_ready"), sem("eT_made"), sem("eT_copied")
        o_made, o_normed = sem("o_made"), sem("o_normed")
        oT_made, oT_copied, proj_made, res_added = sem("oT_made"), sem("oT_copied"), sem("proj_made"), sem("res_added")
        var_ready, rstd_ready, y_ready = sem("var_ready"), sem("rstd_ready"), sem("y_ready")
        dve_chain, pool_chain = sem("dve_chain"), sem("pool_chain")
        bq4_ready = sem("bq4_ready")
        block = st.block()
        ctx_used = n_ready if normed else cT_made
        U = T * C

        loads = [(ident[:, :], ident_d), (head_of[:, :], heads_d),
                 (wq[:, :, :], wq_d.rearrange("(c p) f -> p c f", p=P)),
                 (wkv[:, :, :], wkv_d.rearrange("(c p) f -> p c f", p=P)),
                 (wo[:, :, :], wo_d.rearrange("(c p) f -> p c f", p=P)),
                 (bias3[:, D:2 * D], bo_d.partition_broadcast(3))]
        if bq_d is not None:
            loads += [(bqk[:, 0, :], bq_d), (bqk[:, 1, :], bk_d), (bias3[:, 0:D], bv_d.partition_broadcast(3))]
        if normed:
            loads += [(norms[:, n, :], d) for n, d in enumerate(norms_d)]

        def batches(eng, batch, link=None):
            fours = B // 4
            for b in range(4):
                batch((0, b), (0, b + 1) if b < 3 else (1, 0), (0, b - 1) if b else None)
            if link:
                link.begin(0)
            with eng.Fori(0, fours - 2) as j:
                if link:
                    link.turn = j
                for b in range(4):
                    batch((j + 1, b), (j + 1, b + 1) if b < 3 else (j + 2, 0), (j + 1, b - 1) if b else (j, 3))
            if link:
                link.end(fours - 2)
            for b in range(4):
                batch((fours - 1, b), (fours - 1, b + 1) if b < 3 else None, (fours - 1, b - 1) if b else (fours - 2, 3))

        last_batch = (B // 4 - 1, 3)

        @block.sync
        def _(sp):
            for dst, src in loads:
                sp.dma_start(dst, src).then_inc(w_loaded, 16)

            def load_x(b, at):
                sp.dma_start(x[:, b], batch_tiles(x_in, at)).then_inc(x_loaded[b], 16)

            def load_ctx(p, at):
                sp.dma_start(cx[:, p], ctx_d[at]).then_inc(c_loaded[p], 16)
                if masked:
                    sp.dma_start(mask_i[:, p], mask_d[at].partition_broadcast(P)).then_inc(c_loaded[p], 16)

            for b in range(4):
                load_x(b, b)
            for p in range(2):
                load_ctx(p, p)
                sp.sem_inc(y_stored[p], 16)

            def store(j, b):
                p = b % 2
                sp.wait_ge(y_ready, 4 * j + (b + 1))
                sp.dma_start(batch_tiles(x_out, 4 * j + b), y[:, p]).then_inc(y_stored[p], 16)

            with sp.Fori(0, B // 4 - 1) as j:
                for b in range(4):
                    sp.wait_ge(ctx_used, 4 * j + (b + 1))
                    load_ctx(b % 2, 4 * j + (b + 2))
                    store(j, b)
                    load_x(b, 4 * j + (b + 4))
            for b in range(4):
                if b < 2:
                    sp.wait_ge(ctx_used, B - 3 + b)
                    load_ctx(b % 2, B - 2 + b)
                store(B // 4 - 1, b)
            for p in range(2):
                sp.wait_ge(y_stored[p], 16 * (B // 2 + 1))

        @block.tensor
        def _(pe):
            def front(j, b):
                p, n = b % 2, 4 * j + (b + 1)
                if normed:
                    pe.wait_ge(n_ready, n)
                else:
                    pe.wait_ge(x_loaded[b], 16 * j + 16)
                for c in range(C):
                    for t in range(T):
                        src = xn[:, p, t, c * P:(c + 1) * P] if normed else x[:, b, t, c * P:(c + 1) * P]
                        last = pe.transpose(pG[0][:, (c * T + t) * P:(c * T + t + 1) * P], src, ident[:, :])
                last.then_inc(xT_made, 1)
                if not normed:
                    pe.wait_ge(c_loaded[p], 32 * j + 16 * (b // 2 + 1))
                for c in range(C):
                    src = cn[:, p, c * P:(c + 1) * P] if normed else cx[:, p, c * P:(c + 1) * P]
                    last = pe.transpose(pG[1][:, c * CTX:(c + 1) * CTX], src, ident[0:CTX, 0:CTX])
                last.then_inc(cT_made, 1)

            def project(j, b):
                p, n = b % 2, 4 * j + (b + 1)
                pe.wait_ge(xT_copied, n)
                for f in range(C):
                    for c in range(C):
                        last = pe.matmul(pG[0][:, f * S:(f + 1) * S], wq[:, c, f * P:(f + 1) * P], xT[:, p, c, :],
                                         start=(c == 0), stop=(c == C - 1))
                last.then_inc(q_made, 1)
                pe.wait_ge(cT_copied, n)
                for f in range(C):
                    for c in range(C):
                        last = pe.matmul(pG[1][:, f * CTX:(f + 1) * CTX], wkv[:, c, f * P:(f + 1) * P], cT[:, p, c, :],
                                         start=(c == 0), stop=(c == C - 1))
                last.then_inc(k_made, 1)
                pe.wait_ge(q_copied, n)
                if bv_d is not None:
                    pe.matmul(pG[0][0:CTX, 0:D], ones3[:, 0:CTX], biasr[:, 0:D], start=True, stop=False)
                for c in range(C):
                    last = pe.matmul(pG[0][0:CTX, 0:D], cT[:, p, c, :], wkv[:, c, D:2 * D],
                                     start=(c == 0 and bv_d is None), stop=(c == C - 1))
                last.then_inc(v_made, 1)

            def scores(j, b, u):
                p, c, t = b % 2, u % C, u // C
                pe.wait_ge(low_ready, (4 * U) * j + (U * b + u + 1))
                for h in range(2):
                    cols = slice(h * HB * CTX, (h + 1) * HB * CTX)
                    if masked:
                        pe.matmul(pS[c][:, h, 0:HB * CTX], ones3[:, :],
                                  fill_row[:, p, :].unsqueeze(1).broadcast_to([3, HB, CTX]), start=True, stop=False)
                    last = pe.matmul(pS[c][:, h, 0:HB * CTX], qT[:, p, c, t * P:(t + 1) * P], kheads[:, p, c, cols],
                                     start=not masked, stop=True)
                last.then_inc(scores_made, 1)

            def turn(j, b, u):
                pe.wait_ge(e_ready, (4 * U) * j + (U * b + u + 1))
                for h in range(2):
                    pe.wait_ge(eT_copied, (8 * U) * j + (2 * (U * b + u) + h + 1))
                    for i in range(HB):
                        at = (h * HB + i) * CTX
                        last = pe.transpose(pE[h][:, i, :], e[:, u % 2, at:at + CTX], ident[:, :])
                    last.then_inc(eT_made, 1)

            def values(j, b, t, c):
                p = b % 2
                pe.wait_ge(eT_copied, (8 * U) * j + (2 * U * b + 4 * t + 2 * (c + 1) + 2))
                for h in range(c * HC, (c + 1) * HC):
                    last = pe.matmul(pG[t][:, h * W:(h + 1) * W], eT[:, t, h // HC, h % HC, :], v[:, p, h, :],
                                     start=True, stop=True)
                if c == C - 1:
                    last.then_inc(o_made, 1)

            def turn_out(j, b):
                pe.wait_ge(o_normed, 8 * j + 2 * (b + 1))
                for c in range(C):
                    for t in range(T):
                        last = pe.transpose(pG[0][:, (c * T + t) * P:(c * T + t + 1) * P],
                                            on[:, b % 2, t, c * P:(c + 1) * P], ident[:, :])
                last.then_inc(oT_made, 1)

            def project_out(j, b):
                p = b % 2
                pe.wait_ge(oT_copied, 4 * j + (b + 1))
                for t in range(T):
                    pe.matmul(pG[1][:, t * D:(t + 1) * D], ones3[:, :], biasr[:, D:2 * D], start=True, stop=False)
                    for c in range(C):
                        last = pe.matmul(pG[1][:, t * D:(t + 1) * D], oT[:, p, c, t * P:(t + 1) * P], wo[:, c, :],
                                         start=False, stop=(c == C - 1))
                last.then_inc(proj_made, 1)

            def batch(this, nxt, before):
                j, b = this
                n = 4 * j + (b + 1)
                pe.wait_ge(kheads_ready, n)
                scores(j, b, 0)
                scores(j, b, 1)
                if before is not None:
                    turn_out(*before)
                turn(j, b, 0)
                if before is not None:
                    project_out(*before)
                scores(j, b, 2)
                if nxt is not None:
                    pe.wait_ge(v_copied, n)
                    pe.wait_ge(res_added, n)
                    front(*nxt)
                turn(j, b, 1)
                if nxt is not None:
                    project(*nxt)
                scores(j, b, 3)
                turn(j, b, 2)
                if nxt is not None:
                    pe.wait_ge(v_copied, n + 1)
                    pe.wait_ge(k_copied, n + 1)
                else:
                    pe.wait_ge(v_copied, n)
                    pe.wait_ge(res_added, n)
                values(j, b, 0, 0)
                turn(j, b, 3)
                values(j, b, 0, 1)
                values(j, b, 1, 0)
                values(j, b, 1, 1)

            pe.wait_ge(w_loaded, 16 * len(loads))
            pe.wait_ge(setup_done, 1)
            front(0, 0)
            project(0, 0)
            batches(pe, batch)
            turn_out(*last_batch)
            project_out(*last_batch)

        @block.scalar
        def _(act):
            def front(j, b):
                p, n = b % 2, 4 * j + (b + 1)
                act.wait_ge(xT_made, n)
                for c in range(C):
                    last = act.activation(xT[:, p, c, :], pG[0][:, c * S:(c + 1) * S], ACT.Identity,
                                          **(dict(bias=norms[:, 1, c:c + 1], scale=norms[:, 0, c:c + 1]) if normed else {}))
                last.then_inc(xT_copied, 1)
                act.wait_ge(cT_made, n)
                for c in range(C):
                    last = act.activation(cT[:, p, c, :], pG[1][:, c * CTX:(c + 1) * CTX], ACT.Identity,
                                          **(dict(bias=norms[:, 3, c:c + 1], scale=norms[:, 2, c:c + 1]) if normed else {}))
                last.then_inc(cT_copied, 1)

            def copy_q(j, b):
                p, n = b % 2, 4 * j + (b + 1)
                act.wait_ge(q_made, n)
                for f in range(C):
                    last = act.activation(qT[:, p, f, :], pG[0][:, f * S:(f + 1) * S], ACT.Identity, scale=0.25,
                                          **(dict(bias=bq4[:, f:f + 1]) if bq_d is not None else {}))
                last.then_inc(q_copied, 1)

            def copy_kv(j, b):
                p, n = b % 2, 4 * j + (b + 1)
                act.wait_ge(k_made, n)
                for f in range(C):
                    last = act.activation(kT[:, p, f, :], pG[1][:, f * CTX:(f + 1) * CTX], ACT.Identity,
                                          **(dict(bias=bqk[:, 1, f:f + 1]) if bk_d is not None else {}))
                last.then_inc(k_copied, 1)
                act.wait_ge(v_made, n)
                act.activation(v[:, p, :, 0:DH], pG[0][0:CTX, 0:D].rearrange("p (h e) -> p h e", h=H),
                               ACT.Copy).then_inc(v_copied, 1)

            def expo(j, b, u):
                act.wait_ge(low_ready, (4 * U) * j + (U * b + u + 3))
                act.activation(e[:, u % 2], low[:, u % 2], ACT.Exp).then_inc(e_ready, 1)

            def turned(j, b, u):
                for h in range(2):
                    act.wait_ge(eT_made, (8 * U) * j + (2 * (U * b + u) + h + 1))
                    act.activation(eT[:, u // C, u % C, h * HB:(h + 1) * HB, :], pE[h][:, :, :],
                                   ACT.Copy).then_inc(eT_copied, 1)

            def batch(this, nxt, before):
                j, b = this
                expo(j, b, 0)
                if before is not None:
                    back(*before)
                turned(j, b, 0)
                expo(j, b, 1)
                if nxt is not None:
                    front(*nxt)
                turned(j, b, 1)
                if nxt is not None:
                    copy_q(*nxt)
                expo(j, b, 2)
                if nxt is not None:
                    copy_kv(*nxt)
                turned(j, b, 2)
                expo(j, b, 3)
                turned(j, b, 3)

            def back(j, b):
                act.wait_ge(oT_made, 4 * j + (b + 1))
                act.activation(oT[:, b % 2], pG[0][:, :].rearrange("p (c s) -> p c s", c=C), ACT.Copy).then_inc(oT_copied, 1)

            act.wait_ge(w_loaded, 16 * len(loads))
            act.wait_ge(setup_done, 1)
            act.sem_inc(eT_copied, 2)
            if bq_d is not None:
                act.activation(bq4[:, :], bqk[:, 0, :], ACT.Copy, scale=0.25).then_inc(bq4_ready, 1)
                act.wait_ge(bq4_ready, 1)
            front(0, 0)
            copy_q(0, 0)
            copy_kv(0, 0)
            batches(act, batch)
            back(*last_batch)

        @block.gpsimd
        def _(pool):
            def norm_scale(j, b):
                p = b % 2
                pool.wait_ge(n_var, 4 * j + (b + 1))
                link(pool.tensor_tensor(n_veps[:, p], n_mv[:, p, :, 1], eps[:, :], ALU.add))
                pool.tensor_tensor(n_rstd[:, p], n_veps[:, p], minus_half[:, :], ALU.pow).then_inc(n_rstd_ready, 1)

            def spread_k(j, b):
                p, n = b % 2, 4 * j + (b + 1)
                pool.wait_ge(k_copied, n)
                if masked:
                    link(pool.tensor_tensor(kT[:, p], kT[:, p], seen[:, p].unsqueeze(1).broadcast_to([P, C, CTX]), ALU.mult))
                for c in range(C):
                    last = pool.tensor_tensor(kheads[:, p, c, :].rearrange("p (h s) -> p h s", h=HC),
                                              kT[:, p, c, :].unsqueeze(1).broadcast_to([P, HC, CTX]),
                                              head_of[:, :].unsqueeze(2).broadcast_to([P, HC, CTX]), ALU.mult)
                last.then_inc(kheads_ready, 1)

            def batch(this, nxt, before):
                if nxt is not None and normed:
                    norm_scale(*nxt)
                if before is not None:
                    rstd_of(*before)
                if nxt is not None:
                    spread_k(*nxt)

            def rstd_of(j, b):
                p = b % 2
                pool.wait_ge(var_ready, 4 * j + (b + 1))
                link(pool.tensor_tensor(veps[:, p], mv[:, p, :, 1], eps[:, 0:T], ALU.add))
                pool.tensor_tensor(rstd[:, p], veps[:, p], minus_half[:, 0:T], ALU.pow).then_inc(rstd_ready, 1)

            link = Chain(pool, pool_chain, 4 * (1 + normed + masked))
            pool.memset(eps[:, :], LN_EPS)
            link(pool.memset(minus_half[:, :], -0.5))
            pool.wait_ge(w_loaded, 16 * len(loads))
            if normed:
                norm_scale(0, 0)
            spread_k(0, 0)
            batches(pool, batch, link)
            rstd_of(*last_batch)

        @block.vector
        def _(dve):
            def norm_stats(j, b):
                p = b % 2
                dve.wait_ge(x_loaded[b], 16 * j + 16)
                for t in range(T):
                    dve.bn_stats(n_stats[:, p, t, :], x[:, b, t, :])
                dve.wait_ge(c_loaded[p], (2 * L) * j + L * (b // 2 + 1))
                link(dve.bn_stats(n_stats[0:CTX, p, T, :], cx[:, p, :]))
                dve.memset(spacer[:, :], 0.0)
                for t in range(T):
                    dve.bn_aggr(n_mv[:, p, t, :], n_stats[:, p, t, :])
                dve.bn_aggr(n_mv[0:CTX, p, T, :], n_stats[0:CTX, p, T, :]).then_inc(n_var, 1)
                if masked:
                    dve.tensor_scalar(seen[:, p, :], mask_i[:, p, :], 0.0, None, ALU.not_equal)
                    dve.tensor_scalar(fill_row[:, p, :], mask_i[0:3, p, :], 0.0, fillr[:, 0:1], ALU.is_equal, ALU.mult)

            def norm_apply(j, b):
                p = b % 2
                dve.wait_ge(n_rstd_ready, 4 * j + (b + 1))
                for t in range(T):
                    dve.tensor_scalar(xn[:, p, t, :], x[:, b, t, :], n_mv[:, p, t, 0:1], n_rstd[:, p, t:t + 1],
                                      ALU.subtract, ALU.mult)
                dve.tensor_scalar(cn[:, p, :], cx[:, p, :], n_mv[0:CTX, p, T, 0:1], n_rstd[0:CTX, p, T:T + 1],
                                  ALU.subtract, ALU.mult).then_inc(n_ready, 1)

            def unit(j, b, u):
                c = u % C
                dve.wait_ge(scores_made, (4 * U) * j + (U * b + u + 1))
                s = pS[c][:, :, 0:HB * CTX].rearrange("p g (h s) -> p g h s", h=HB)
                m = top[:, c, :].rearrange("p (g h) -> p g h", g=2)
                link(dve.tensor_reduce(m, s, AX.X, ALU.max))
                dve.tensor_tensor(low[:, u % 2].rearrange("p (g h s) -> p g h s", g=2, h=HB), s,
                                  m.unsqueeze(3).broadcast_to([P, 2, HB, CTX]), ALU.subtract).then_inc(low_ready, 1)

            def normalize(j, b, t):
                p = b % 2
                dve.wait_ge(o_made, 8 * j + (2 * b + t + 1))
                o = pG[t][:, 0:H * W].rearrange("p (h w) -> p h w", h=H)
                link(dve.reciprocal(rec[:, t, :], o[:, :, DH]))
                dve.tensor_tensor(on[:, p, t, :].rearrange("p (h e) -> p h e", h=H), o[:, :, 0:DH],
                                  rec[:, t, :].unsqueeze(2).broadcast_to([P, H, DH]), ALU.mult).then_inc(o_normed, 1)

            def batch(this, nxt, before):
                unit(*this, 0)
                if nxt is not None and normed:
                    norm_stats(*nxt)
                unit(*this, 1)
                if nxt is not None and normed:
                    norm_apply(*nxt)
                if before is not None:
                    residual(*before)
                unit(*this, 2)
                if before is not None:
                    finish(*before)
                unit(*this, 3)
                normalize(*this, 0)
                normalize(*this, 1)

            def residual(j, b):
                p = b % 2
                dve.wait_ge(proj_made, 4 * j + (b + 1))
                link(dve.tensor_tensor(r[:, p], pG[1][:, :].rearrange("p (t d) -> p t d", t=T), x[:, b], ALU.add))
                dve.sem_inc(res_added, 1)
                for t in range(T):
                    last = dve.bn_stats(stats[:, p, t, :], r[:, p, t, :])
                link(last)
                dve.memset(spacer[:, :], 0.0)
                for t in range(T):
                    last = dve.bn_aggr(mv[:, p, t, :], stats[:, p, t, :])
                last.then_inc(var_ready, 1)

            def finish(j, b):
                p = b % 2
                dve.wait_ge(rstd_ready, 4 * j + (b + 1))
                dve.wait_ge(y_stored[p], 32 * j + 16 * (b // 2 + 1))
                for t in range(T):
                    last = dve.tensor_scalar(y[:, p, t, :], r[:, p, t, :], mv[:, p, t, 0:1], rstd[:, p, t:t + 1],
                                             ALU.subtract, ALU.mult)
                last.then_inc(y_ready, 1)

            L = 16 * (1 + masked)
            link = Chain(dve, dve_chain, 4 * (U + 4 + normed))
            dve.wait_ge(w_loaded, 16 * len(loads))
            dve.memset(ones3[:, :], 1.0)
            dve.memset(n_mv[:, :, :, :], 1.0)
            dve.memset(v[:, :, :, DH:W], 1.0)
            if bv_d is None:
                link(dve.memset(bias3[:, 0:D], 0.0))
            split_in_three(link, bias3, rest3, parts3, ident, biasr)
            link(dve.memset(fill3[:, :], -1e9))
            split_in_three(link, fill3, fill_rest, fill_parts, ident, fillr)
            dve.sem_inc(setup_done, 1)
            dve.sem_inc(low_ready, 2)
            dve.sem_inc(res_added, 1)
            if normed:
                norm_stats(0, 0)
                norm_apply(0, 0)
            batches(dve, batch, link)
            residual(*last_batch)
            finish(*last_batch)


def expert_attention(nc, x_in, x_out, wg_d, wq_d, wkv_d, wo_d, bqkv_d, bo_d, ln_d, ident_d, iota_d, posmask_d,
                     sum4_d, pick4_d):
    E, F, SP, G8, NG = H, 64, 4, 8, 8
    NT = NG * G8
    SL = 2 * SP
    ES = NT * SL
    xg_in = x_in.rearrange("b (g t s) d -> g s b t d", g=NG, t=G8)
    xg_out = x_out.rearrange("b (g t s) d -> g s b t d", g=NG, t=G8)
    with Stage(nc, "ea") as outer:
        ident = outer.sb("ident", [P, P])
        xg = outer.sb("xg", [P, 2, G8, D])
        sel = outer.sb("sel", [P, NT, P])
        hg = outer.sb("hg", [P, C, E, ES])

        def load_group(sp, g, q, sem_):
            for s in range(SP):
                sp.dma_start(xg[s * B:(s + 1) * B, q], xg_in[g][s]).then_inc(sem_, 16)

        with Stage(nc, "route") as st:
            sb, ps, sem = st.sb, st.ps, st.sem
            wg = sb("wg", [P, C, E])
            iota = sb("iota", [P, B])
            iota64 = sb("iota64", [P, B])
            posmask = sb("posmask", [P, SP])
            hT = sb("hT", [P, 2, C, P])
            lg = sb("lg", [P, NT, E])
            pr = sb("pr", [P, NT, E])
            tmax = sb("tmax", [P, NT])
            tsum = sb("tsum", [P, NT])
            SG = NG * SP
            pT = sb("pT", [P, SG, B])
            eq = sb("eq", [P, SG, B])
            m = sb("m", [P, SG])
            i1 = sb("i1", [P, SG])
            i2 = sb("i2", [P, SG])
            lo_hi = sb("lo_hi", [P, 2, SG])
            hot = sb("hot", [P, 2, SG, B])
            ph = [ps(f"ph{q}", [P, C, P]) for q in range(2)]
            pl = [ps(f"pl{q}", [P, G8, E]) for q in range(2)]
            pt = [ps(f"pt{q}", [P, 4, P]) for q in range(4)]
            w_loaded = sem("w_loaded")
            x_loaded = [sem(f"x_loaded{q}") for q in range(2)]
            hT_made, hT_copied, lg_made, lg_copied = sem("hT_made"), sem("hT_copied"), sem("lg_made"), sem("lg_copied")
            low_ready, exp_done, pr_ready = sem("low_ready"), sem("exp_done"), sem("pr_ready")
            pT_made, hot_ready, hotT_made = sem("pT_made"), sem("hot_ready"), sem("hotT_made")
            chain, sel_ready = sem("chain"), sem("sel_ready")
            block = st.block()
            loads = [(ident[:, :], ident_d), (wg[:, :, :], wg_d.rearrange("(c p) e -> p c e", p=P)),
                     (iota[:, :], iota_d), (posmask[:, :], posmask_d)]

            @block.sync
            def _(sp):
                for dst, src in loads:
                    sp.dma_start(dst, src).then_inc(w_loaded, 16)
                for q in range(2):
                    load_group(sp, q, q, x_loaded[q])
                with sp.Fori(0, NG // 2 - 1) as j:
                    for q in range(2):
                        sp.wait_ge(lg_made, 2 * j + (q + 1))
                        load_group(sp, 2 * j + (q + 2), q, x_loaded[q])

            @block.tensor
            def _(pe):
                pe.wait_ge(w_loaded, 16 * len(loads))

                def turn(j, q, t):
                    if t == 0:
                        pe.wait_ge(x_loaded[q], 64 * j + 64)
                    pe.wait_ge(hT_copied, (2 * G8) * j + (G8 * q + t + 1))
                    for c in range(C):
                        last = pe.transpose(ph[t % 2][:, c, :], xg[:, q, t, c * P:(c + 1) * P], ident[:, :])
                    last.then_inc(hT_made, 1)

                def score(j, q, t):
                    if t == 0:
                        pe.wait_ge(lg_copied, 2 * j + (q + 1))
                    pe.wait_ge(hT_copied, (2 * G8) * j + (G8 * q + t + 3))
                    for c in range(C):
                        last = pe.matmul(pl[q][:, t, :], hT[:, t % 2, c, :], wg[:, c, :], start=(c == 0), stop=(c == C - 1))
                    if t == G8 - 1:
                        last.then_inc(lg_made, 1)

                with pe.Fori(0, NG // 2) as j:
                    for q in range(2):
                        turn(j, q, 0)
                        for t in range(G8):
                            if t + 1 < G8:
                                turn(j, q, t + 1)
                            score(j, q, t)
                pe.wait_ge(pr_ready, 1)
                for g in range(NG):
                    last = pe.transpose(pt[g // 4][:, g % 4, :], pr[:, g * G8:(g + 1) * G8, :].rearrange("p t e -> p (t e)"), ident[:, :])
                    if g % 4 == 3:
                        last.then_inc(pT_made, 1)
                pe.wait_ge(hot_ready, 1)
                for i in range(2):
                    for g in range(NG):
                        n = (i * NG + g) // 4
                        last = pe.transpose(pt[n][:, g % 4, :], hot[:, i, g * SP:(g + 1) * SP, :].rearrange("p s b -> p (s b)"), ident[:, :])
                        if g % 4 == 3:
                            last.then_inc(hotT_made, 1)

            @block.scalar
            def _(act):
                act.sem_inc(hT_copied, 2)
                with act.Fori(0, NG // 2) as j:
                    for q in range(2):
                        for t in range(G8):
                            act.wait_ge(hT_made, (2 * G8) * j + (G8 * q + t + 1))
                            act.activation(hT[:, t % 2], ph[t % 2][:, :, :], ACT.Copy).then_inc(hT_copied, 1)
                act.wait_ge(low_ready, 1)
                act.activation(pr[:, :, :], lg[:, :, :], ACT.Exp).then_inc(exp_done, 1)

            @block.vector
            def _(dve):
                link = Chain(dve, chain, 0)
                dve.wait_ge(w_loaded, 16 * len(loads))
                link(dve.tensor_scalar(iota64[:, :], iota[:, :], 64.0, None, ALU.add))
                dve.sem_inc(lg_copied, 2)
                with dve.Fori(0, NG // 2) as j:
                    for q in range(2):
                        dve.wait_ge(lg_made, 2 * j + (q + 1))
                        dve.tensor_copy(lg[:, bass.ds((2 * G8) * j + G8 * q, G8), :], pl[q][:, :, :]).then_inc(lg_copied, 1)
                dve.wait_ge(lg_copied, NG + 2)
                link(dve.tensor_reduce(tmax[:, :], lg[:, :, :], AX.X, ALU.max))
                dve.tensor_tensor(lg[:, :, :], lg[:, :, :], tmax[:, :].unsqueeze(2).broadcast_to([P, NT, E]),
                                  ALU.subtract).then_inc(low_ready, 1)
                dve.wait_ge(exp_done, 1)
                link(dve.tensor_reduce(tsum[:, :], pr[:, :, :], AX.X, ALU.add))
                link(dve.reciprocal(tsum[:, :], tsum[:, :]))
                dve.tensor_tensor(pr[:, :, :], pr[:, :, :], tsum[:, :].unsqueeze(2).broadcast_to([P, NT, E]),
                                  ALU.mult).then_inc(pr_ready, 1)
                for n in range(2):
                    dve.wait_ge(pT_made, n + 1)
                    last = dve.tensor_copy(pT[:, n * 16:(n + 1) * 16, :].rearrange("p s b -> p (s b)"),
                                           pt[n][:, :, :].rearrange("p g t -> p (g t)"))
                link(last)

                def wide(a):
                    return a.unsqueeze(2).broadcast_to([P, SG, B])

                def row(a):
                    return a[:, :].unsqueeze(1).broadcast_to([P, SG, B])

                def first_of_top(index):
                    link(dve.tensor_reduce(m[:, :], pT[:, :, :], AX.X, ALU.max))
                    link(dve.tensor_tensor(eq[:, :, :], pT[:, :, :], wide(m[:, :]), ALU.is_equal))
                    link(dve.scalar_tensor_tensor(out=eq[:, :, :], in0=eq[:, :, :], scalar=-64.0, in1=row(iota64),
                                                  op0=ALU.mult, op1=ALU.add))
                    link(dve.tensor_reduce(index[:, :], eq[:, :, :], AX.X, ALU.min))

                first_of_top(i1)
                link(dve.tensor_tensor(eq[:, :, :], row(iota), wide(i1[:, :]), ALU.is_equal))
                link(dve.scalar_tensor_tensor(out=pT[:, :, :], in0=eq[:, :, :], scalar=-4.0, in1=pT[:, :, :],
                                              op0=ALU.mult, op1=ALU.add))
                first_of_top(i2)
                dve.tensor_tensor(lo_hi[:, 0, :], i1[:, :], i2[:, :], ALU.min)
                link(dve.tensor_tensor(lo_hi[:, 1, :], i1[:, :], i2[:, :], ALU.max))
                for i in range(2):
                    last = dve.tensor_tensor(hot[:, i], row(iota), wide(lo_hi[:, i, :]), ALU.is_equal)
                last.then_inc(hot_ready, 1)
                for i in range(2):
                    for g in range(NG):
                        n = (i * NG + g) // 4
                        dve.wait_ge(hotT_made, n + 1)
                        slots = sel[:, g * G8:(g + 1) * G8, :].rearrange("p t (e s i) -> p (t e) s i", e=E, i=2)[:, :, :, i]
                        dve.tensor_tensor(slots, pt[n][:, g % 4, :].unsqueeze(2).broadcast_to([P, P, SP]),
                                          posmask[:, :].unsqueeze(1).broadcast_to([P, P, SP]), ALU.mult).then_inc(sel_ready, 1)

        with Stage(nc, "gather") as st:
            sem = st.sem
            pg = [st.ps(f"pg{q}", [P, C, P]) for q in range(4)]
            x_loaded = [sem(f"x_loaded{q}") for q in range(2)]
            made, copied = sem("made"), sem("copied")
            block = st.block()

            @block.sync
            def _(sp):
                for q in range(2):
                    load_group(sp, q, q, x_loaded[q])
                with sp.Fori(0, NG // 2 - 1) as j:
                    for q in range(2):
                        sp.wait_ge(made, (2 * G8) * j + G8 * (q + 1))
                        load_group(sp, 2 * j + (q + 2), q, x_loaded[q])

            @block.tensor
            def _(pe):
                with pe.Fori(0, NG // 2) as j:
                    for q in range(2):
                        pe.wait_ge(x_loaded[q], 64 * j + 64)
                        for t in range(G8):
                            pe.wait_ge(copied, (2 * G8) * j + (G8 * q + t + 1))
                            for c in range(C):
                                last = pe.matmul(pg[t % 4][:, c, :], xg[:, q, t, c * P:(c + 1) * P],
                                                 sel[:, bass.ds((2 * G8) * j + (G8 * q + t), 1), :].rearrange("p o s -> p (o s)"),
                                                 start=True, stop=True)
                            last.then_inc(made, 1)

            @block.scalar
            def _(act):
                act.sem_inc(copied, 4)
                with act.Fori(0, NG // 2) as j:
                    for q in range(2):
                        for t in range(G8):
                            act.wait_ge(made, (2 * G8) * j + (G8 * q + t + 1))
                            act.activation(hg[:, :, :, bass.ds((2 * G8 * SL) * j + SL * (G8 * q + t), SL)],
                                           pg[t % 4][:, :, :].rearrange("p c (e s) -> p c e s", e=E), ACT.Copy).then_inc(copied, 1)

        with Stage(nc, "expert") as st:
            sb, ps, sem = st.sb, st.ps, st.sem
            wq = sb("wq", [P, 2, C, F])
            wkv = sb("wkv", [P, 2, C, 2 * F])
            wo = sb("wo", [P, 2, D])
            bqkv = sb("bqkv", [P, 2, 2])
            bo = sb("bo", [P, C])
            sum4 = sb("sum4", [F, 4, P])
            pick4 = sb("pick4", [4, 4, P])
            q_sb = sb("q", [F, 2, ES])
            kv = sb("kv", [P, 2, ES])
            prod = sb("prod", [F, 2, 4, S])
            nmax = sb("nmax", [4, 2])
            rsum = sb("rsum", [4, 2])
            prob = sb("prob", [4, 2, S])
            pv = sb("pv", [P, 4, S])
            av = sb("av", [P, 2, ES])
            pq, pkv, pa = ps("pq", [F, 512]), ps("pkv", [P, 512]), ps("pa", [P, 512])
            pb = ps("pb", [P, 4, S])
            po = [ps(f"po{c}", [P, 512]) for c in range(C)]
            w_loaded = [sem(f"w_loaded{q}") for q in range(2)]
            c_loaded = sem("c_loaded")
            q_made, kv_made, q_ready, kv_ready = sem("q_made"), sem("kv_made"), sem("q_ready"), sem("kv_ready")
            prod_ready, att_made, max_ready, exp_done = sem("prod_ready"), sem("att_made"), sem("max_ready"), sem("exp_done")
            prob_ready, spread_made, av_ready = sem("prob_ready"), sem("spread_made"), sem("av_ready")
            out_made, out_copied, chain = sem("out_made"), sem("out_copied"), sem("chain")
            block = st.block()
            PER = 4

            @block.sync
            def _(sp):
                for dst, src in ((sum4[:, :, :], sum4_d), (pick4[:, :, :], pick4_d), (bo[:, :], bo_d)):
                    sp.dma_start(dst, src).then_inc(c_loaded, 16)

                def load(h, q):
                    sp.dma_start(wq[:, q], wq_d[h].rearrange("(c p) f -> p c f", p=P)).then_inc(w_loaded[q], 16)
                    sp.dma_start(wkv[:, q], wkv_d[h].rearrange("(c p) f -> p c f", p=P)).then_inc(w_loaded[q], 16)
                    sp.dma_start(wo[F:P, q], wo_d[h]).then_inc(w_loaded[q], 16)
                    sp.dma_start(bqkv[:, q], bqkv_d[h]).then_inc(w_loaded[q], 16)

                load(0, 0)
                load(1, 1)
                with sp.Fori(0, E // 2 - 1) as j:
                    for q in range(2):
                        sp.wait_ge(out_made, 2 * j + (q + 1))
                        load(2 * j + (q + 2), q)

            @block.tensor
            def _(pe):
                def project(j, q):
                    pe.wait_ge(w_loaded[q], (16 * PER) * j + 16 * PER)
                    pe.wait_ge(kv_ready, 2 * j + (q + 1))
                    pe.wait_ge(q_ready, 2 * j + (q + 1))
                    for c in range(C):
                        tok = hg[:, c, bass.ds(2 * j + q, 1), :].rearrange("p o s -> p (o s)")
                        last = pe.matmul(pq[:, :], wq[:, q, c, :], tok, start=(c == 0), stop=(c == C - 1))
                    last.then_inc(q_made, 1)
                    for c in range(C):
                        tok = hg[:, c, bass.ds(2 * j + q, 1), :].rearrange("p o s -> p (o s)")
                        last = pe.matmul(pkv[:, :], wkv[:, q, c, :], tok, start=(c == 0), stop=(c == C - 1))
                    last.then_inc(kv_made, 1)

                def attend(j, q):
                    pe.wait_ge(prod_ready, 2 * j + (q + 1))
                    for n in range(4):
                        last = pe.matmul(pa[:, 0:S], sum4[:, n, :], prod[:, q, n, :], start=(n == 0), stop=(n == 3))
                    last.then_inc(att_made, 1)

                def mix(j, q):
                    pe.wait_ge(prob_ready, 2 * j + (q + 1))
                    pe.wait_ge(av_ready, 2 * j + (q + 1))
                    for n in range(4):
                        last = pe.matmul(pb[:, n, :], pick4[:, n, :], prob[:, q, :], start=True, stop=True)
                    last.then_inc(spread_made, 1)
                    pe.wait_ge(av_ready, 2 * j + (q + 2))
                    pe.wait_ge(out_copied, 2 * j + (q + 1))
                    for c in range(C):
                        last = pe.matmul(po[c][:, :], wo[F:P, q, c * P:(c + 1) * P], av[F:P, q, :], start=True, stop=True)
                    last.then_inc(out_made, 1)

                pe.wait_ge(c_loaded, 48)
                project(0, 0)
                with pe.Fori(0, E // 2 - 1) as j:
                    for q in range(2):
                        attend(j, q)
                        project(*((j, 1) if q == 0 else (j + 1, 0)))
                        mix(j, q)
                attend(E // 2 - 1, 0)
                project(E // 2 - 1, 1)
                mix(E // 2 - 1, 0)
                attend(E // 2 - 1, 1)
                mix(E // 2 - 1, 1)

            @block.scalar
            def _(act):
                def keys(j, q):
                    act.wait_ge(kv_made, 2 * j + (q + 1))
                    act.activation(kv[:, q, :], pkv[:, :], ACT.Identity, bias=bqkv[:, q, 0:1]).then_inc(kv_ready, 1)

                def rest(j, q, nxt):
                    act.wait_ge(max_ready, 2 * j + (q + 1))
                    act.activation(prob[:, q, :], pa[0:4, 0:S], ACT.Exp, bias=nmax[:, q:q + 1],
                                   accum_out=rsum[:, q:q + 1]).then_inc(exp_done, 1)
                    if nxt is not None:
                        keys(*nxt)
                    act.wait_ge(out_made, 2 * j + (q + 1))
                    for c in range(C):
                        last = act.activation(hg[:, c, bass.ds(2 * j + q, 1), :].rearrange("p o s -> p (o s)"), po[c][:, :],
                                              ACT.Identity, bias=bo[:, c:c + 1])
                    last.then_inc(out_copied, 1)

                act.sem_inc(kv_ready, 1)
                act.sem_inc(out_copied, 1)
                act.wait_ge(c_loaded, 48)
                keys(0, 0)
                with act.Fori(0, E // 2 - 1) as j:
                    rest(j, 0, (j, 1))
                    rest(j, 1, (j + 1, 0))
                rest(E // 2 - 1, 0, (E // 2 - 1, 1))
                rest(E // 2 - 1, 1, None)

            @block.vector
            def _(dve):
                def pairs(j, q):
                    dve.wait_ge(q_made, 2 * j + (q + 1))
                    dve.tensor_scalar(q_sb[:, q, :], pq[:, :], bqkv[0:F, q, 1:2], 0.125, ALU.add, ALU.mult).then_inc(q_ready, 1)
                    dve.wait_ge(q_ready, 2 * j + (q + 2))
                    dve.wait_ge(kv_ready, 2 * j + (q + 2))
                    dve.tensor_tensor(prod[:, q].rearrange("p (i k) b -> p i k b", i=2),
                                      q_sb[:, q, :].rearrange("p (b i) -> p i b", i=2).unsqueeze(2).broadcast_to([F, 2, 2, S]),
                                      kv[0:F, q, :].rearrange("p (b k) -> p k b", k=2).unsqueeze(1).broadcast_to([F, 2, 2, S]),
                                      ALU.mult).then_inc(prod_ready, 1)

                def softmax(j, q):
                    dve.wait_ge(att_made, 2 * j + (q + 1))
                    dve.tensor_reduce(nmax[:, q:q + 1], pa[0:4, 0:S], AX.X, ALU.max, negate=True).then_inc(max_ready, 1)
                    dve.wait_ge(exp_done, 2 * j + (q + 1))
                    link(dve.reciprocal(rsum[:, q:q + 1], rsum[:, q:q + 1]))
                    dve.tensor_scalar(prob[:, q, :], prob[:, q, :], rsum[:, q:q + 1], None, ALU.mult).then_inc(prob_ready, 1)

                def weigh(j, q):
                    dve.wait_ge(spread_made, 2 * j + (q + 1))
                    v = kv[F:P, q, :].rearrange("p (b k) -> p k b", k=2).unsqueeze(1).broadcast_to([F, 2, 2, S])
                    link(dve.tensor_tensor(pv[F:P].rearrange("p (i k) b -> p i k b", i=2),
                                           pb[F:P].rearrange("p (i k) b -> p i k b", i=2), v, ALU.mult))
                    w = pv[F:P].rearrange("p (i k) b -> p i k b", i=2)
                    dve.tensor_tensor(av[F:P, q, :].rearrange("p (b i) -> p i b", i=2), w[:, :, 0, :], w[:, :, 1, :],
                                      ALU.add).then_inc(av_ready, 1)

                link = Chain(dve, chain, 4)
                dve.sem_inc(q_ready, 1)
                dve.sem_inc(av_ready, 1)
                pairs(0, 0)
                link.begin(0)
                with dve.Fori(0, E // 2 - 1) as j:
                    link.turn = j
                    for q in range(2):
                        softmax(j, q)
                        pairs(*((j, 1) if q == 0 else (j + 1, 0)))
                        weigh(j, q)
                link.end(E // 2 - 1)
                softmax(E // 2 - 1, 0)
                pairs(E // 2 - 1, 1)
                weigh(E // 2 - 1, 0)
                softmax(E // 2 - 1, 1)
                weigh(E // 2 - 1, 1)

        with Stage(nc, "scatter") as st:
            sb, ps, sem = st.sb, st.ps, st.sem
            NP = G8 // 2
            PT = 2 * NP
            last_pair = (NG // 2 - 1, PT - 1)
            slots = sb("slots", [P, 2, 2, C + 1, P])
            turned = sb("turned", [P, 2, 2, C + 1, P])
            ln_gb = sb("ln_gb", [P, 2, D])
            spacer = sb("spacer", [P, 1])
            eps = sb("eps", [P, 2])
            minus_half = sb("minus_half", [P, 2])
            r = sb("r", [P, 2, 2, D])
            z = sb("z", [P, 2, 2, D])
            r2 = sb("r2", [P, 2, 2, D])
            stats = sb("stats", [P, 2, 2, 6])
            mv = sb("mv", [P, 2, 2, 2])
            stats2 = sb("stats2", [P, 2, 2, 6])
            mv2 = sb("mv2", [P, 2, 2, 2])
            veps = sb("veps", [P, 2, 2, 2])
            rstd = sb("rstd", [P, 2, 2])
            rstd2 = sb("rstd2", [P, 2, 2])
            yg = sb("yg", [P, 2, G8, D])
            pt = [ps(f"pt{k}", [P, C + 1, P]) for k in range(4)]
            py = [ps(f"py{k}", [P, 2, D]) for k in range(2)]
            w_loaded = sem("w_loaded")
            x_loaded = [sem(f"x_loaded{q}") for q in range(2)]
            y_stored = [sem(f"y_stored{q}") for q in range(2)]
            slots_ready, turn_made, turn_copied = sem("slots_ready"), sem("turn_made"), sem("turn_copied")
            y_made, res_added, var_ready, rstd_ready = sem("y_made"), sem("res_added"), sem("var_ready"), sem("rstd_ready")
            z_ready, affine_done, var2_ready, rstd2_ready = sem("z_ready"), sem("affine_done"), sem("var2_ready"), sem("rstd2_ready")
            y_ready, chain, pool_chain = sem("y_ready"), sem("chain"), sem("pool_chain")
            block = st.block()

            @block.sync
            def _(sp):
                for n in range(2):
                    sp.dma_start(ln_gb[:, n, :], ln_d[n].partition_broadcast(P)).then_inc(w_loaded, 16)
                for q in range(2):
                    load_group(sp, q, q, x_loaded[q])
                    sp.sem_inc(y_stored[q], 64)

                def store(j, q):
                    sp.wait_ge(y_ready, (2 * NP) * j + NP * (q + 1))
                    for s in range(SP):
                        sp.dma_start(xg_out[2 * j + q][s], yg[s * B:(s + 1) * B, q]).then_inc(y_stored[q], 16)

                with sp.Fori(0, NG // 2 - 1) as j:
                    for q in range(2):
                        store(j, q)
                        load_group(sp, 2 * j + (q + 2), q, x_loaded[q])
                store(NG // 2 - 1, 0)
                store(NG // 2 - 1, 1)
                for q in range(2):
                    sp.wait_ge(y_stored[q], 64 * (NG // 2 + 1))

            @block.tensor
            def _(pe):
                def turn(j, k):
                    n, p = PT * j + (k + 1), k % 2
                    pe.wait_ge(slots_ready, n)
                    pe.wait_ge(turn_copied, n)
                    for t in range(2):
                        for c in range(C + 1):
                            last = pe.transpose(pt[2 * p + t][:, c, :], slots[:, p, t, c, :], ident[:, :])
                    last.then_inc(turn_made, 1)

                def scatter(j, k):
                    n, p = PT * j + (k + 1), k % 2
                    pe.wait_ge(turn_copied, n + 2)
                    pe.wait_ge(res_added, n)
                    for t in range(2):
                        last = pe.matmul(py[p][:, t, :], turned[:, p, t, C, :],
                                         turned[:, p, t, 0:C, :].rearrange("p c d -> p (c d)"), start=True, stop=True)
                    last.then_inc(y_made, 1)

                def pair(this, nxt):
                    if nxt is not None:
                        turn(*nxt)
                    scatter(*this)

                turn(0, 0)
                in_turns(pe, pair, NG // 2, PT, (0, 1))

            @block.scalar
            def _(act):
                def stage(j, k):
                    for t in range(2):
                        tile = (PT * 2) * j + (2 * k + t)
                        act.activation(slots[:, k % 2, t, 0:C, :].rearrange("p c (e s) -> p c e s", e=E),
                                       hg[:, :, :, bass.ds(tile * SL, SL)], ACT.Copy)
                        last = act.activation(slots[:, k % 2, t, C, :], sel[:, bass.ds(tile, 1), :].rearrange("p o s -> p (o s)"),
                                              ACT.Copy)
                    last.then_inc(slots_ready, 1)

                def copy(j, k):
                    act.wait_ge(turn_made, PT * j + (k + 1))
                    for t in range(2):
                        last = act.activation(turned[:, k % 2, t], pt[2 * (k % 2) + t][:, :, :], ACT.Copy)
                    last.then_inc(turn_copied, 1)

                def pair(nxt, after):
                    if nxt is not None:
                        copy(*nxt)
                    if after is not None:
                        act.wait_ge(turn_made, PT * after[0] + (after[1] - 1))
                        stage(*after)

                act.sem_inc(turn_copied, 2)
                stage(0, 0)
                stage(0, 1)
                copy(0, 0)
                in_turns(act, pair, NG // 2, PT, (1, 2))

            @block.gpsimd
            def _(pool):
                def rstd_of(out, v, m, ready, done, n):
                    pool.wait_ge(ready, n)
                    link(pool.tensor_tensor(v, m, eps[:, :], ALU.add))
                    pool.tensor_tensor(out, v, minus_half[:, :], ALU.pow).then_inc(done, 1)

                def first(j, k):
                    rstd_of(rstd[:, k % 2], veps[:, 0, k % 2], mv[:, k % 2, :, 1], var_ready, rstd_ready, PT * j + (k + 1))

                def affine(j, k):
                    p = k % 2
                    pool.wait_ge(z_ready, PT * j + (k + 1))
                    link(pool.tensor_tensor(z[:, p], z[:, p], ln_gb[:, 0, :].unsqueeze(1).broadcast_to([P, 2, D]), ALU.mult))
                    pool.tensor_tensor(z[:, p], z[:, p], ln_gb[:, 1, :].unsqueeze(1).broadcast_to([P, 2, D]),
                                       ALU.add).then_inc(affine_done, 1)

                def second(j, k):
                    rstd_of(rstd2[:, k % 2], veps[:, 1, k % 2], mv2[:, k % 2, :, 1], var2_ready, rstd2_ready, PT * j + (k + 1))

                def pair(this, one_back, two_back):
                    first(*this)
                    if one_back is not None:
                        affine(*one_back)
                    if two_back is not None:
                        second(*two_back)

                link = Chain(pool, pool_chain, PT * 3)
                pool.memset(eps[:, :], LN_EPS)
                link(pool.memset(minus_half[:, :], -0.5))
                pool.wait_ge(w_loaded, 32)
                in_turns(pool, pair, NG // 2, PT, (0, -1, -2), link)
                affine(*last_pair)
                second(last_pair[0], last_pair[1] - 1)
                second(*last_pair)

            @block.vector
            def _(dve):
                def moments(st_, mv_, src, ready):
                    for t in range(2):
                        last = dve.bn_stats(st_[:, t, :], src[:, t, :])
                    link(last)
                    dve.memset(spacer[:, :], 0.0)
                    for t in range(2):
                        last = dve.bn_aggr(mv_[:, t, :], st_[:, t, :])
                    last.then_inc(ready, 1)

                def apply(out, src, mv_, rs):
                    for t in range(2):
                        last = dve.tensor_scalar(out[:, t, :], src[:, t, :], mv_[:, t, 0:1], rs[:, t:t + 1],
                                                 ALU.subtract, ALU.mult)
                    return last

                def x_of(k):
                    return xg[:, k // NP, 2 * (k % NP):2 * (k % NP) + 2, :]

                def scattered(j, k):
                    p = k % 2
                    if k % NP == 0:
                        dve.wait_ge(x_loaded[k // NP], 64 * j + 64)
                    if not (type(j) is int and PT * j + k < 2):
                        dve.wait_ge(z_ready, PT * j + (k - 1))
                    dve.wait_ge(y_made, PT * j + (k + 1))
                    link(dve.tensor_tensor(r[:, p], py[p][:, :, :], x_of(k), ALU.add))
                    dve.sem_inc(res_added, 1)
                    moments(stats[:, p], mv[:, p], r[:, p], var_ready)

                def first_norm(j, k):
                    p = k % 2
                    dve.wait_ge(rstd_ready, PT * j + (k + 1))
                    apply(z[:, p], r[:, p], mv[:, p], rstd[:, p]).then_inc(z_ready, 1)

                def residual(j, k):
                    p = k % 2
                    if not (type(j) is int and PT * j + k < 2):
                        dve.wait_ge(y_ready, PT * j + (k - 1))
                    dve.wait_ge(affine_done, PT * j + (k + 1))
                    link(dve.tensor_tensor(r2[:, p], z[:, p], x_of(k), ALU.add))
                    moments(stats2[:, p], mv2[:, p], r2[:, p], var2_ready)

                def finish(j, k):
                    p, q = k % 2, k // NP
                    dve.wait_ge(rstd2_ready, PT * j + (k + 1))
                    if k % NP == 0:
                        dve.wait_ge(y_stored[q], 64 * j + 64)
                    at = 2 * (k % NP)
                    apply(yg[:, q, at:at + 2], r2[:, p], mv2[:, p], rstd2[:, p]).then_inc(y_ready, 1)

                def pair(this, one_back, two_back, three_back):
                    scattered(*this)
                    if one_back is not None:
                        first_norm(*one_back)
                    if two_back is not None:
                        residual(*two_back)
                    if three_back is not None:
                        finish(*three_back)

                link = Chain(dve, chain, PT * 4)
                dve.sem_inc(res_added, 2)
                in_turns(dve, pair, NG // 2, PT, (0, -1, -2, -3), link)
                turn, k = last_pair
                first_norm(turn, k)
                residual(turn, k - 1)
                finish(turn, k - 2)
                residual(turn, k)
                finish(turn, k - 1)
                finish(turn, k)


def mamba(nc, x_in, x_out, ct_dram, g_d, win_d, wout_d, conv_d, wx_d, dtp_d, alog_d, ident_d):
    DI = wout_d.shape[0]
    IC = DI // P
    N = alog_d.shape[2]
    GB = 2
    NG = B // GB
    TT = GB * T
    GS = GB * S
    xf_in = x_in.rearrange("(g b) (t p) d -> g p (b t) d", b=GB, p=P)
    xf_out = x_out.rearrange("(g b) (t p) d -> g p (b t) d", b=GB, p=P)
    with Stage(nc, "ma") as st:
        sb, ps, sem = st.sb, st.ps, st.sem
        ident = sb("ident", [P, P])
        gain = sb("gain", [P, C])
        win = sb("win", [P, C, 2 * DI])
        wout = sb("wout", [P, IC, D])
        wx = sb("wx", [P, IC, 2 * N + 1])
        conv = sb("conv", [P, IC, 5])
        dtp = sb("dtp", [P, 3, IC])
        A = sb("A", [P, IC, N])
        k256 = sb("k256", [P, TT])
        eps6 = sb("eps6", [P, TT])
        eps5 = sb("eps5", [P, TT])
        minus_half = sb("minus_half", [P, TT])
        spacer = sb("spacer", [P, 1])
        x = sb("x", [P, TT, D])
        xr = sb("xr", [P, TT, D])
        square = sb("square", [P, TT, D])
        ssq = sb("ssq", [P, TT])
        ms = sb("ms", [P, TT])
        rms = sb("rms", [P, TT])
        xn = sb("xn", [P, TT, D])
        xnT = sb("xnT", [P, C, GS])
        xc = sb("xc", [P, 2, IC, GS])
        sz = sb("sz", [P, 2, IC, GS])
        dt = sb("dt", [P, 2, IC, GS])
        par_t = sb("par_t", [P, 2, TT, 2 * N + 1])
        ct = sb("ct", [N + 1, GS])
        lrep = sb("lrep", [P, GS])
        av = sb("av", [P, IC, GS])
        ln1 = sb("ln1", [P, IC, GS])
        w1 = sb("w1", [P, IC, GS])
        uT = sb("uT", [P, 2, TT, DI])
        bu = sb("bu", [P, 2, TT, DI])
        a = sb("a", [P, 2, IC, GS])
        h = sb("h", [P, 2, IC, GS])
        crep = sb("crep", [P, 4, GS])
        ch = sb("ch", [P, 2, IC, GS])
        yv = w1
        r = sb("r", [P, TT, D])
        stats = sb("stats", [P, TT, 6])
        mv = sb("mv", [P, TT, 2])
        veps = sb("veps", [P, TT])
        rstd = sb("rstd", [P, TT])
        y = sb("y", [P, TT, D])
        u = av
        py = [ps(f"py{c}", [P, GS]) for c in range(IC)]
        pbu = [ps(f"pbu{k}", [P, GS]) for k in range(2)]
        pm = [ps(f"pm{k}", [P, GS]) for k in range(2)]

        w_loaded, x_loaded, xr_loaded, y_stored = sem("w_loaded"), sem("x_loaded"), sem("xr_loaded"), sem("y_stored")
        ct_stored, lrep_loaded = sem("ct_stored"), sem("lrep_loaded")
        crep_loaded = [sem(f"crep_loaded{k}") for k in range(4)]
        setup_done, ssq_ready, rms_ready, xn_ready = sem("setup_done"), sem("ssq_ready"), sem("rms_ready"), sem("xn_ready")
        xT_made, xT_copied, in_made = sem("xT_made"), sem("xT_copied"), sem("in_made")
        z_made, exp_ready = sem("z_made"), sem("exp_ready")
        conv_done, z_copied, silu_done = sem("conv_done"), sem("z_copied"), sem("silu_done")
        par_made, par_copied, ct_made, ct_copied = sem("par_made"), sem("par_copied"), sem("ct_made"), sem("ct_copied")
        ln_ready, dt_ready, u_ready, uT_made, uT_copied = sem("ln_ready"), sem("dt_ready"), sem("u_ready"), sem("uT_made"), sem("uT_copied")
        bu_ready, bu_turned, a_ready, scanned = sem("bu_ready"), sem("bu_turned"), sem("a_ready"), sem("scanned")
        multiplied, summed, gated, yv_ready = sem("multiplied"), sem("summed"), sem("gated"), sem("yv_ready")
        out_made, res_added, var_ready, rstd_ready, y_ready = sem("out_made"), sem("res_added"), sem("var_ready"), sem("rstd_ready"), sem("y_ready")
        act_chain, dve_chain, pool_chain = sem("act_chain"), sem("dve_chain"), sem("pool_chain")
        block = st.block()
        loads = [(ident[:, :], ident_d), (gain[:, :], g_d), (win[:, :, :], win_d.rearrange("(c p) f -> p c f", p=P)),
                 (wout[:, :, :], wout_d.rearrange("(c p) f -> p c f", p=P)),
                 (wx[:, :, :], wx_d.rearrange("(c p) f -> p c f", p=P)),
                 (conv[:, :, :], conv_d), (dtp[:, :, :], dtp_d), (A[:, :, :], alog_d)]

        def groups(eng, group, link=None, turns=NG // 2 - 1):
            if link:
                link.turn = None
            group(0, 0, True, False)
            if link:
                link.begin(0)
            with eng.Fori(0, turns) as j:
                if link:
                    link.turn = j
                group(2 * j + 1, 1, False, False)
                group(2 * j + 2, 0, False, False)
            if link:
                link.end(turns)
            for g in range(2 * turns + 1, NG):
                group(g, g % 2, False, g == NG - 1)

        @block.sync
        def _(sp):
            def load_x(g):
                sp.dma_start(x[:, :, :], xf_in[g]).then_inc(x_loaded, 16)

            def load_c(g, par, s):
                sp.dma_start(crep[:, s % 4, :], ct_dram[par, s, :].partition_broadcast(P)).then_inc(crep_loaded[s % 4], 16)

            def spread(g, par):
                sp.wait_ge(ct_copied, g + 1)
                sp.dma_start(ct_dram[par], ct[:, :]).then_inc(ct_stored, 16)
                sp.wait_ge(ct_stored, 16 * g + 32)
                sp.dma_start(lrep[:, :], ct_dram[par, N, :].partition_broadcast(P)).then_inc(lrep_loaded, 16)

            def group(g, par, first, last):
                for s in range(N):
                    if s == 2 and not last:
                        if not (type(g) is int and g + 2 >= NG):
                            sp.wait_ge(xn_ready, g + 2)
                            load_x(g + 2)
                    if s == 9:
                        if not first:
                            sp.wait_ge(y_ready, g)
                            sp.dma_start(xf_out[g - 1], y[:, :, :]).then_inc(y_stored, 16)
                        sp.dma_start(xr[:, :, :], xf_in[g]).then_inc(xr_loaded, 16)
                    if s == 11 and not last:
                        spread(g + 1, 1 - par)
                    sp.wait_ge(multiplied, N * g + (s + 3))
                    if s + 4 < N:
                        load_c(g, par, s + 4)
                    elif not last:
                        load_c(g + 1, 1 - par, s + 4 - N)

            for dst, src in loads:
                sp.dma_start(dst, src).then_inc(w_loaded, 16)
            sp.sem_inc(y_stored, 16)
            sp.sem_inc(ct_stored, 16)
            load_x(0)
            sp.wait_ge(xn_ready, 1)
            load_x(1)
            spread(0, 0)
            for s in range(4):
                load_c(0, 0, s)
            groups(sp, group, turns=NG // 2 - 2)
            sp.wait_ge(y_ready, NG)
            sp.dma_start(xf_out[NG - 1], y[:, :, :]).then_inc(y_stored, 16)
            sp.wait_ge(y_stored, 16 * (NG + 1))

        @block.tensor
        def _(pe):
            def turn_x(n, c):
                if c == 0:
                    pe.wait_ge(xn_ready, n + 1)
                    if not (type(n) is int and n == 0):
                        pe.wait_ge(uT_copied, 4 * n)
                for t in range(TT):
                    last = pe.transpose(pm[c][:, t * P:(t + 1) * P], xn[:, t, c * P:(c + 1) * P], ident[:, :])
                last.then_inc(xT_made, 1)

            def project_in(n, f, after_out):
                if f == 0:
                    pe.wait_ge(xT_copied, 2 * n + 2)
                    if after_out:
                        pe.wait_ge(res_added, 2 * n - 2)
                for half, copied, done in ((0, conv_done, in_made), (1, z_copied, z_made)):
                    if f > 0:
                        pe.wait_ge(copied, 4 * n + f)
                    for c in range(C):
                        last = pe.matmul(pm[half][:, :], win[:, c, half * DI + f * P:half * DI + (f + 1) * P], xnT[:, c, :],
                                         start=(c == 0), stop=(c == C - 1))
                    last.then_inc(done, 1)

            def parameters(n, par):
                pe.wait_ge(silu_done, n + 1)
                for t in range(TT):
                    for c in range(IC):
                        last = pe.matmul(pm[0][:, t * 64:t * 64 + 2 * N + 1], xc[:, par, c, t * P:(t + 1) * P], wx[:, c, :],
                                         start=(c == 0), stop=(c == IC - 1))
                last.then_inc(par_made, 1)
                for c in range(IC):
                    last = pe.matmul(pm[1][0:N + 1, :], wx[:, c, N:2 * N + 1], xc[:, par, c, :],
                                     start=(c == 0), stop=(c == IC - 1))
                last.then_inc(ct_made, 1)

            def turn_u(n, t):
                if t == 0:
                    pe.wait_ge(u_ready, n + 1)
                    pe.wait_ge(par_copied, n + 1)
                elif t == 1:
                    pe.wait_ge(ct_copied, n + 1)
                else:
                    pe.wait_ge(uT_copied, 4 * n + (t - 1))
                for c in range(IC):
                    last = pe.transpose(pm[t % 2][:, c * P:(c + 1) * P], u[:, c, t * P:(t + 1) * P], ident[:, :])
                last.then_inc(uT_made, 1)

            def state(g, s, sum_g, sum_s):
                pe.wait_ge(bu_ready, N * g + (s + 1))
                for c in range(IC):
                    pe.wait_ge(scanned, (N * IC) * g + (IC * s + c + 7))
                    for t in range(TT):
                        last = pe.transpose(pbu[c % 2][:, t * P:(t + 1) * P], bu[:, s % 2, t, c * P:(c + 1) * P], ident[:, :])
                    last.then_inc(bu_turned, 1)
                    if sum_g is not None:
                        sum_states(sum_g, sum_s, c)

            def sum_states(g, s, c):
                if c == 0:
                    pe.wait_ge(multiplied, N * g + (s + 3))
                if s == 0:
                    pe.wait_ge(gated, IC * g + (c + 1))
                last = pe.matmul(py[c][:, :], ident[:, :], ch[:, s % 2, c, :], start=(s == 0), stop=(s == N - 1))
                if c == IC - 1:
                    last.then_inc(summed, 1)

            def project_out(g, k, prep):
                if k == 0:
                    pe.wait_ge(yv_ready, g + 1)
                    if prep:
                        pe.wait_ge(xT_copied, 2 * g + 6)
                    else:
                        pe.wait_ge(uT_copied, 4 * g + 8)
                for t in range(2):
                    for c in range(IC):
                        last = pe.matmul(pm[k][:, t * D:(t + 1) * D], yv[:, c, (2 * k + t) * P:(2 * k + t + 1) * P],
                                         wout[:, c, :], start=(c == 0), stop=(c == IC - 1))
                last.then_inc(out_made, 1)

            def group(g, par, first, last):
                n, prep = g + 1, not last
                for s in range(N):
                    if s >= 2:
                        state(g, s, g, s - 2)
                    else:
                        state(g, s, None if first else g - 1, N + s - 2)
                    if s == 2 and prep:
                        turn_x(n, 0)
                        turn_x(n, 1)
                    if s in (3, 4) and not first:
                        project_out(g - 1, s - 3, prep)
                    if 5 <= s < 5 + IC and prep:
                        project_in(n, s - 5, not first)
                    if s == 10 and prep:
                        parameters(n, 1 - par)
                    if s == N - 1 and prep:
                        for t in range(TT):
                            turn_u(n, t)

            pe.wait_ge(w_loaded, 16 * len(loads))
            turn_x(0, 0)
            turn_x(0, 1)
            for f in range(IC):
                project_in(0, f, False)
            parameters(0, 0)
            for t in range(TT):
                turn_u(0, t)
            groups(pe, group)
            for s in (N - 2, N - 1):
                for c in range(IC):
                    sum_states(NG - 1, s, c)
            pe.wait_ge(yv_ready, NG)
            pe.wait_ge(res_added, 2 * NG - 2)
            for k in range(2):
                for t in range(2):
                    for c in range(IC):
                        last = pe.matmul(pm[k][:, t * D:(t + 1) * D], yv[:, c, (2 * k + t) * P:(2 * k + t + 1) * P],
                                         wout[:, c, :], start=(c == 0), stop=(c == IC - 1))
                last.then_inc(out_made, 1)

        @block.scalar
        def _(act):
            link = Chain(act, act_chain, 2 * 2)

            def squares(n):
                act.wait_ge(x_loaded, 16 * n + 16)
                for t in range(TT):
                    last = act.activation(square[:, t, :], x[:, t, :], ACT.Square, accum_out=ssq[:, t:t + 1])
                last.then_inc(ssq_ready, 1)

            def copy_xT(n, c):
                act.wait_ge(xT_made, 2 * n + (c + 1))
                act.activation(xnT[:, c, :], pm[c][:, :], ACT.Copy, scale=gain[:, c:c + 1]).then_inc(xT_copied, 1)

            def copy_z(n, par, f):
                act.wait_ge(z_made, 4 * n + (f + 1))
                act.activation(sz[:, par, f, :], pm[1][:, :], ACT.Copy).then_inc(z_copied, 1)

            def silu(n, par):
                act.wait_ge(z_copied, 4 * n + 4)
                act.activation(sz[:, par], sz[:, par], ACT.Silu)
                act.wait_ge(conv_done, 4 * n + 4)
                act.activation(xc[:, par], xc[:, par], ACT.Silu).then_inc(silu_done, 1)

            def copy_parameters(n, par):
                act.wait_ge(par_made, n + 1)
                act.activation(par_t[:, par], pm[0][:, 0:TT * 64].rearrange("p (t k) -> p t k", k=64)[:, :, 0:2 * N + 1],
                               ACT.Copy).then_inc(par_copied, 1)
                act.wait_ge(ct_made, n + 1)
                act.wait_ge(ct_stored, 16 * n + 16)
                act.activation(ct[:, :], pm[1][0:N + 1, :], ACT.Copy).then_inc(ct_copied, 1)

            def step_size(n, par):
                act.wait_ge(lrep_loaded, 16 * n + 16)
                for c in range(IC):
                    act.activation(dt[:, par, c, :], lrep[:, :], ACT.Relu, bias=dtp[:, 1, c:c + 1], scale=dtp[:, 0, c:c + 1])
                    last = act.activation(av[:, c, :], lrep[:, :], ACT.Abs, bias=dtp[:, 1, c:c + 1], scale=dtp[:, 0, c:c + 1])
                link(last)

            def step_size_log(n):
                link(act.activation(av[:, :, :], av[:, :, :], ACT.Exp, scale=-1.0))
                act.sem_inc(exp_ready, 1)
                act.activation(ln1[:, :, :], av[:, :, :], ACT.Ln, bias=1.0).then_inc(ln_ready, 1)

            def copy_uT(n, par, t):
                act.wait_ge(uT_made, 4 * n + (t + 1))
                act.activation(uT[:, par, t, :], pm[t % 2][:, :], ACT.Copy).then_inc(uT_copied, 1)

            def scale_b(g, par, s):
                if s == 0:
                    act.wait_ge(uT_copied, 4 * g + 4)
                    act.wait_ge(par_copied, g + 1)
                act.wait_ge(bu_turned, (N * IC) * g + (IC * s + 4))
                for t in range(TT):
                    last = act.activation(bu[:, s % 2, t, :], uT[:, par, t, :], ACT.Copy, scale=par_t[:, par, t, s:s + 1])
                last.then_inc(bu_ready, 1)

            def decay(g, par, s):
                if s == 0:
                    act.wait_ge(dt_ready, g + 1)
                for c in range(IC):
                    act.wait_ge(scanned, (N * IC) * g + (IC * s + c + 1))
                    act.activation(a[:, s % 2, c, :].rearrange("p (b t) -> p b t", b=GB)[:, :, 1:S],
                                   dt[:, par, c, :].rearrange("p (b t) -> p b t", b=GB)[:, :, 1:S],
                                   ACT.Exp, scale=A[:, c, s:s + 1]).then_inc(a_ready, 1)

            def group(g, par, first, last):
                n, prep, np_ = g + 1, not last, 1 - par
                for s in range(N):
                    decay(g, par, s)
                    if s == 0 and prep:
                        squares(n)
                    if s == 3 and prep:
                        copy_xT(n, 0)
                        copy_xT(n, 1)
                    if 6 <= s < 6 + IC and prep:
                        copy_z(n, np_, s - 6)
                    if s == 10 and prep:
                        silu(n, np_)
                    if s == 11 and prep:
                        copy_parameters(n, np_)
                    if s == 12 and prep:
                        step_size(n, np_)
                    if s == 13 and prep:
                        step_size_log(n)
                    if s + 1 < N:
                        scale_b(g, par, s + 1)
                    elif prep:
                        for t in range(TT):
                            copy_uT(n, np_, t)
                        scale_b(n, np_, 0)

            act.wait_ge(w_loaded, 16 * len(loads))
            link(act.activation(A[:, :, :], A[:, :, :], ACT.Exp))
            link(act.activation(A[:, :, :], A[:, :, :], ACT.Copy, scale=-1.0))
            act.wait_ge(setup_done, 1)
            squares(0)
            copy_xT(0, 0)
            copy_xT(0, 1)
            for f in range(IC):
                copy_z(0, 0, f)
            silu(0, 0)
            copy_parameters(0, 0)
            step_size(0, 0)
            step_size_log(0)
            for t in range(TT):
                copy_uT(0, 0, t)
            scale_b(0, 0, 0)
            groups(act, group, link)

        @block.gpsimd
        def _(pool):
            link = Chain(pool, pool_chain, 2 * 3)

            def rms_scale(n):
                pool.wait_ge(ssq_ready, n + 1)
                link(pool.tensor_tensor(ms[:, :], ssq[:, :], k256[:, :], ALU.mult))
                link(pool.tensor_tensor(ms[:, :], ms[:, :], eps6[:, :], ALU.add))
                pool.tensor_tensor(rms[:, :], ms[:, :], minus_half[:, :], ALU.pow).then_inc(rms_ready, 1)

            def times_c(g, s):
                pool.wait_ge(scanned, (N * IC) * g + (IC * s + IC + 8))
                pool.wait_ge(crep_loaded[s % 4], (4 * 16) * g + 16 * (s // 4 + 1))
                pool.wait_ge(summed, N * g + (s + 1))
                pool.tensor_tensor(ch[:, s % 2], h[:, s % 2], crep[:, s % 4, :].unsqueeze(1).broadcast_to([P, IC, GS]),
                                   ALU.mult).then_inc(multiplied, 1)

            def rstd_of(g):
                pool.wait_ge(var_ready, g + 1)
                link(pool.tensor_tensor(veps[:, :], mv[:, :, 1], eps5[:, :], ALU.add))
                pool.tensor_tensor(rstd[:, :], veps[:, :], minus_half[:, :], ALU.pow).then_inc(rstd_ready, 1)

            def group(g, par, first, last):
                for s in range(N):
                    if s == 1 and not last:
                        rms_scale(g + 1)
                    if s == 7 and not first:
                        rstd_of(g - 1)
                    times_c(g, s)

            pool.memset(k256[:, :], 1.0 / D)
            pool.memset(eps6[:, :], 1e-6)
            pool.memset(eps5[:, :], LN_EPS)
            link(pool.memset(minus_half[:, :], -0.5))
            pool.sem_inc(multiplied, 2)
            pool.sem_inc(summed, 2)
            rms_scale(0)
            groups(pool, group, link)
            rstd_of(NG - 1)

        @block.vector
        def _(dve):
            link = Chain(dve, dve_chain, 2 * (4 * 4 + 4 + 1 + 1))

            def normalize(n):
                dve.wait_ge(rms_ready, n + 1)
                for t in range(TT):
                    last = dve.tensor_scalar(xn[:, t, :], x[:, t, :], rms[:, t:t + 1], None, ALU.mult)
                last.then_inc(xn_ready, 1)

            def convolve(n, par, f):
                dve.wait_ge(in_made, 4 * n + (f + 1))
                out = xc[:, par, f, :].rearrange("p (b t) -> p b t", b=GB)
                src = pm[0][:, :].rearrange("p (b t) -> p b t", b=GB)
                link(dve.tensor_scalar(out, src, conv[:, f, 3:4], conv[:, f, 4:5], ALU.mult, ALU.add))
                for k in range(1, 4):
                    link(dve.scalar_tensor_tensor(out=out[:, :, k:S], in0=src[:, :, 0:S - k], scalar=conv[:, f, 3 - k:4 - k],
                                                  in1=out[:, :, k:S], op0=ALU.mult, op1=ALU.add))
                dve.sem_inc(conv_done, 1)

            def step_size(n, par):
                dve.wait_ge(exp_ready, n + 1)
                link(dve.tensor_scalar(w1[:, :, :], av[:, :, :], 1.0, 1.0, ALU.add, ALU.subtract))
                link(dve.tensor_tensor(w1[:, :, :], av[:, :, :], w1[:, :, :], ALU.subtract))

            def step_size_sum(n, par):
                dve.wait_ge(ln_ready, n + 1)
                link(dve.tensor_tensor(dt[:, par], dt[:, par], ln1[:, :, :], ALU.add))
                link(dve.tensor_tensor(dt[:, par], dt[:, par], w1[:, :, :], ALU.add))
                dve.sem_inc(dt_ready, 1)
                dve.tensor_tensor(u[:, :, :], dt[:, par], xc[:, par], ALU.mult).then_inc(u_ready, 1)

            def scans(g, s, before=None, between=None):
                dve.wait_ge(multiplied, N * g + (s + 1))
                for c in range(IC):
                    if before:
                        before(c)
                    m = (N * IC) * g + (IC * s + c + 1)
                    dve.wait_ge(a_ready, m)
                    dve.wait_ge(bu_turned, m + 8)
                    dve.tensor_tensor_scan(out=h[:, s % 2, c, :], data0=a[:, s % 2, c, :], data1=pbu[c % 2][:, :],
                                           initial=0.0, op0=ALU.mult, op1=ALU.add).then_inc(scanned, 1)
                    if between and c == 1:
                        between()

            def gate(g, par, c):
                if c == 0:
                    dve.wait_ge(summed, N * g + (N + 2))
                last = dve.scalar_tensor_tensor(out=yv[:, c, :], in0=xc[:, par, c, :], scalar=dtp[:, 2, c:c + 1],
                                                in1=py[c][:, :], op0=ALU.mult, op1=ALU.add)
                if c < IC - 1:
                    last.then_inc(gated, 1)
                else:
                    link(last)
                    dve.sem_inc(gated, 1)

            def gate_end(par):
                dve.tensor_tensor(yv[:, :, :], yv[:, :, :], sz[:, par], ALU.mult).then_inc(yv_ready, 1)

            def residual(g, k):
                dve.wait_ge(out_made, 2 * g + (k + 1))
                if k == 0:
                    dve.wait_ge(xr_loaded, 16 * g + 16)
                dve.scalar_tensor_tensor(out=r[:, 2 * k:2 * k + 2, :], in0=xr[:, 2 * k:2 * k + 2, :], scalar=2.0,
                                         in1=pm[k][:, :].rearrange("p (t d) -> p t d", t=2),
                                         op0=ALU.mult, op1=ALU.add).then_inc(res_added, 1)
                if k == 1:
                    dve.wait_ge(res_added, 2 * g + 2)
                    for t in range(TT):
                        last = dve.bn_stats(stats[:, t, :], r[:, t, :])
                    link(last)
                    dve.memset(spacer[:, :], 0.0)
                    for t in range(TT):
                        last = dve.bn_aggr(mv[:, t, :], stats[:, t, :])
                    last.then_inc(var_ready, 1)

            def finish(g):
                dve.wait_ge(rstd_ready, g + 1)
                dve.wait_ge(y_stored, 16 * g + 16)
                for t in range(TT):
                    last = dve.tensor_scalar(y[:, t, :], r[:, t, :], mv[:, t, 0:1], rstd[:, t:t + 1], ALU.subtract, ALU.mult)
                last.then_inc(y_ready, 1)

            def group(g, par, first, last):
                n, prep, np_ = g + 1, not last, 1 - par
                for s in range(N):
                    before = between = None
                    if s == 2 and not first:
                        before = lambda c: gate(g - 1, np_, c)
                    if s == 5 and not first:
                        between = lambda: residual(g - 1, 1)
                    if 6 <= s < 6 + IC and prep:
                        between = lambda: convolve(n, np_, s - 6)
                    scans(g, s, before, between)
                    if s == 2 and not first:
                        gate_end(np_)
                    if s == 1 and prep:
                        normalize(n)
                    if s == 4 and not first:
                        residual(g - 1, 0)
                    if s == 8 and not first:
                        finish(g - 1)
                    if s == 13 and prep:
                        step_size(n, np_)
                    if s == 14 and prep:
                        step_size_sum(n, np_)

            for p in range(2):
                dve.memset(a[:, p], 0.0)
            link(dve.memset(spacer[:, :], 0.0))
            dve.sem_inc(setup_done, 1)
            dve.sem_inc(bu_turned, 8)
            dve.sem_inc(scanned, 8)
            dve.sem_inc(gated, IC)
            dve.wait_ge(w_loaded, 16 * len(loads))
            normalize(0)
            for f in range(IC):
                convolve(0, 0, f)
            step_size(0, 0)
            step_size_sum(0, 0)
            groups(dve, group, link)
            for c in range(IC):
                gate(NG - 1, 1, c)
            gate_end(1)
            residual(NG - 1, 0)
            residual(NG - 1, 1)
            finish(NG - 1)


def bit_ffn(nc, x_in, x_out, wgu_d, wd_d, ident_d):
    I = wd_d.shape[0]
    IC = I // P
    ROUND = 12582912.0
    FLOOR = 1e-5
    NT = 2 * B
    BT = 8
    with Stage(nc, "ff") as st:
        sb, ps, sem = st.sb, st.ps, st.sem
        ident = sb("ident", [P, P])
        identb = sb("identb", [P, P], bf16)
        ones = sb("ones", [P, P])
        wgu_f = sb("wgu_f", [P, 2, C, I])
        wd_f = sb("wd_f", [P, IC, D])
        wgu = sb("wgu", [P, 2, C, I], bf16)
        wd = sb("wd", [P, IC, D], bf16)
        wsum = sb("wsum", [P, 3])
        wmean = sb("wmean", [P, 3])
        wscale = sb("wscale", [P, 3])
        wm127 = sb("wm127", [P, 3])
        eps = sb("eps", [P, 1])
        minus_half = sb("minus_half", [P, 1])
        spacer = sb("spacer", [P, 1])
        x = sb("x", [P, 4, T, D])
        xmax = sb("xmax", [P, 2])
        xs = sb("xs", [P, 1])
        fgu = sb("fgu", [P, 2, 2])
        xr = sb("xr", [P, D])
        xq = sb("xq", [P, 2, D], bf16)
        xT = sb("xT", [P, 2, C, P], bf16)
        g = sb("g", [P, I])
        h = sb("h", [P, I])
        hmax = sb("hmax", [P, 2])
        hs = sb("hs", [P, 1])
        fd = sb("fd", [P, 2])
        hr = sb("hr", [P, I])
        hq = sb("hq", [P, I], bf16)
        hT = sb("hT", [P, IC, P], bf16)
        r = sb("r", [P, 2, D])
        stats = sb("stats", [P, 2, 6])
        mv = sb("mv", [P, 2, 2])
        veps = sb("veps", [P, 1])
        rstd = sb("rstd", [P, 2])
        y = sb("y", [P, 2, T, D])
        pgate, pup = ps("pgate", [P, I]), ps("pup", [P, I])
        px, ph, pd = ps("px", [P, C, P], bf16), ps("ph", [P, IC, P], bf16), ps("pd", [P, 512])

        w_loaded, wsum_ready, wtotal_made, setup_done = sem("w_loaded"), sem("wsum_ready"), sem("wtotal_made"), sem("setup_done")
        x_loaded = [sem(f"x_loaded{b}") for b in range(4)]
        y_stored = [sem(f"y_stored{p}") for p in range(2)]
        xq_ready, xT_made, xT_copied = sem("xq_ready"), sem("xT_made"), sem("xT_copied")
        gate_made, up_made, g_ready, h_ready, hs_ready = sem("gate_made"), sem("up_made"), sem("g_ready"), sem("h_ready"), sem("hs_ready")
        hr_ready, hq_ready, hT_made, hT_copied = sem("hr_ready"), sem("hq_ready"), sem("hT_made"), sem("hT_copied")
        down_made, var_ready, rstd_ready, y_ready = sem("down_made"), sem("var_ready"), sem("rstd_ready"), sem("y_ready")
        chain, pool_chain = sem("chain"), sem("pool_chain")
        block = st.block()

        def tiles(eng, tile, link=None):
            turns = NT // BT

            def around(turn, k):
                return [divmod(BT * turn + k + d, BT) if 0 <= BT * turn + k + d < NT else None for d in (-1, 0, 1, 2)]

            for k in range(BT):
                tile(*around(0, k))
            if link:
                link.begin(0)
            with eng.Fori(0, turns - 2) as j:
                if link:
                    link.turn = j
                for k in range(BT):
                    tile((j + 1, k - 1) if k else (j, BT - 1), (j + 1, k),
                         *((j + 1, k + d) if k + d < BT else (j + 2, k + d - BT) for d in (1, 2)))
            if link:
                link.end(turns - 2)
            for k in range(BT):
                tile(*around(turns - 1, k))

        last_tile = (NT // BT - 1, BT - 1)

        @block.sync
        def _(sp):
            for dst, src in ((ident[:, :], ident_d), (wgu_f[:, 0], wgu_d[0].rearrange("(c p) i -> p c i", p=P)),
                             (wgu_f[:, 1], wgu_d[1].rearrange("(c p) i -> p c i", p=P)),
                             (wd_f[:, :, :], wd_d.rearrange("(c p) f -> p c f", p=P))):
                sp.dma_start(dst, src).then_inc(w_loaded, 16)
            for b in range(4):
                sp.dma_start(x[:, b], batch_tiles(x_in, b)).then_inc(x_loaded[b], 16)
            for p in range(2):
                sp.sem_inc(y_stored[p], 16)

            def store(j, b):
                sp.wait_ge(y_ready, BT * j + 2 * (b + 1))
                sp.dma_start(batch_tiles(x_out, 4 * j + b), y[:, b % 2]).then_inc(y_stored[b % 2], 16)

            with sp.Fori(0, B // 4 - 1) as j:
                for b in range(4):
                    store(j, b)
                    sp.dma_start(x[:, b], batch_tiles(x_in, 4 * j + (b + 4))).then_inc(x_loaded[b], 16)
            for b in range(4):
                store(B // 4 - 1, b)
            for p in range(2):
                sp.wait_ge(y_stored[p], 16 * (B // 2 + 1))

        @block.tensor
        def _(pe):
            def turn_x(j, k):
                pe.wait_ge(xq_ready, BT * j + (k + 1))
                for c in range(C):
                    last = pe.transpose(px[:, c, :], xq[:, k % 2, c * P:(c + 1) * P], identb[:, :])
                last.then_inc(xT_made, 1)

            def gate_up(j, k):
                pe.wait_ge(xT_copied, BT * j + (k + 1))
                pe.wait_ge(h_ready, BT * j + (k + 1))
                for m, out, done in ((0, pgate, gate_made), (1, pup, up_made)):
                    for half in range(2):
                        for c in range(C):
                            last = pe.matmul(out[:, half * 512:(half + 1) * 512], xT[:, k % 2, c, :],
                                             wgu[:, m, c, half * 512:(half + 1) * 512], start=(c == 0), stop=(c == C - 1))
                    last.then_inc(done, 1)

            def down(j, k):
                pe.wait_ge(hq_ready, BT * j + (k + 1))
                for c in range(IC):
                    last = pe.transpose(ph[:, c, :], hq[:, c * P:(c + 1) * P], identb[:, :])
                last.then_inc(hT_made, 1)
                pe.wait_ge(hT_copied, BT * j + (k + 1))
                for c in range(IC):
                    last = pe.matmul(pd[:, 0:D], hT[:, c, :], wd[:, c, :], start=(c == 0), stop=(c == IC - 1))
                last.then_inc(down_made, 1)

            pe.wait_ge(wsum_ready, 1)
            pe.matmul(pd[:, 0:3], ones[:, :], wsum[:, :], start=True, stop=True).then_inc(wtotal_made, 1)
            pe.wait_ge(setup_done, 1)
            turn_x(0, 0)
            gate_up(0, 0)
            turn_x(0, 1)

            def tile(before, this, nxt, after):
                if nxt is not None:
                    gate_up(*nxt)
                if after is not None:
                    turn_x(*after)
                down(*this)

            tiles(pe, tile)

        @block.scalar
        def _(act):
            def copy_x(j, k):
                act.wait_ge(xT_made, BT * j + (k + 1))
                act.activation(xT[:, k % 2], px[:, :, :], ACT.Copy).then_inc(xT_copied, 1)

            def gate(j, k):
                act.wait_ge(gate_made, BT * j + (k + 1))
                act.activation(g[:, :], pgate[:, :], ACT.Silu, scale=fgu[:, k % 2, 0:1]).then_inc(g_ready, 1)

            def scale_h(j, k):
                act.wait_ge(hs_ready, BT * j + (k + 1))
                act.activation(hr[:, :], h[:, :], ACT.Copy, scale=hs[:, 0:1], bias=ROUND).then_inc(hr_ready, 1)

            def copy_h(j, k):
                act.wait_ge(hT_made, BT * j + (k + 1))
                act.activation(hT[:, :, :], ph[:, :, :], ACT.Copy).then_inc(hT_copied, 1)

            def tile(before, this, nxt, after):
                if nxt is not None:
                    gate(*nxt)
                scale_h(*this)
                if after is not None:
                    copy_x(*after)
                copy_h(*this)

            act.wait_ge(setup_done, 1)
            copy_x(0, 0)
            gate(0, 0)
            copy_x(0, 1)
            tiles(act, tile)

        @block.gpsimd
        def _(pool):
            link = Chain(pool, pool_chain, BT)
            pool.memset(eps[:, :], LN_EPS)
            link(pool.memset(minus_half[:, :], -0.5))
            link.begin(0)
            with pool.Fori(0, NT // BT) as j:
                link.turn = j
                for k in range(BT):
                    pool.wait_ge(var_ready, BT * j + (k + 1))
                    link(pool.tensor_tensor(veps[:, :], mv[:, k % 2, 1:2], eps[:, :], ALU.add))
                    pool.tensor_tensor(rstd[:, k % 2:k % 2 + 1], veps[:, :], minus_half[:, :], ALU.pow).then_inc(rstd_ready, 1)
            link.end(NT // BT)

        @block.vector
        def _(dve):
            def quantize_x(j, k):
                xt, p = x[:, k // 2, k % 2, :], k % 2
                if p == 0:
                    dve.wait_ge(x_loaded[k // 2], 16 * j + 16)
                link(dve.tensor_reduce(xmax[:, p:p + 1], xt, AX.X, ALU.max, apply_absolute_value=True))
                link(dve.tensor_scalar(xmax[:, p:p + 1], xmax[:, p:p + 1], FLOOR, None, ALU.max))
                dve.tensor_scalar(fgu[:, p, :], wm127[:, 0:2], xmax[:, p:p + 1], None, ALU.mult)
                link(dve.reciprocal(xs[:, :], xmax[:, p:p + 1]))
                link(dve.tensor_scalar(xs[:, :], xs[:, :], 127.0, None, ALU.mult))
                link(dve.tensor_scalar(xr[:, :], xt, xs[:, 0:1], ROUND, ALU.mult, ALU.add))
                dve.tensor_scalar(xq[:, p, :], xr[:, :], ROUND, 127.0, ALU.subtract, ALU.min).then_inc(xq_ready, 1)

            def hidden(j, k):
                n, p = BT * j + (k + 1), k % 2
                dve.wait_ge(g_ready, n)
                dve.wait_ge(up_made, n)
                link(dve.scalar_tensor_tensor(out=h[:, :], in0=pup[:, :], scalar=fgu[:, p, 1:2], in1=g[:, :],
                                              op0=ALU.mult, op1=ALU.mult))
                dve.sem_inc(h_ready, 1)
                link(dve.tensor_reduce(hmax[:, p:p + 1], h[:, :], AX.X, ALU.max, apply_absolute_value=True))
                link(dve.tensor_scalar(hmax[:, p:p + 1], hmax[:, p:p + 1], FLOOR, None, ALU.max))
                dve.tensor_tensor(fd[:, p:p + 1], wm127[:, 2:3], hmax[:, p:p + 1], ALU.mult)
                link(dve.reciprocal(hs[:, :], hmax[:, p:p + 1]))
                dve.tensor_scalar(hs[:, :], hs[:, :], 127.0, None, ALU.mult).then_inc(hs_ready, 1)

            def quantize_h(j, k):
                dve.wait_ge(hr_ready, BT * j + (k + 1))
                dve.tensor_scalar(hq[:, :], hr[:, :], ROUND, 127.0, ALU.subtract, ALU.min).then_inc(hq_ready, 1)

            def residual(j, k):
                p = k % 2
                dve.wait_ge(down_made, BT * j + (k + 1))
                link(dve.scalar_tensor_tensor(out=r[:, p, :], in0=pd[:, 0:D], scalar=fd[:, p:p + 1],
                                              in1=x[:, k // 2, k % 2, :], op0=ALU.mult, op1=ALU.add))
                link(dve.bn_stats(stats[:, p, :], r[:, p, :]))
                dve.memset(spacer[:, :], 0.0)
                dve.bn_aggr(mv[:, p, :], stats[:, p, :]).then_inc(var_ready, 1)

            def finish(j, k):
                p, b = k % 2, k // 2
                dve.wait_ge(rstd_ready, BT * j + (k + 1))
                if p == 0:
                    dve.wait_ge(y_stored[b % 2], 32 * j + 16 * (b // 2 + 1))
                dve.tensor_scalar(y[:, b % 2, p, :], r[:, p, :], mv[:, p, 0:1], rstd[:, p:p + 1],
                                  ALU.subtract, ALU.mult).then_inc(y_ready, 1)

            link = Chain(dve, chain, BT * (5 + 4 + 2))
            dve.memset(ones[:, :], 1.0)
            dve.wait_ge(w_loaded, 64)
            dve.tensor_copy(identb[:, :], ident[:, :])
            weights = ((wgu_f[:, 0].rearrange("p c i -> p (c i)"), wgu[:, 0].rearrange("p c i -> p (c i)")),
                       (wgu_f[:, 1].rearrange("p c i -> p (c i)"), wgu[:, 1].rearrange("p c i -> p (c i)")),
                       (wd_f[:, :, :].rearrange("p c i -> p (c i)"), wd[:, :, :].rearrange("p c i -> p (c i)")))
            for m, (w, _) in enumerate(weights):
                last = dve.tensor_reduce(wsum[:, m:m + 1], w, AX.X, ALU.add, apply_absolute_value=True)
            last.then_inc(wsum_ready, 1)
            dve.wait_ge(wtotal_made, 1)
            link(dve.tensor_scalar(wmean[:, :], pd[:, 0:3], 1.0 / (I * D), FLOOR, ALU.mult, ALU.max))
            dve.tensor_scalar(wm127[:, :], wmean[:, :], 1.0 / 127.0, None, ALU.mult)
            link(dve.reciprocal(wscale[:, :], wmean[:, :]))
            for m, (w, _) in enumerate(weights):
                last = dve.tensor_scalar(w, w, wscale[:, m:m + 1], ROUND, ALU.mult, ALU.add)
            link(last)
            for m, (w, _) in enumerate(weights):
                last = dve.tensor_scalar(w, w, ROUND, 1.0, ALU.subtract, ALU.min)
            link(last)
            for w, q in weights:
                last = dve.tensor_scalar(q, w, -1.0, None, ALU.max)
            link(last)
            dve.sem_inc(setup_done, 2)
            dve.sem_inc(h_ready, 1)
            quantize_x(0, 0)
            quantize_x(0, 1)

            def tile(before, this, nxt, after):
                hidden(*this)
                if after is not None:
                    quantize_x(*after)
                if before is not None:
                    residual(*before)
                quantize_h(*this)
                if before is not None:
                    finish(*before)

            tiles(dve, tile, link)
            residual(*last_tile)
            finish(*last_tile)


STAGES = 6


def decoder(nc, a, out):
    scratch = [nc.dram_tensor(f"act{n}", [B, S, D], fp32, kind="Internal").ap() for n in range(6)]
    acts = [a["x"], *scratch][:STAGES] + [out]
    linear_attention(nc, acts[0], acts[1], a["L0_attn_WqT"], a["L0_attn_bq"], a["L0_attn_WkvT"], a["L0_attn_bkv"],
                     a["L0_attn_WoT"], a["L0_attn_bo"], a["ident"], a["head_blocks"])
    if STAGES > 1:
        cross_attention(nc, "xa0", acts[1], acts[2], a["ctx"], a["L0_xattn_wq"], a["L0_xattn_wkv"], a["L0_xattn_wproj"],
                        a["L0_xattn_bproj"], a["ident"], a["head_columns"], mask_d=a["mask"],
                        norms_d=[a["L0_xattn_" + n] for n in ("g_x", "b_x", "g_kv", "b_kv")])
    if STAGES > 2:
        expert_attention(nc, acts[2], acts[3], a["L0_ffn_Wg"], a["L0_ffn_Wq"], a["L0_ffn_Wkv"], a["L0_ffn_Wo"], a["L0_ffn_bqkv"],
                         a["L0_ffn_bo"], a["L0_ffn_ln"], a["ident"], a["batch_iota"], a["position_mask"], a["sum4"], a["pick4"])
    if STAGES > 3:
        ct_dram = nc.dram_tensor("ma_ct_dram", [2, 17, 2 * S], fp32, kind="Internal").ap()
        mamba(nc, acts[3], acts[4], ct_dram, a["L1_attn_g"], a["L1_attn_WinT"], a["L1_attn_WoutT"], a["L1_attn_conv"],
              a["L1_attn_WxT"], a["L1_attn_dtp"], a["L1_attn_Alog"], a["ident"])
    if STAGES > 4:
        cross_attention(nc, "xa1", acts[4], acts[5], a["ctx"], a["L1_xattn_WqT"], a["L1_xattn_WkvT"], a["L1_xattn_WoT"],
                        a["L1_xattn_bo"], a["ident"], a["head_columns"],
                        bq_d=a["L1_xattn_bq"], bk_d=a["L1_xattn_bk"], bv_d=a["L1_xattn_bv"])
    if STAGES > 5:
        bit_ffn(nc, acts[5], acts[6], a["L1_ffn_wguT"], a["L1_ffn_wdT"], a["ident"])


def kernel(**inputs):
    import numpy as _np
    import concourse.bacc as _bacc
    from concourse import mybir as _mybir
    from concourse.bass_utils import run_bass_kernel_spmd as _run

    def columns(v):
        return v.reshape(-1, P).T

    src = {name: _np.asarray(a) for name, a in inputs.items()}
    lay = {"x": src["x"]}
    lay["L0_attn_WqT"] = src["L0_attn_Wq"].T
    lay["L0_attn_bq"] = columns(src["L0_attn_bq"])
    lay["L0_attn_WkvT"] = _np.concatenate([src["L0_attn_Wk"].T, src["L0_attn_Wv"].T], axis=1)
    lay["L0_attn_bkv"] = _np.concatenate([src["L0_attn_bk"], src["L0_attn_bv"]])
    lay["L0_attn_WoT"] = src["L0_attn_Wo"].T
    lay["L0_attn_bo"] = src["L0_attn_bo"]
    lay["ctx"] = src["ctx_1024"]
    lay["mask"] = src["mask_BxS2_ik0"]
    lay["L0_xattn_wq"], lay["L0_xattn_wkv"], lay["L0_xattn_wproj"] = src["L0_xattn_w_q"], src["L0_xattn_w_kv"], src["L0_xattn_w_proj"]
    lay["L0_xattn_bproj"] = src["L0_xattn_b_proj"]
    for n in ("g_x", "b_x", "g_kv", "b_kv"):
        lay["L0_xattn_" + n] = columns(src["L0_xattn_" + n])
    lay["L1_xattn_WqT"] = src["L1_xattn_Wq"].T
    lay["L1_xattn_WkvT"] = _np.concatenate([src["L1_xattn_Wk"].T, src["L1_xattn_Wv"].T], axis=1)
    lay["L1_xattn_WoT"] = src["L1_xattn_Wo"].T
    lay["L1_xattn_bq"], lay["L1_xattn_bk"] = columns(src["L1_xattn_bq"]), columns(src["L1_xattn_bk"])
    lay["L1_xattn_bv"], lay["L1_xattn_bo"] = src["L1_xattn_bv"], src["L1_xattn_bo"]
    for n in ("Wg", "Wq", "Wkv", "Wo"):
        lay["L0_ffn_" + n] = src["L0_ffn_" + n]
    bqkv = _np.zeros((H, P, 2), _np.float32)
    bqkv[:, :, 0] = src["L0_ffn_bkv"]
    bqkv[:, 0:64, 1] = src["L0_ffn_bq"]
    lay["L0_ffn_bqkv"] = bqkv
    lay["L0_ffn_bo"] = columns(src["L0_ffn_bo"])
    lay["L0_ffn_ln"] = _np.stack([src["L0_ffn_ln_g"], src["L0_ffn_ln_b"]])
    lay["L1_attn_g"] = columns(src["L1_attn_g"])
    lay["L1_attn_WinT"], lay["L1_attn_WoutT"], lay["L1_attn_WxT"] = src["L1_attn_W_in"].T, src["L1_attn_W_out"].T, src["L1_attn_W_x"].T
    lay["L1_attn_conv"] = _np.concatenate([src["L1_attn_conv_w"], src["L1_attn_conv_b"][:, None]], 1).reshape(-1, P, 5).transpose(1, 0, 2)
    lay["L1_attn_dtp"] = _np.stack([columns(v) for v in (src["L1_attn_W_dt"][:, 0], src["L1_attn_b_dt"], src["L1_attn_D"])], axis=1)
    lay["L1_attn_Alog"] = src["L1_attn_A_log"].reshape(-1, P, src["L1_attn_A_log"].shape[1]).transpose(1, 0, 2)
    lay["L1_ffn_wguT"] = _np.stack([src["L1_ffn_w_gate"].T, src["L1_ffn_w_up"].T])
    lay["L1_ffn_wdT"] = src["L1_ffn_w_down"].T
    lay["ident"] = _np.eye(P, dtype=_np.float32)
    lay["batch_iota"] = _np.tile(_np.arange(B, dtype=_np.float32), (P, 1))
    lay["position_mask"] = _np.kron(_np.eye(P // B), _np.ones((B, 1))).astype(_np.float32)
    lay["sum4"] = _np.tile(_np.eye(4, P, dtype=_np.float32), (64, 1, 1))
    lay["pick4"] = _np.repeat(_np.eye(4, dtype=_np.float32)[:, :, None], P, axis=2)
    lay["head_columns"] = _np.kron(_np.eye(P // DH), _np.ones((DH, 1))).astype(_np.float32)
    lay["head_blocks"] = _np.kron(_np.eye(P // DH), _np.ones((DH, DH))).astype(_np.float32)

    nc = _bacc.Bacc("TRN2", target_bir_lowering=False, num_devices=1)
    arrays, args = {}, {}
    for name, a in lay.items():
        arrays[f"in_{name}"] = a = _np.ascontiguousarray(a)
        args[name] = nc.dram_tensor(f"in_{name}", a.shape, _mybir.dt.from_np(a.dtype), kind="ExternalInput").ap()
    out = nc.dram_tensor("out_0_dram", (B, S, D), _mybir.dt.float32, kind="ExternalOutput").ap()
    decoder(nc, args, out)
    r = _run(nc, [arrays], core_ids=[0])
    return r.results[0]["out_0_dram"]
```

```python
import concourse.bass as bass
from concourse import mybir
from contextlib import ExitStack

fp32 = mybir.dt.float32
bf16 = mybir.dt.bfloat16
i32 = mybir.dt.int32
ALU = mybir.AluOpType
ACT = mybir.ActivationFunctionType
AX = mybir.AxisListType

P = 128
B = 32
S = 256
D = 256
T = S // P
C = D // P
H = 16
DH = D // H
CTX = 77
PAIRS = B // 2
LN_EPS = 1e-5


class Stage:

    def __init__(self, nc, name):
        self.nc, self.name, self.ctx = nc, name, ExitStack()

    def __enter__(self):
        self.ctx.__enter__()
        self.ctx.enter_context(self.nc.cleanup_on_exit())
        return self

    def __exit__(self, *e):
        return self.ctx.__exit__(*e)

    def sb(self, name, shape, dt=fp32):
        return self.ctx.enter_context(self.nc.sbuf_tensor(f"{self.name}_{name}", shape, dt))

    def ps(self, name, shape, dt=fp32):
        return self.ctx.enter_context(self.nc.psum_tensor(f"{self.name}_{name}", shape, dt))

    def sem(self, name):
        return self.nc.alloc_semaphore(name=f"{self.name}_{name}")

    def block(self):
        return self.ctx.enter_context(self.nc.Block())


class Chain:

    def __init__(self, eng, sem, per_turn):
        self.eng, self.sem, self.per_turn, self.done, self.turn = eng, sem, per_turn, 0, None

    def begin(self, turn):
        assert self.turn is None
        self.base, self.turn, self.n = self.done, turn, 0

    def end(self, turns):
        assert self.n == self.per_turn, (self.n, self.per_turn)
        self.done, self.turn = self.base + turns * self.per_turn, None

    def __call__(self, ins):
        ins.then_inc(self.sem, 1)
        if self.turn is None:
            self.done += 1
            self.eng.wait_ge(self.sem, self.done)
        else:
            self.n += 1
            self.eng.wait_ge(self.sem, self.turn * self.per_turn + (self.base + self.n))


def in_turns(eng, step, turns, per, around, link=None):

    def peeled(turn, k):
        places = [per * turn + k + d for d in around]
        return [divmod(n, per) if 0 <= n < per * turns else None for n in places]

    for k in range(per):
        step(*peeled(0, k))
    if link:
        link.begin(0)
    with eng.Fori(0, turns - 2) as j:
        if link:
            link.turn = j
        for k in range(per):
            step(*((j, k + d + per) if k + d < 0 else (j + 1, k + d) if k + d < per else (j + 2, k + d - per) for d in around))
    if link:
        link.end(turns - 2)
    for k in range(per):
        step(*peeled(turns - 1, k))


def batch_tiles(x, b):
    return x[b].rearrange("(t p) d -> p t d", p=P)


def split_in_three(link, row, rest, parts, pick, out):
    v = link.eng
    for k in range(3):
        link(v.tensor_copy(parts[:, k, :], row[:, :] if k == 0 else rest[:, :]))
        if k < 2:
            link(v.tensor_tensor(rest[:, :], row[:, :] if k == 0 else rest[:, :], parts[:, k, :], ALU.subtract))
    link(v.tensor_scalar(rest[:, :], parts[:, 0, :], pick[:, 0:1], None, ALU.mult))
    for k in (1, 2):
        link(v.scalar_tensor_tensor(out=rest[:, :] if k == 1 else out[:, :], in0=parts[:, k, :],
                                    scalar=pick[:, k:k + 1], in1=rest[:, :], op0=ALU.mult, op1=ALU.add))


def linear_attention(nc, x_in, x_out, wqT, bq, wkvT, bkv, woT, bo, ident_d, blocks_d):
    with Stage(nc, "la") as st:
        sb, ps, sem = st.sb, st.ps, st.sem
        ident = sb("ident", [P, P])
        blocks = sb("blocks", [P, P])
        wq = sb("wq", [P, C, D])
        wkv = sb("wkv", [P, C, 2 * D])
        wo = sb("wo", [P, C, D])
        bq_c = sb("bq_c", [P, C])
        bias3 = sb("bias3", [3, 3 * D])
        rest3 = sb("rest3", [3, 3 * D])
        parts3 = sb("parts3", [3, 3, 3 * D], bf16)
        biasr = sb("biasr", [3, 3 * D], bf16)
        ones3 = sb("ones3", [3, P], bf16)
        minus_half = sb("minus_half", [P, T])
        eps = sb("eps", [P, T])
        spacer = sb("spacer", [P, 1])
        x = sb("x", [P, 4, T, D])
        xT = sb("xT", [P, 2, C, S])
        eq = sb("eq", [P, 2, C, S])
        rq = sb("rq", [P, 2, C, S])
        qT = sb("qT", [P, 2, C, S])
        ek = sb("ek", [P, 2, T, D])
        rk = sb("rk", [P, 2, T, D])
        k = sb("k", [P, 2, T, D])
        v = sb("v", [P, 2, T, D])
        kv = sb("kv", [P, 2, C, P])
        oT = sb("oT", [P, 2, C, S])
        r = sb("r", [P, 2, T, D])
        stats = sb("stats", [P, 2, T, 6])
        mv = sb("mv", [P, 2, T, 2])
        veps = sb("veps", [P, 2, T])
        rstd = sb("rstd", [P, 2, T])
        y = sb("y", [P, 2, T, D])
        pA = [ps(f"pA{p}", [P, C, S]) for p in range(2)]
        pB = [ps(f"pB{p}", [P, C, S]) for p in range(2)]
        pC = [ps(f"pC{p}", [P, T, 2 * D]) for p in range(2)]

        w_loaded, setup_done = sem("w_loaded"), sem("setup_done")
        x_loaded = [sem(f"x_loaded{b}") for b in range(4)]
        y_stored = [sem(f"y_stored{p}") for p in range(2)]
        xT_made, xT_copied = sem("xT_made"), sem("xT_copied")
        q_made, kv_made = sem("q_made"), sem("kv_made")
        exp_done, v_copied, qk_ready = sem("exp_done"), sem("v_copied"), sem("qk_ready")
        outer_made, outer_masked = sem("outer_made"), sem("outer_masked")
        oT_made, oT_copied = sem("oT_made"), sem("oT_copied")
        proj_made, pB_free = sem("proj_made"), sem("pB_free")
        var_ready, rstd_ready, y_ready = sem("var_ready"), sem("rstd_ready"), sem("y_ready")
        dve_chain, pool_chain = sem("dve_chain"), sem("pool_chain")
        block = st.block()

        @block.sync
        def _(sp):
            for dst, src in ((ident[:, :], ident_d), (blocks[:, :], blocks_d),
                             (wq[:, :, :], wqT.rearrange("(c p) f -> p c f", p=P)),
                             (wkv[:, :, :], wkvT.rearrange("(c p) f -> p c f", p=P)),
                             (wo[:, :, :], woT.rearrange("(c p) f -> p c f", p=P)),
                             (bq_c[:, :], bq),
                             (bias3[:, 0:2 * D], bkv.partition_broadcast(3)),
                             (bias3[:, 2 * D:3 * D], bo.partition_broadcast(3))):
                sp.dma_start(dst, src).then_inc(w_loaded, 16)
            for b in range(4):
                sp.dma_start(x[:, b], batch_tiles(x_in, b)).then_inc(x_loaded[b], 16)
            for p in range(2):
                sp.sem_inc(y_stored[p], 16)

            def store(j, q, p):
                sp.wait_ge(y_ready, 4 * j + (2 * q + p + 1))
                sp.dma_start(batch_tiles(x_out, 4 * j + (2 * q + p)), y[:, p]).then_inc(y_stored[p], 16)

            with sp.Fori(0, B // 4 - 1) as j:
                for q in range(2):
                    for p in range(2):
                        store(j, q, p)
                        sp.dma_start(x[:, 2 * q + p], batch_tiles(x_in, 4 * j + (2 * q + p + 4))).then_inc(x_loaded[2 * q + p], 16)
            for q in range(2):
                for p in range(2):
                    store(B // 4 - 1, q, p)
            for p in range(2):
                sp.wait_ge(y_stored[p], 16 * (B // 2 + 1))

        @block.tensor
        def _(pe):
            def pair(j, q):
                for p in range(2):
                    pe.wait_ge(x_loaded[2 * q + p], 16 * j + 16)
                    for c in range(C):
                        for t in range(T):
                            last = pe.transpose(pA[p][:, c, t * P:(t + 1) * P],
                                                x[:, 2 * q + p, t, c * P:(c + 1) * P], ident[:, :])
                    last.then_inc(xT_made, 1)
                for p in range(2):
                    n = 4 * j + (2 * q + p + 1)
                    pe.wait_ge(xT_copied, n)
                    pe.wait_ge(pB_free, n)
                    for f in range(C):
                        for c in range(C):
                            last = pe.matmul(pB[p][:, f, :], wq[:, c, f * P:(f + 1) * P], xT[:, p, c, :],
                                             start=(c == 0), stop=(c == C - 1))
                    last.then_inc(q_made, 1)
                    for t in range(T):
                        pe.matmul(pC[p][:, t, :], ones3[:, :], biasr[:, 0:2 * D], start=True, stop=False)
                        for c in range(C):
                            last = pe.matmul(pC[p][:, t, :], xT[:, p, c, t * P:(t + 1) * P], wkv[:, c, :],
                                             start=False, stop=(c == C - 1))
                    last.then_inc(kv_made, 1)
                for p in range(2):
                    n = 4 * j + (2 * q + p + 1)
                    pe.wait_ge(v_copied, n)
                    pe.wait_ge(qk_ready, n)
                    for c in range(C):
                        for t in range(T):
                            last = pe.matmul(pA[p][:, c, 0:P], k[:, p, t, c * P:(c + 1) * P],
                                             v[:, p, t, c * P:(c + 1) * P], start=(t == 0), stop=(t == T - 1))
                    last.then_inc(outer_made, 1)
                for p in range(2):
                    pe.wait_ge(outer_masked, 4 * j + (2 * q + p + 1))
                    for c in range(C):
                        last = pe.matmul(pC[p][:, 0, c * S:(c + 1) * S], kv[:, p, c, :], qT[:, p, c, :],
                                         start=True, stop=True)
                    last.then_inc(oT_made, 1)
                for p in range(2):
                    pe.wait_ge(oT_copied, 4 * j + (2 * q + p + 1))
                    for t in range(T):
                        pe.matmul(pB[p][:, t, :], ones3[:, :], biasr[:, 2 * D:3 * D], start=True, stop=False)
                        for c in range(C):
                            last = pe.matmul(pB[p][:, t, :], oT[:, p, c, t * P:(t + 1) * P], wo[:, c, :],
                                             start=False, stop=(c == C - 1))
                    last.then_inc(proj_made, 1)

            pe.wait_ge(w_loaded, 16 * 8)
            pe.wait_ge(setup_done, 1)
            with pe.Fori(0, B // 4) as j:
                for q in range(2):
                    pair(j, q)

        @block.scalar
        def _(act):
            def pair(j, q):
                for p in range(2):
                    act.wait_ge(xT_made, 4 * j + (2 * q + p + 1))
                    act.activation(xT[:, p], pA[p][:, :, :], ACT.Copy).then_inc(xT_copied, 1)
                for p in range(2):
                    n = 4 * j + (2 * q + p + 1)
                    act.wait_ge(q_made, n)
                    for f in range(C):
                        last = act.activation(eq[:, p, f, :], pB[p][:, f, :], ACT.Exp, bias=bq_c[:, f:f + 1])
                    last.then_inc(exp_done, 1)
                    act.wait_ge(kv_made, n)
                    act.activation(ek[:, p], pC[p][:, :, 0:D], ACT.Exp)
                    act.activation(v[:, p], pC[p][:, :, D:2 * D], ACT.Copy).then_inc(v_copied, 1)
                for p in range(2):
                    act.wait_ge(oT_made, 4 * j + (2 * q + p + 1))
                    act.activation(oT[:, p], pC[p][:, 0, :].rearrange("p (c s) -> p c s", c=C),
                                   ACT.Copy).then_inc(oT_copied, 1)

            act.wait_ge(w_loaded, 16 * 8)
            with act.Fori(0, B // 4) as j:
                for q in range(2):
                    pair(j, q)

        @block.gpsimd
        def _(pool):
            link = Chain(pool, pool_chain, 4)
            pool.memset(eps[:, :], LN_EPS)
            link(pool.memset(minus_half[:, :], -0.5))
            link.begin(0)
            with pool.Fori(0, B // 4) as j:
                link.turn = j
                for b in range(4):
                    pool.wait_ge(var_ready, 4 * j + (b + 1))
                    link(pool.tensor_tensor(veps[:, b % 2], mv[:, b % 2, :, 1], eps[:, :], ALU.add))
                    pool.tensor_tensor(rstd[:, b % 2], veps[:, b % 2], minus_half[:, :], ALU.pow).then_inc(rstd_ready, 1)
            link.end(B // 4)

        @block.vector
        def _(dve):
            def pair(j, q):
                for p in range(2):
                    n = 4 * j + (2 * q + p + 1)
                    dve.wait_ge(exp_done, n)
                    for f in range(C):
                        dve.tensor_scalar(rq[:, p, f, :], pB[p][:, f, :], bq_c[:, f:f + 1], 0.0, ALU.add, ALU.max)
                    dve.wait_ge(v_copied, n)
                    link(dve.tensor_scalar(rk[:, p], pC[p][:, :, 0:D], 0.0, None, ALU.max))
                    dve.scalar_tensor_tensor(out=qT[:, p], in0=eq[:, p], scalar=1.0, in1=rq[:, p],
                                             op0=ALU.min, op1=ALU.add)
                    dve.scalar_tensor_tensor(out=k[:, p], in0=ek[:, p], scalar=1.0, in1=rk[:, p],
                                             op0=ALU.min, op1=ALU.add).then_inc(qk_ready, 1)
                for p in range(2):
                    dve.wait_ge(outer_made, 4 * j + (2 * q + p + 1))
                    dve.tensor_tensor(kv[:, p], pA[p][:, :, 0:P], blocks[:, :].unsqueeze(1).broadcast_to([P, C, P]),
                                      ALU.mult).then_inc(outer_masked, 1)
                for p in range(2):
                    dve.wait_ge(proj_made, 4 * j + (2 * q + p + 1))
                    link(dve.tensor_tensor(r[:, p], pB[p][:, :, :], x[:, 2 * q + p], ALU.add))
                    dve.sem_inc(pB_free, 1)
                    for t in range(T):
                        last = dve.bn_stats(stats[:, p, t, :], r[:, p, t, :])
                    link(last)
                    dve.memset(spacer[:, :], 0.0)
                    for t in range(T):
                        last = dve.bn_aggr(mv[:, p, t, :], stats[:, p, t, :])
                    last.then_inc(var_ready, 1)
                for p in range(2):
                    dve.wait_ge(rstd_ready, 4 * j + (2 * q + p + 1))
                    dve.wait_ge(y_stored[p], 32 * j + 16 * (q + 1))
                    for t in range(T):
                        last = dve.tensor_scalar(y[:, p, t, :], r[:, p, t, :], mv[:, p, t, 0:1], rstd[:, p, t:t + 1],
                                                 ALU.subtract, ALU.mult)
                    last.then_inc(y_ready, 1)

            link = Chain(dve, dve_chain, 3 * 4)
            dve.wait_ge(w_loaded, 16 * 8)
            dve.memset(ones3[:, :], 1.0)
            split_in_three(link, bias3, rest3, parts3, ident[0:3, 0:3], biasr)
            dve.sem_inc(setup_done, 1)
            dve.sem_inc(pB_free, 2)
            link.begin(0)
            with dve.Fori(0, B // 4) as j:
                link.turn = j
                for q in range(2):
                    pair(j, q)
            link.end(B // 4)


def cross_attention(nc, name, x_in, x_out, ctx_d, wq_d, wkv_d, wo_d, bo_d, ident_d, heads_d,
                    bq_d=None, bk_d=None, bv_d=None, mask_d=None, norms_d=None):
    normed, masked = norms_d is not None, mask_d is not None
    HC = H // C
    HB = HC // 2
    W = 2 * DH
    with Stage(nc, name) as st:
        sb, ps, sem = st.sb, st.ps, st.sem
        ident = sb("ident", [P, P])
        head_of = sb("head_of", [P, HB])
        wq = sb("wq", [P, C, D])
        wkv = sb("wkv", [P, C, 2 * D])
        wo = sb("wo", [P, C, D])
        bqk = sb("bqk", [P, 2, C])
        bq4 = sb("bq4", [P, C])
        norms = sb("norms", [P, 4, C])
        bias3 = sb("bias3", [3, 2 * D])
        rest3 = sb("rest3", [3, 2 * D])
        parts3 = sb("parts3", [3, 3, 2 * D], bf16)
        biasr = sb("biasr", [3, 2 * D], bf16)
        pick = sb("pick", [P, 3])
        fill = sb("fill", [P, 1])
        fill_rest = sb("fill_rest", [P, 1])
        fill_parts = sb("fill_parts", [P, 3, 1], bf16)
        fillr = sb("fillr", [P, 1])
        ones = sb("ones", [P, P], bf16)
        spacer = sb("spacer", [P, 1])
        eps = sb("eps", [P, 3])
        minus_half = sb("minus_half", [P, 3])
        x = sb("x", [P, 4, T, D])
        cx = sb("cx", [CTX, 2, D])
        mask_i = sb("mask_i", [P, 2, CTX], i32)
        seen = sb("seen", [P, 2, CTX])
        fill_row = sb("fill_row", [P, 2, CTX], bf16)
        n_stats = sb("n_stats", [P, 2, 3, 6])
        n_mv = sb("n_mv", [P, 2, 3, 2])
        n_veps = sb("n_veps", [P, 2, 3])
        n_rstd = sb("n_rstd", [P, 2, 3])
        xn = sb("xn", [P, 2, T, D])
        cn = sb("cn", [CTX, 2, D])
        xT = sb("xT", [P, 2, C, S])
        cT = sb("cT", [P, 2, C, CTX])
        qT = sb("qT", [P, 2, C, S])
        kT = sb("kT", [P, 2, C, CTX])
        kheads = sb("kheads", [P, 2, C, HB * CTX])
        v = sb("v", [CTX, 2, H, W])
        top = sb("top", [P, 2, HC])
        low = sb("low", [P, 2, HC * CTX])
        e = sb("e", [P, 2, HC * CTX])
        esum = sb("esum", [P, 2, HC])
        rec = sb("rec", [P, 2, HC])
        prob = sb("prob", [P, 2, HC * CTX])
        eT = sb("eT", [CTX, C, HC, T, P])
        oT = sb("oT", [P, 2, C, S])
        r = sb("r", [P, 2, T, D])
        stats = sb("stats", [P, 2, T, 6])
        mv = sb("mv", [P, 2, T, 2])
        veps = sb("veps", [P, 2, T])
        rstd = sb("rstd", [P, 2, T])
        y = sb("y", [P, 2, T, D])
        pS = [ps(f"pS{k}", [P, 2, 512]) for k in range(2)]
        pE = [ps(f"pE{h}", [CTX, HB, P]) for h in range(2)]
        pG = [ps(f"pG{g}", [P, 512]) for g in range(2)]

        w_loaded, setup_done = sem("w_loaded"), sem("setup_done")
        x_loaded = [sem(f"x_loaded{b}") for b in range(4)]
        c_loaded = [sem(f"c_loaded{p}") for p in range(2)]
        y_stored = [sem(f"y_stored{p}") for p in range(2)]
        n_var, n_rstd_ready, n_ready = sem("n_var"), sem("n_rstd_ready"), sem("n_ready")
        xT_made, xT_copied, cT_made, cT_copied = sem("xT_made"), sem("xT_copied"), sem("cT_made"), sem("cT_copied")
        q_made, q_copied, k_made, k_copied = sem("q_made"), sem("q_copied"), sem("k_made"), sem("k_copied")
        v_made, v_copied, kheads_ready = sem("v_made"), sem("v_copied"), sem("kheads_ready")
        scores_made, low_ready = sem("scores_made"), sem("low_ready")
        e_ready, prob_ready, eT_made, eT_copied = sem("e_ready"), sem("prob_ready"), sem("eT_made"), sem("eT_copied")
        rec_ready = sem("rec_ready")
        oT_made, oT_copied, proj_made, res_added = sem("oT_made"), sem("oT_copied"), sem("proj_made"), sem("res_added")
        var_ready, rstd_ready, y_ready = sem("var_ready"), sem("rstd_ready"), sem("y_ready")
        dve_chain, pool_chain = sem("dve_chain"), sem("pool_chain")
        bq4_ready = sem("bq4_ready")
        block = st.block()
        ctx_used = n_ready if normed else cT_made
        U = T * C

        loads = [(ident[:, :], ident_d), (head_of[:, :], heads_d),
                 (wq[:, :, :], wq_d.rearrange("(c p) f -> p c f", p=P)),
                 (wkv[:, :, :], wkv_d.rearrange("(c p) f -> p c f", p=P)),
                 (wo[:, :, :], wo_d.rearrange("(c p) f -> p c f", p=P)),
                 (bias3[:, D:2 * D], bo_d.partition_broadcast(3))]
        if bq_d is not None:
            loads += [(bqk[:, 0, :], bq_d), (bqk[:, 1, :], bk_d), (bias3[:, 0:D], bv_d.partition_broadcast(3))]
        if normed:
            loads += [(norms[:, n, :], d) for n, d in enumerate(norms_d)]

        def batches(eng, batch, link=None):
            in_turns(eng, batch, B // 4, 4, (0, 1, -1), link)

        def unit_number(j, b, u):
            return (4 * U) * j + (U * b + u)

        last_batch = (B // 4 - 1, 3)

        @block.sync
        def _(sp):
            for dst, src in loads:
                sp.dma_start(dst, src).then_inc(w_loaded, 16)

            def load_x(b, at):
                sp.dma_start(x[:, b], batch_tiles(x_in, at)).then_inc(x_loaded[b], 16)

            def load_ctx(p, at):
                sp.dma_start(cx[:, p], ctx_d[at]).then_inc(c_loaded[p], 16)
                if masked:
                    sp.dma_start(mask_i[:, p], mask_d[at].partition_broadcast(P)).then_inc(c_loaded[p], 16)

            for b in range(4):
                load_x(b, b)
            for p in range(2):
                load_ctx(p, p)
                sp.sem_inc(y_stored[p], 16)

            def store(j, b):
                p = b % 2
                sp.wait_ge(y_ready, 4 * j + (b + 1))
                sp.dma_start(batch_tiles(x_out, 4 * j + b), y[:, p]).then_inc(y_stored[p], 16)

            with sp.Fori(0, B // 4 - 1) as j:
                for b in range(4):
                    sp.wait_ge(ctx_used, 4 * j + (b + 1))
                    load_ctx(b % 2, 4 * j + (b + 2))
                    store(j, b)
                    load_x(b, 4 * j + (b + 4))
            for b in range(4):
                if b < 2:
                    sp.wait_ge(ctx_used, B - 3 + b)
                    load_ctx(b % 2, B - 2 + b)
                store(B // 4 - 1, b)
            for p in range(2):
                sp.wait_ge(y_stored[p], 16 * (B // 2 + 1))

        @block.tensor
        def _(pe):
            def front(j, b):
                p, n = b % 2, 4 * j + (b + 1)
                if normed:
                    pe.wait_ge(n_ready, n)
                else:
                    pe.wait_ge(x_loaded[b], 16 * j + 16)
                for c in range(C):
                    for t in range(T):
                        src = xn[:, p, t, c * P:(c + 1) * P] if normed else x[:, b, t, c * P:(c + 1) * P]
                        last = pe.transpose(pG[0][:, (c * T + t) * P:(c * T + t + 1) * P], src, ident[:, :])
                last.then_inc(xT_made, 1)
                if not normed:
                    pe.wait_ge(c_loaded[p], 32 * j + 16 * (b // 2 + 1))
                for c in range(C):
                    src = cn[:, p, c * P:(c + 1) * P] if normed else cx[:, p, c * P:(c + 1) * P]
                    last = pe.transpose(pG[1][:, c * CTX:(c + 1) * CTX], src, ident[0:CTX, 0:CTX])
                last.then_inc(cT_made, 1)

            def project(j, b):
                p, n = b % 2, 4 * j + (b + 1)
                pe.wait_ge(xT_copied, n)
                for f in range(C):
                    for c in range(C):
                        last = pe.matmul(pG[0][:, f * S:(f + 1) * S], wq[:, c, f * P:(f + 1) * P], xT[:, p, c, :],
                                         start=(c == 0), stop=(c == C - 1))
                last.then_inc(q_made, 1)
                pe.wait_ge(cT_copied, n)
                for f in range(C):
                    for c in range(C):
                        last = pe.matmul(pG[1][:, f * CTX:(f + 1) * CTX], wkv[:, c, f * P:(f + 1) * P], cT[:, p, c, :],
                                         start=(c == 0), stop=(c == C - 1))
                last.then_inc(k_made, 1)
                pe.wait_ge(q_copied, n)
                if bv_d is not None:
                    pe.matmul(pG[0][0:CTX, 0:D], ones[0:3, 0:CTX], biasr[:, 0:D], start=True, stop=False)
                for c in range(C):
                    last = pe.matmul(pG[0][0:CTX, 0:D], cT[:, p, c, :], wkv[:, c, D:2 * D],
                                     start=(c == 0 and bv_d is None), stop=(c == C - 1))
                last.then_inc(v_made, 1)

            def scores(j, b, u):
                p, c, t = b % 2, u // T, u % T
                pe.wait_ge(low_ready, (4 * U) * j + (U * b + u + 1))
                for h in range(2):
                    rows = slice(h * P // 2, (h + 1) * P // 2)
                    if masked:
                        pe.matmul(pS[u % 2][:, h, 0:HB * CTX], ones[rows, :],
                                  fill_row[rows, p, :].unsqueeze(1).broadcast_to([P // 2, HB, CTX]), start=True, stop=False)
                    last = pe.matmul(pS[u % 2][:, h, 0:HB * CTX], qT[rows, p, c, t * P:(t + 1) * P], kheads[rows, p, c, :],
                                     start=not masked, stop=True)
                last.then_inc(scores_made, 1)

            def turn(j, b, u):
                pe.wait_ge(prob_ready, (4 * U) * j + (U * b + u + 1))
                for h in range(2):
                    pe.wait_ge(eT_copied, (8 * U) * j + (2 * (U * b + u) + h + 1))
                    for i in range(HB):
                        at = (h * HB + i) * CTX
                        last = pe.transpose(pE[h][:, i, :], prob[:, u % 2, at:at + CTX], ident[:, :])
                    last.then_inc(eT_made, 1)

            def values(j, b, c):
                pe.wait_ge(eT_copied, 2 * unit_number(j, b, T * c + T) + 2)
                out = pG[1 - c][:, 0:S]
                for h in range(HC):
                    at = (h // 2) * W
                    last = pe.matmul(out[at:at + W, :], v[:, b % 2, c * HC + h, :], eT[:, c, h, :, :].rearrange("s t p -> s (t p)"),
                                     start=(h % 2 == 0), stop=(h % 2 == 1))
                last.then_inc(oT_made, 1)

            def project_out(j, b):
                p = b % 2
                pe.wait_ge(oT_copied, (4 * C) * j + C * (b + 1))
                for t in range(T):
                    pe.matmul(pG[1][:, t * D:(t + 1) * D], ones[0:3, :], biasr[:, D:2 * D], start=True, stop=False)
                    for c in range(C):
                        last = pe.matmul(pG[1][:, t * D:(t + 1) * D], oT[:, p, c, t * P:(t + 1) * P], wo[:, c, :],
                                         start=False, stop=(c == C - 1))
                last.then_inc(proj_made, 1)

            def first_scores(j, b, u):
                if u == 0:
                    pe.wait_ge(kheads_ready, 4 * j + (b + 1))
                scores(j, b, u)

            def batch(this, nxt, before):
                j, b = this
                n = 4 * j + (b + 1)
                if before is not None:
                    project_out(*before)
                turn(j, b, 0)
                scores(j, b, 2)
                turn(j, b, 1)
                if nxt is not None:
                    pe.wait_ge(v_copied, n)
                    pe.wait_ge(res_added, n)
                    front(*nxt)
                scores(j, b, 3)
                if nxt is not None:
                    project(*nxt)
                    pe.wait_ge(k_copied, n + 1)
                else:
                    pe.wait_ge(res_added, n)
                    pe.wait_ge(k_copied, n)
                values(j, b, 0)
                if nxt is not None:
                    first_scores(*nxt, 0)
                turn(j, b, 2)
                turn(j, b, 3)
                if nxt is not None:
                    first_scores(*nxt, 1)
                    pe.wait_ge(v_copied, n + 1)
                else:
                    pe.wait_ge(v_copied, n)
                values(j, b, 1)

            pe.wait_ge(w_loaded, 16 * len(loads))
            pe.wait_ge(setup_done, 1)
            front(0, 0)
            project(0, 0)
            first_scores(0, 0, 0)
            first_scores(0, 0, 1)
            batches(pe, batch)
            project_out(*last_batch)

        @block.scalar
        def _(act):
            def front(j, b):
                p, n = b % 2, 4 * j + (b + 1)
                act.wait_ge(xT_made, n)
                for c in range(C):
                    last = act.activation(xT[:, p, c, :], pG[0][:, c * S:(c + 1) * S], ACT.Identity,
                                          **(dict(bias=norms[:, 1, c:c + 1], scale=norms[:, 0, c:c + 1]) if normed else {}))
                last.then_inc(xT_copied, 1)
                act.wait_ge(cT_made, n)
                for c in range(C):
                    last = act.activation(cT[:, p, c, :], pG[1][:, c * CTX:(c + 1) * CTX], ACT.Identity,
                                          **(dict(bias=norms[:, 3, c:c + 1], scale=norms[:, 2, c:c + 1]) if normed else {}))
                last.then_inc(cT_copied, 1)

            def copy_q(j, b):
                p, n = b % 2, 4 * j + (b + 1)
                act.wait_ge(q_made, n)
                for f in range(C):
                    last = act.activation(qT[:, p, f, :], pG[0][:, f * S:(f + 1) * S], ACT.Identity, scale=0.25,
                                          **(dict(bias=bq4[:, f:f + 1]) if bq_d is not None else {}))
                last.then_inc(q_copied, 1)

            def copy_k(j, b):
                p, n = b % 2, 4 * j + (b + 1)
                act.wait_ge(k_made, n)
                for f in range(C):
                    last = act.activation(kT[:, p, f, :], pG[1][:, f * CTX:(f + 1) * CTX], ACT.Identity,
                                          **(dict(bias=bqk[:, 1, f:f + 1]) if bk_d is not None else {}))
                last.then_inc(k_copied, 1)

            def copy_v(j, b):
                p, n = b % 2, 4 * j + (b + 1)
                act.wait_ge(v_made, n)
                for half in range(2):
                    last = act.activation(v[:, p, :, :].rearrange("s (i k) w -> s i k w", k=2)[:, :, half, half * DH:(half + 1) * DH],
                                          pG[0][0:CTX, 0:D].rearrange("s (i k e) -> s i k e", k=2, e=DH)[:, :, half, :], ACT.Copy)
                last.then_inc(v_copied, 1)

            def expo(j, b, u):
                m = unit_number(j, b, u)
                act.wait_ge(low_ready, m + 3)
                if not (type(m) is int and m < 2):
                    act.wait_ge(prob_ready, m - 1)
                act.activation(e[:, u % 2], low[:, u % 2], ACT.Exp).then_inc(e_ready, 1)

            def turned(j, b, u):
                for h in range(2):
                    act.wait_ge(eT_made, (8 * U) * j + (2 * (U * b + u) + h + 1))
                    act.activation(eT[:, u // T, h * HB:(h + 1) * HB, u % T, :], pE[h][:, :, :],
                                   ACT.Copy).then_inc(eT_copied, 1)

            def copy_out(j, b, c):
                act.wait_ge(oT_made, (4 * C) * j + (C * b + c + 1))
                act.activation(oT[:, b % 2, c, :], pG[1 - c][:, 0:S], ACT.Copy).then_inc(oT_copied, 1)

            def batch(this, nxt, before):
                j, b = this
                turned(j, b, 0)
                turned(j, b, 1)
                if nxt is not None:
                    front(*nxt)
                expo(j, b, 2)
                if nxt is not None:
                    copy_q(*nxt)
                    copy_k(*nxt)
                expo(j, b, 3)
                if nxt is not None:
                    copy_v(*nxt)
                copy_out(j, b, 0)
                turned(j, b, 2)
                if nxt is not None:
                    expo(*nxt, 0)
                turned(j, b, 3)
                copy_out(j, b, 1)
                if nxt is not None:
                    expo(*nxt, 1)

            act.wait_ge(w_loaded, 16 * len(loads))
            act.wait_ge(setup_done, 1)
            act.sem_inc(eT_copied, 2)
            if bq_d is not None:
                act.activation(bq4[:, :], bqk[:, 0, :], ACT.Copy, scale=0.25).then_inc(bq4_ready, 1)
                act.wait_ge(bq4_ready, 1)
            front(0, 0)
            copy_q(0, 0)
            copy_k(0, 0)
            copy_v(0, 0)
            expo(0, 0, 0)
            expo(0, 0, 1)
            batches(act, batch)

        @block.gpsimd
        def _(pool):
            def norm_scale(j, b):
                p = b % 2
                pool.wait_ge(n_var, 4 * j + (b + 1))
                link(pool.tensor_tensor(n_veps[:, p], n_mv[:, p, :, 1], eps[:, :], ALU.add))
                pool.tensor_tensor(n_rstd[:, p], n_veps[:, p], minus_half[:, :], ALU.pow).then_inc(n_rstd_ready, 1)

            def spread_k(j, b):
                p, n = b % 2, 4 * j + (b + 1)
                pool.wait_ge(k_copied, n)
                if masked:
                    link(pool.tensor_tensor(kT[:, p], kT[:, p], seen[:, p].unsqueeze(1).broadcast_to([P, C, CTX]), ALU.mult))
                for c in range(C):
                    last = pool.tensor_tensor(kheads[:, p, c, :].rearrange("p (h s) -> p h s", h=HB),
                                              kT[:, p, c, :].unsqueeze(1).broadcast_to([P, HB, CTX]),
                                              head_of[:, :].unsqueeze(2).broadcast_to([P, HB, CTX]), ALU.mult)
                last.then_inc(kheads_ready, 1)

            def divide(j, b, u):
                m = unit_number(j, b, u)
                pool.wait_ge(rec_ready, m + 1)
                if not (type(m) is int and m < 2):
                    pool.wait_ge(eT_made, 2 * m - 2)
                pool.tensor_tensor(prob[:, u % 2].rearrange("p (h s) -> p h s", h=HC), e[:, u % 2].rearrange("p (h s) -> p h s", h=HC),
                                   rec[:, u % 2].unsqueeze(2).broadcast_to([P, HC, CTX]), ALU.mult).then_inc(prob_ready, 1)

            def batch(this, nxt, before):
                divide(*this, 1)
                if nxt is not None and normed:
                    norm_scale(*nxt)
                if before is not None:
                    rstd_of(*before)
                divide(*this, 2)
                if nxt is not None:
                    spread_k(*nxt)
                divide(*this, 3)
                if nxt is not None:
                    divide(*nxt, 0)

            def rstd_of(j, b):
                p = b % 2
                pool.wait_ge(var_ready, 4 * j + (b + 1))
                link(pool.tensor_tensor(veps[:, p], mv[:, p, :, 1], eps[:, 0:T], ALU.add))
                pool.tensor_tensor(rstd[:, p], veps[:, p], minus_half[:, 0:T], ALU.pow).then_inc(rstd_ready, 1)

            link = Chain(pool, pool_chain, 4 * (1 + normed + masked))
            pool.memset(eps[:, :], LN_EPS)
            link(pool.memset(minus_half[:, :], -0.5))
            pool.wait_ge(w_loaded, 16 * len(loads))
            if normed:
                norm_scale(0, 0)
            spread_k(0, 0)
            divide(0, 0, 0)
            batches(pool, batch, link)
            rstd_of(*last_batch)

        @block.vector
        def _(dve):
            def norm_stats(j, b):
                p = b % 2
                dve.wait_ge(x_loaded[b], 16 * j + 16)
                for t in range(T):
                    dve.bn_stats(n_stats[:, p, t, :], x[:, b, t, :])
                dve.wait_ge(c_loaded[p], (2 * L) * j + L * (b // 2 + 1))
                link(dve.bn_stats(n_stats[0:CTX, p, T, :], cx[:, p, :]))
                dve.memset(spacer[:, :], 0.0)
                for t in range(T):
                    dve.bn_aggr(n_mv[:, p, t, :], n_stats[:, p, t, :])
                dve.bn_aggr(n_mv[0:CTX, p, T, :], n_stats[0:CTX, p, T, :]).then_inc(n_var, 1)
                if masked:
                    dve.tensor_scalar(seen[:, p, :], mask_i[:, p, :], 0.0, None, ALU.not_equal)
                    dve.tensor_scalar(fill_row[:, p, :], mask_i[:, p, :], 0.0, fillr[:, 0:1], ALU.is_equal, ALU.mult)

            def norm_apply(j, b):
                p = b % 2
                dve.wait_ge(n_rstd_ready, 4 * j + (b + 1))
                for t in range(T):
                    dve.tensor_scalar(xn[:, p, t, :], x[:, b, t, :], n_mv[:, p, t, 0:1], n_rstd[:, p, t:t + 1],
                                      ALU.subtract, ALU.mult)
                dve.tensor_scalar(cn[:, p, :], cx[:, p, :], n_mv[0:CTX, p, T, 0:1], n_rstd[0:CTX, p, T:T + 1],
                                  ALU.subtract, ALU.mult).then_inc(n_ready, 1)

            def unit(j, b, u):
                dve.wait_ge(scores_made, (4 * U) * j + (U * b + u + 1))
                s = pS[u % 2][:, :, 0:HB * CTX].rearrange("p g (h s) -> p g h s", h=HB)
                m = top[:, u % 2, :].rearrange("p (g h) -> p g h", g=2)
                link(dve.tensor_reduce(m, s, AX.X, ALU.max))
                dve.tensor_tensor(low[:, u % 2].rearrange("p (g h s) -> p g h s", g=2, h=HB), s,
                                  m.unsqueeze(3).broadcast_to([P, 2, HB, CTX]), ALU.subtract).then_inc(low_ready, 1)

            def sums(j, b, u):
                dve.wait_ge(e_ready, unit_number(j, b, u) + 1)
                link(dve.tensor_reduce(esum[:, u % 2, :], e[:, u % 2].rearrange("p (h s) -> p h s", h=HC), AX.X, ALU.add))
                dve.reciprocal(rec[:, u % 2, :], esum[:, u % 2, :]).then_inc(rec_ready, 1)

            def batch(this, nxt, before):
                sums(*this, 1)
                if nxt is not None and normed:
                    norm_stats(*nxt)
                if before is not None:
                    residual(*before)
                if nxt is not None and normed:
                    norm_apply(*nxt)
                if before is not None:
                    moments(*before)
                unit(*this, 2)
                sums(*this, 2)
                unit(*this, 3)
                sums(*this, 3)
                if before is not None:
                    finish(*before)
                if nxt is not None:
                    unit(*nxt, 0)
                    sums(*nxt, 0)
                    unit(*nxt, 1)

            def residual(j, b):
                p = b % 2
                dve.wait_ge(proj_made, 4 * j + (b + 1))
                link(dve.tensor_tensor(r[:, p], pG[1][:, :].rearrange("p (t d) -> p t d", t=T), x[:, b], ALU.add))
                dve.sem_inc(res_added, 1)

            def moments(j, b):
                p = b % 2
                for t in range(T):
                    last = dve.bn_stats(stats[:, p, t, :], r[:, p, t, :])
                link(last)
                dve.memset(spacer[:, :], 0.0)
                for t in range(T):
                    last = dve.bn_aggr(mv[:, p, t, :], stats[:, p, t, :])
                last.then_inc(var_ready, 1)

            def finish(j, b):
                p = b % 2
                dve.wait_ge(rstd_ready, 4 * j + (b + 1))
                dve.wait_ge(y_stored[p], 32 * j + 16 * (b // 2 + 1))
                for t in range(T):
                    last = dve.tensor_scalar(y[:, p, t, :], r[:, p, t, :], mv[:, p, t, 0:1], rstd[:, p, t:t + 1],
                                             ALU.subtract, ALU.mult)
                last.then_inc(y_ready, 1)

            L = 16 * (1 + masked)
            link = Chain(dve, dve_chain, 4 * (2 * U + 2 + normed))
            dve.wait_ge(w_loaded, 16 * len(loads))
            dve.memset(ones[:, :], 1.0)
            dve.memset(n_mv[:, :, :, :], 1.0)
            dve.memset(v[:, :, :, :], 0.0)
            if bv_d is None:
                link(dve.memset(bias3[:, 0:D], 0.0))
            split_in_three(link, bias3, rest3, parts3, ident[0:3, 0:3], biasr)
            if masked:
                dve.tensor_tensor(pick[:, :], ident[:, 0:3], ident[:, P // 2:P // 2 + 3], ALU.add)
                link(dve.memset(fill[:, :], -1e9))
                split_in_three(link, fill, fill_rest, fill_parts, pick, fillr)
            dve.sem_inc(setup_done, 1)
            dve.sem_inc(low_ready, 2)
            dve.sem_inc(res_added, 1)
            if normed:
                norm_stats(0, 0)
                norm_apply(0, 0)
            unit(0, 0, 0)
            sums(0, 0, 0)
            unit(0, 0, 1)
            batches(dve, batch, link)
            residual(*last_batch)
            moments(*last_batch)
            finish(*last_batch)


def expert_attention(nc, x_in, x_out, wg_d, wq_d, wkv_d, wo_d, bqkv_d, bo_d, ln_d, ident_d, iota_d, posmask_d,
                     sum4_d, pick4_d):
    E, F, SP, G8, NG = H, 64, 4, 8, 8
    NT = NG * G8
    SL = 2 * SP
    ES = NT * SL
    xg_in = x_in.rearrange("b (g t s) d -> g s b t d", g=NG, t=G8)
    xg_out = x_out.rearrange("b (g t s) d -> g s b t d", g=NG, t=G8)
    with Stage(nc, "ea") as outer:
        ident = outer.sb("ident", [P, P])
        xg = outer.sb("xg", [P, 2, G8, D])
        sel = outer.sb("sel", [P, NT, P])
        hg = outer.sb("hg", [P, C, E, ES])

        def load_group(sp, g, q, sem_):
            for s in range(SP):
                sp.dma_start(xg[s * B:(s + 1) * B, q], xg_in[g][s]).then_inc(sem_, 16)

        with Stage(nc, "route") as st:
            sb, ps, sem = st.sb, st.ps, st.sem
            wg = sb("wg", [P, C, E])
            iota = sb("iota", [P, B])
            iota64 = sb("iota64", [P, B])
            posmask = sb("posmask", [P, SP])
            hT = sb("hT", [P, 2, C, P])
            lg = sb("lg", [P, NT, E])
            pr = sb("pr", [P, NT, E])
            tmax = sb("tmax", [P, NT])
            tsum = sb("tsum", [P, NT])
            SG = NG * SP
            pT = sb("pT", [P, SG, B])
            eq = sb("eq", [P, SG, B])
            m = sb("m", [P, SG])
            i1 = sb("i1", [P, SG])
            i2 = sb("i2", [P, SG])
            lo_hi = sb("lo_hi", [P, 2, SG])
            hot = sb("hot", [P, 2, SG, B])
            ph = [ps(f"ph{q}", [P, C, P]) for q in range(2)]
            pl = [ps(f"pl{q}", [P, G8, E]) for q in range(2)]
            pt = [ps(f"pt{q}", [P, 4, P]) for q in range(4)]
            w_loaded = sem("w_loaded")
            x_loaded = [sem(f"x_loaded{q}") for q in range(2)]
            hT_made, hT_copied, lg_made, lg_copied = sem("hT_made"), sem("hT_copied"), sem("lg_made"), sem("lg_copied")
            low_ready, exp_done, pr_ready = sem("low_ready"), sem("exp_done"), sem("pr_ready")
            pT_made, hot_ready, hotT_made = sem("pT_made"), sem("hot_ready"), sem("hotT_made")
            chain, sel_ready = sem("chain"), sem("sel_ready")
            block = st.block()
            loads = [(ident[:, :], ident_d), (wg[:, :, :], wg_d.rearrange("(c p) e -> p c e", p=P)),
                     (iota[:, :], iota_d), (posmask[:, :], posmask_d)]

            @block.sync
            def _(sp):
                for dst, src in loads:
                    sp.dma_start(dst, src).then_inc(w_loaded, 16)
                for q in range(2):
                    load_group(sp, q, q, x_loaded[q])
                with sp.Fori(0, NG // 2 - 1) as j:
                    for q in range(2):
                        sp.wait_ge(lg_made, 2 * j + (q + 1))
                        load_group(sp, 2 * j + (q + 2), q, x_loaded[q])

            @block.tensor
            def _(pe):
                pe.wait_ge(w_loaded, 16 * len(loads))

                def turn(j, q, t):
                    if t == 0:
                        pe.wait_ge(x_loaded[q], 64 * j + 64)
                    pe.wait_ge(hT_copied, (2 * G8) * j + (G8 * q + t + 1))
                    for c in range(C):
                        last = pe.transpose(ph[t % 2][:, c, :], xg[:, q, t, c * P:(c + 1) * P], ident[:, :])
                    last.then_inc(hT_made, 1)

                def score(j, q, t):
                    if t == 0:
                        pe.wait_ge(lg_copied, 2 * j + (q + 1))
                    pe.wait_ge(hT_copied, (2 * G8) * j + (G8 * q + t + 3))
                    for c in range(C):
                        last = pe.matmul(pl[q][:, t, :], hT[:, t % 2, c, :], wg[:, c, :], start=(c == 0), stop=(c == C - 1))
                    if t == G8 - 1:
                        last.then_inc(lg_made, 1)

                with pe.Fori(0, NG // 2) as j:
                    for q in range(2):
                        turn(j, q, 0)
                        for t in range(G8):
                            if t + 1 < G8:
                                turn(j, q, t + 1)
                            score(j, q, t)
                pe.wait_ge(pr_ready, 1)
                for g in range(NG):
                    last = pe.transpose(pt[g // 4][:, g % 4, :], pr[:, g * G8:(g + 1) * G8, :].rearrange("p t e -> p (t e)"), ident[:, :])
                    if g % 4 == 3:
                        last.then_inc(pT_made, 1)
                pe.wait_ge(hot_ready, 1)
                for i in range(2):
                    for g in range(NG):
                        n = (i * NG + g) // 4
                        last = pe.transpose(pt[n][:, g % 4, :], hot[:, i, g * SP:(g + 1) * SP, :].rearrange("p s b -> p (s b)"), ident[:, :])
                        if g % 4 == 3:
                            last.then_inc(hotT_made, 1)

            @block.scalar
            def _(act):
                act.sem_inc(hT_copied, 2)
                with act.Fori(0, NG // 2) as j:
                    for q in range(2):
                        for t in range(G8):
                            act.wait_ge(hT_made, (2 * G8) * j + (G8 * q + t + 1))
                            act.activation(hT[:, t % 2], ph[t % 2][:, :, :], ACT.Copy).then_inc(hT_copied, 1)
                act.wait_ge(low_ready, 1)
                act.activation(pr[:, :, :], lg[:, :, :], ACT.Exp).then_inc(exp_done, 1)

            @block.vector
            def _(dve):
                link = Chain(dve, chain, 0)
                dve.wait_ge(w_loaded, 16 * len(loads))
                link(dve.tensor_scalar(iota64[:, :], iota[:, :], 64.0, None, ALU.add))
                dve.sem_inc(lg_copied, 2)
                with dve.Fori(0, NG // 2) as j:
                    for q in range(2):
                        dve.wait_ge(lg_made, 2 * j + (q + 1))
                        dve.tensor_copy(lg[:, bass.ds((2 * G8) * j + G8 * q, G8), :], pl[q][:, :, :]).then_inc(lg_copied, 1)
                dve.wait_ge(lg_copied, NG + 2)
                link(dve.tensor_reduce(tmax[:, :], lg[:, :, :], AX.X, ALU.max))
                dve.tensor_tensor(lg[:, :, :], lg[:, :, :], tmax[:, :].unsqueeze(2).broadcast_to([P, NT, E]),
                                  ALU.subtract).then_inc(low_ready, 1)
                dve.wait_ge(exp_done, 1)
                link(dve.tensor_reduce(tsum[:, :], pr[:, :, :], AX.X, ALU.add))
                link(dve.reciprocal(tsum[:, :], tsum[:, :]))
                dve.tensor_tensor(pr[:, :, :], pr[:, :, :], tsum[:, :].unsqueeze(2).broadcast_to([P, NT, E]),
                                  ALU.mult).then_inc(pr_ready, 1)
                for n in range(2):
                    dve.wait_ge(pT_made, n + 1)
                    last = dve.tensor_copy(pT[:, n * 16:(n + 1) * 16, :].rearrange("p s b -> p (s b)"),
                                           pt[n][:, :, :].rearrange("p g t -> p (g t)"))
                link(last)

                def wide(a):
                    return a.unsqueeze(2).broadcast_to([P, SG, B])

                def row(a):
                    return a[:, :].unsqueeze(1).broadcast_to([P, SG, B])

                def first_of_top(index):
                    link(dve.tensor_reduce(m[:, :], pT[:, :, :], AX.X, ALU.max))
                    link(dve.tensor_tensor(eq[:, :, :], pT[:, :, :], wide(m[:, :]), ALU.is_equal))
                    link(dve.scalar_tensor_tensor(out=eq[:, :, :], in0=eq[:, :, :], scalar=-64.0, in1=row(iota64),
                                                  op0=ALU.mult, op1=ALU.add))
                    link(dve.tensor_reduce(index[:, :], eq[:, :, :], AX.X, ALU.min))

                first_of_top(i1)
                link(dve.tensor_tensor(eq[:, :, :], row(iota), wide(i1[:, :]), ALU.is_equal))
                link(dve.scalar_tensor_tensor(out=pT[:, :, :], in0=eq[:, :, :], scalar=-4.0, in1=pT[:, :, :],
                                              op0=ALU.mult, op1=ALU.add))
                first_of_top(i2)
                dve.tensor_tensor(lo_hi[:, 0, :], i1[:, :], i2[:, :], ALU.min)
                link(dve.tensor_tensor(lo_hi[:, 1, :], i1[:, :], i2[:, :], ALU.max))
                for i in range(2):
                    last = dve.tensor_tensor(hot[:, i], row(iota), wide(lo_hi[:, i, :]), ALU.is_equal)
                last.then_inc(hot_ready, 1)
                for i in range(2):
                    for g in range(NG):
                        n = (i * NG + g) // 4
                        dve.wait_ge(hotT_made, n + 1)
                        slots = sel[:, g * G8:(g + 1) * G8, :].rearrange("p t (e s i) -> p (t e) s i", e=E, i=2)[:, :, :, i]
                        dve.tensor_tensor(slots, pt[n][:, g % 4, :].unsqueeze(2).broadcast_to([P, P, SP]),
                                          posmask[:, :].unsqueeze(1).broadcast_to([P, P, SP]), ALU.mult).then_inc(sel_ready, 1)

        with Stage(nc, "gather") as st:
            sem = st.sem
            pg = [st.ps(f"pg{q}", [P, C, P]) for q in range(4)]
            x_loaded = [sem(f"x_loaded{q}") for q in range(2)]
            made, copied = sem("made"), sem("copied")
            block = st.block()

            @block.sync
            def _(sp):
                for q in range(2):
                    load_group(sp, q, q, x_loaded[q])
                with sp.Fori(0, NG // 2 - 1) as j:
                    for q in range(2):
                        sp.wait_ge(made, (2 * G8) * j + G8 * (q + 1))
                        load_group(sp, 2 * j + (q + 2), q, x_loaded[q])

            @block.tensor
            def _(pe):
                with pe.Fori(0, NG // 2) as j:
                    for q in range(2):
                        pe.wait_ge(x_loaded[q], 64 * j + 64)
                        for t in range(G8):
                            pe.wait_ge(copied, (2 * G8) * j + (G8 * q + t + 1))
                            for c in range(C):
                                last = pe.matmul(pg[t % 4][:, c, :], xg[:, q, t, c * P:(c + 1) * P],
                                                 sel[:, bass.ds((2 * G8) * j + (G8 * q + t), 1), :].rearrange("p o s -> p (o s)"),
                                                 start=True, stop=True)
                            last.then_inc(made, 1)

            @block.scalar
            def _(act):
                act.sem_inc(copied, 4)
                with act.Fori(0, NG // 2) as j:
                    for q in range(2):
                        for t in range(G8):
                            act.wait_ge(made, (2 * G8) * j + (G8 * q + t + 1))
                            act.activation(hg[:, :, :, bass.ds((2 * G8 * SL) * j + SL * (G8 * q + t), SL)],
                                           pg[t % 4][:, :, :].rearrange("p c (e s) -> p c e s", e=E), ACT.Copy).then_inc(copied, 1)

        with Stage(nc, "expert") as st:
            sb, ps, sem = st.sb, st.ps, st.sem
            WS = 4
            wq = sb("wq", [P, WS, C, F])
            wkv = sb("wkv", [P, WS, C, 2 * F])
            wo = sb("wo", [P, WS, D])
            bqkv = sb("bqkv", [P, WS, 2])
            bo = sb("bo", [P, C])
            sum4 = sb("sum4", [F, 4, P])
            pick4 = sb("pick4", [4, 4, P])
            q_sb = sb("q", [F, 2, ES])
            kv = sb("kv", [P, 2, ES])
            prod = sb("prod", [F, 2, 4, S])
            nmax = sb("nmax", [4, 2])
            rsum = sb("rsum", [4, 2])
            prob = sb("prob", [4, 2, S])
            pv = sb("pv", [P, 4, S])
            av = sb("av", [P, 2, ES])
            pq, pkv, pa = ps("pq", [F, 512]), ps("pkv", [P, 512]), ps("pa", [P, 512])
            pb = ps("pb", [P, 4, S])
            po = [ps(f"po{c}", [P, 512]) for c in range(C)]
            w_loaded = [sem(f"w_loaded{q}") for q in range(WS)]
            c_loaded = sem("c_loaded")
            q_made, kv_made, q_ready, kv_ready = sem("q_made"), sem("kv_made"), sem("q_ready"), sem("kv_ready")
            prod_ready, att_made, max_ready, exp_done = sem("prod_ready"), sem("att_made"), sem("max_ready"), sem("exp_done")
            prob_ready, spread_made, av_ready = sem("prob_ready"), sem("spread_made"), sem("av_ready")
            out_made, out_copied, chain = sem("out_made"), sem("out_copied"), sem("chain")
            block = st.block()
            PER = 4

            @block.sync
            def _(sp):
                for dst, src in ((sum4[:, :, :], sum4_d), (pick4[:, :, :], pick4_d), (bo[:, :], bo_d)):
                    sp.dma_start(dst, src).then_inc(c_loaded, 16)

                def load(h, q):
                    sp.dma_start(wq[:, q], wq_d[h].rearrange("(c p) f -> p c f", p=P)).then_inc(w_loaded[q], 16)
                    sp.dma_start(wkv[:, q], wkv_d[h].rearrange("(c p) f -> p c f", p=P)).then_inc(w_loaded[q], 16)
                    sp.dma_start(wo[F:P, q], wo_d[h]).then_inc(w_loaded[q], 16)
                    sp.dma_start(bqkv[:, q], bqkv_d[h]).then_inc(w_loaded[q], 16)

                for q in range(WS):
                    load(q, q)
                with sp.Fori(0, E // WS - 1) as j:
                    for q in range(WS):
                        sp.wait_ge(out_made, WS * j + (q + 1))
                        load(WS * j + (q + WS), q)

            @block.tensor
            def _(pe):
                def project(j, k):
                    n = WS * j + (k + 1)
                    pe.wait_ge(w_loaded[k], (16 * PER) * j + 16 * PER)
                    pe.wait_ge(kv_ready, n)
                    pe.wait_ge(q_ready, n)
                    for c in range(C):
                        tok = hg[:, c, bass.ds(WS * j + k, 1), :].rearrange("p o s -> p (o s)")
                        last = pe.matmul(pq[:, :], wq[:, k, c, :], tok, start=(c == 0), stop=(c == C - 1))
                    last.then_inc(q_made, 1)
                    for c in range(C):
                        tok = hg[:, c, bass.ds(WS * j + k, 1), :].rearrange("p o s -> p (o s)")
                        last = pe.matmul(pkv[:, :], wkv[:, k, c, :], tok, start=(c == 0), stop=(c == C - 1))
                    last.then_inc(kv_made, 1)

                def attend(j, k):
                    pe.wait_ge(prod_ready, WS * j + (k + 1))
                    for n in range(4):
                        last = pe.matmul(pa[:, 0:S], sum4[:, n, :], prod[:, k % 2, n, :], start=(n == 0), stop=(n == 3))
                    last.then_inc(att_made, 1)

                def spread(j, k):
                    pe.wait_ge(prob_ready, WS * j + (k + 1))
                    pe.wait_ge(av_ready, WS * j + (k + 1))
                    for n in range(4):
                        last = pe.matmul(pb[:, n, :], pick4[:, n, :], prob[:, k % 2, :], start=True, stop=True)
                    last.then_inc(spread_made, 1)

                def output(j, k):
                    pe.wait_ge(av_ready, WS * j + (k + 2))
                    pe.wait_ge(out_copied, WS * j + (k + 1))
                    for c in range(C):
                        last = pe.matmul(po[c][:, :], wo[F:P, k, c * P:(c + 1) * P], av[F:P, k % 2, :], start=True, stop=True)
                    last.then_inc(out_made, 1)

                def expert(this, nxt, after):
                    spread(*this)
                    if nxt is not None:
                        attend(*nxt)
                    output(*this)
                    if after is not None:
                        project(*after)

                pe.wait_ge(c_loaded, 48)
                project(0, 0)
                attend(0, 0)
                project(0, 1)
                in_turns(pe, expert, E // WS, WS, (0, 1, 2))

            @block.scalar
            def _(act):
                def keys(j, k):
                    act.wait_ge(kv_made, WS * j + (k + 1))
                    act.activation(kv[:, k % 2, :], pkv[:, :], ACT.Identity, bias=bqkv[:, k, 0:1]).then_inc(kv_ready, 1)

                def expo(j, k):
                    act.wait_ge(max_ready, WS * j + (k + 1))
                    act.activation(prob[:, k % 2, :], pa[0:4, 0:S], ACT.Exp, bias=nmax[:, k % 2:k % 2 + 1],
                                   accum_out=rsum[:, k % 2:k % 2 + 1]).then_inc(exp_done, 1)

                def output(j, k):
                    act.wait_ge(out_made, WS * j + (k + 1))
                    for c in range(C):
                        last = act.activation(hg[:, c, bass.ds(WS * j + k, 1), :].rearrange("p o s -> p (o s)"), po[c][:, :],
                                              ACT.Identity, bias=bo[:, c:c + 1])
                    last.then_inc(out_copied, 1)

                def expert(this, nxt, after):
                    if nxt is not None:
                        expo(*nxt)
                    output(*this)
                    if after is not None:
                        keys(*after)

                act.sem_inc(kv_ready, 1)
                act.sem_inc(out_copied, 1)
                act.wait_ge(c_loaded, 48)
                keys(0, 0)
                expo(0, 0)
                keys(0, 1)
                in_turns(act, expert, E // WS, WS, (0, 1, 2))

            @block.vector
            def _(dve):
                def pairs(j, k):
                    q = k % 2
                    dve.wait_ge(q_made, WS * j + (k + 1))
                    dve.tensor_scalar(q_sb[:, q, :], pq[:, :], bqkv[0:F, k, 1:2], 0.125, ALU.add, ALU.mult).then_inc(q_ready, 1)
                    dve.wait_ge(q_ready, WS * j + (k + 2))
                    dve.wait_ge(kv_ready, WS * j + (k + 2))
                    dve.tensor_tensor(prod[:, q].rearrange("p (i k) b -> p i k b", i=2),
                                      q_sb[:, q, :].rearrange("p (b i) -> p i b", i=2).unsqueeze(2).broadcast_to([F, 2, 2, S]),
                                      kv[0:F, q, :].rearrange("p (b k) -> p k b", k=2).unsqueeze(1).broadcast_to([F, 2, 2, S]),
                                      ALU.mult).then_inc(prod_ready, 1)

                def softmax(j, k):
                    q = k % 2
                    dve.wait_ge(att_made, WS * j + (k + 1))
                    dve.tensor_reduce(nmax[:, q:q + 1], pa[0:4, 0:S], AX.X, ALU.max, negate=True).then_inc(max_ready, 1)
                    dve.wait_ge(exp_done, WS * j + (k + 1))
                    link(dve.reciprocal(rsum[:, q:q + 1], rsum[:, q:q + 1]))
                    dve.tensor_scalar(prob[:, q, :], prob[:, q, :], rsum[:, q:q + 1], None, ALU.mult).then_inc(prob_ready, 1)

                def weigh(j, k):
                    q = k % 2
                    dve.wait_ge(spread_made, WS * j + (k + 1))
                    v = kv[F:P, q, :].rearrange("p (b k) -> p k b", k=2).unsqueeze(1).broadcast_to([F, 2, 2, S])
                    link(dve.tensor_tensor(pv[F:P].rearrange("p (i k) b -> p i k b", i=2),
                                           pb[F:P].rearrange("p (i k) b -> p i k b", i=2), v, ALU.mult))
                    w = pv[F:P].rearrange("p (i k) b -> p i k b", i=2)
                    dve.tensor_tensor(av[F:P, q, :].rearrange("p (b i) -> p i b", i=2), w[:, :, 0, :], w[:, :, 1, :],
                                      ALU.add).then_inc(av_ready, 1)

                def expert(this, nxt):
                    if nxt is not None:
                        pairs(*nxt)
                    weigh(*this)
                    if nxt is not None:
                        softmax(*nxt)

                link = Chain(dve, chain, WS * 2)
                dve.sem_inc(q_ready, 1)
                dve.sem_inc(av_ready, 1)
                pairs(0, 0)
                softmax(0, 0)
                in_turns(dve, expert, E // WS, WS, (0, 1), link)

        with Stage(nc, "scatter") as st:
            sb, ps, sem = st.sb, st.ps, st.sem
            NP = G8 // 2
            PT = 2 * NP
            last_pair = (NG // 2 - 1, PT - 1)
            slots = sb("slots", [P, 2, 2, C + 1, P])
            turned = sb("turned", [P, 2, 2, C + 1, P])
            ln_gb = sb("ln_gb", [P, 2, D])
            spacer = sb("spacer", [P, 1])
            eps = sb("eps", [P, 2])
            minus_half = sb("minus_half", [P, 2])
            r = sb("r", [P, 2, 2, D])
            z = sb("z", [P, 2, 2, D])
            r2 = sb("r2", [P, 2, 2, D])
            stats = sb("stats", [P, 2, 2, 6])
            mv = sb("mv", [P, 2, 2, 2])
            stats2 = sb("stats2", [P, 2, 2, 6])
            mv2 = sb("mv2", [P, 2, 2, 2])
            veps = sb("veps", [P, 2, 2, 2])
            rstd = sb("rstd", [P, 2, 2])
            rstd2 = sb("rstd2", [P, 2, 2])
            yg = sb("yg", [P, 2, G8, D])
            pt = [ps(f"pt{k}", [P, C + 1, P]) for k in range(4)]
            py = [ps(f"py{k}", [P, 2, D]) for k in range(2)]
            w_loaded = sem("w_loaded")
            x_loaded = [sem(f"x_loaded{q}") for q in range(2)]
            y_stored = [sem(f"y_stored{q}") for q in range(2)]
            slots_ready, turn_made, turn_copied = sem("slots_ready"), sem("turn_made"), sem("turn_copied")
            y_made, res_added, var_ready, rstd_ready = sem("y_made"), sem("res_added"), sem("var_ready"), sem("rstd_ready")
            z_ready, affine_done, var2_ready, rstd2_ready = sem("z_ready"), sem("affine_done"), sem("var2_ready"), sem("rstd2_ready")
            y_ready, chain, pool_chain = sem("y_ready"), sem("chain"), sem("pool_chain")
            block = st.block()

            @block.sync
            def _(sp):
                for n in range(2):
                    sp.dma_start(ln_gb[:, n, :], ln_d[n].partition_broadcast(P)).then_inc(w_loaded, 16)
                for q in range(2):
                    load_group(sp, q, q, x_loaded[q])
                    sp.sem_inc(y_stored[q], 64)

                def store(j, q):
                    sp.wait_ge(y_ready, (2 * NP) * j + NP * (q + 1))
                    for s in range(SP):
                        sp.dma_start(xg_out[2 * j + q][s], yg[s * B:(s + 1) * B, q]).then_inc(y_stored[q], 16)

                with sp.Fori(0, NG // 2 - 1) as j:
                    for q in range(2):
                        store(j, q)
                        load_group(sp, 2 * j + (q + 2), q, x_loaded[q])
                store(NG // 2 - 1, 0)
                store(NG // 2 - 1, 1)
                for q in range(2):
                    sp.wait_ge(y_stored[q], 64 * (NG // 2 + 1))

            @block.tensor
            def _(pe):
                def turn(j, k):
                    n, p = PT * j + (k + 1), k % 2
                    pe.wait_ge(slots_ready, n)
                    pe.wait_ge(turn_copied, n)
                    for t in range(2):
                        for c in range(C + 1):
                            last = pe.transpose(pt[2 * p + t][:, c, :], slots[:, p, t, c, :], ident[:, :])
                    last.then_inc(turn_made, 1)

                def scatter(j, k):
                    n, p = PT * j + (k + 1), k % 2
                    pe.wait_ge(turn_copied, n + 2)
                    pe.wait_ge(res_added, n)
                    for t in range(2):
                        last = pe.matmul(py[p][:, t, :], turned[:, p, t, C, :],
                                         turned[:, p, t, 0:C, :].rearrange("p c d -> p (c d)"), start=True, stop=True)
                    last.then_inc(y_made, 1)

                def pair(this, nxt):
                    if nxt is not None:
                        turn(*nxt)
                    scatter(*this)

                turn(0, 0)
                in_turns(pe, pair, NG // 2, PT, (0, 1))

            @block.scalar
            def _(act):
                def stage(j, k):
                    for t in range(2):
                        tile = (PT * 2) * j + (2 * k + t)
                        act.activation(slots[:, k % 2, t, 0:C, :].rearrange("p c (e s) -> p c e s", e=E),
                                       hg[:, :, :, bass.ds(tile * SL, SL)], ACT.Copy)
                        last = act.activation(slots[:, k % 2, t, C, :], sel[:, bass.ds(tile, 1), :].rearrange("p o s -> p (o s)"),
                                              ACT.Copy)
                    last.then_inc(slots_ready, 1)

                def copy(j, k):
                    act.wait_ge(turn_made, PT * j + (k + 1))
                    for t in range(2):
                        last = act.activation(turned[:, k % 2, t], pt[2 * (k % 2) + t][:, :, :], ACT.Copy)
                    last.then_inc(turn_copied, 1)

                def pair(nxt, after):
                    if nxt is not None:
                        copy(*nxt)
                    if after is not None:
                        act.wait_ge(turn_made, PT * after[0] + (after[1] - 1))
                        stage(*after)

                act.sem_inc(turn_copied, 2)
                stage(0, 0)
                stage(0, 1)
                copy(0, 0)
                in_turns(act, pair, NG // 2, PT, (1, 2))

            @block.gpsimd
            def _(pool):
                def rstd_of(out, v, m, ready, done, n):
                    pool.wait_ge(ready, n)
                    link(pool.tensor_tensor(v, m, eps[:, :], ALU.add))
                    pool.tensor_tensor(out, v, minus_half[:, :], ALU.pow).then_inc(done, 1)

                def first(j, k):
                    rstd_of(rstd[:, k % 2], veps[:, 0, k % 2], mv[:, k % 2, :, 1], var_ready, rstd_ready, PT * j + (k + 1))

                def affine(j, k):
                    p = k % 2
                    pool.wait_ge(z_ready, PT * j + (k + 1))
                    link(pool.tensor_tensor(z[:, p], z[:, p], ln_gb[:, 0, :].unsqueeze(1).broadcast_to([P, 2, D]), ALU.mult))
                    pool.tensor_tensor(z[:, p], z[:, p], ln_gb[:, 1, :].unsqueeze(1).broadcast_to([P, 2, D]),
                                       ALU.add).then_inc(affine_done, 1)

                def second(j, k):
                    rstd_of(rstd2[:, k % 2], veps[:, 1, k % 2], mv2[:, k % 2, :, 1], var2_ready, rstd2_ready, PT * j + (k + 1))

                def pair(this, one_back, two_back):
                    first(*this)
                    if one_back is not None:
                        affine(*one_back)
                    if two_back is not None:
                        second(*two_back)

                link = Chain(pool, pool_chain, PT * 3)
                pool.memset(eps[:, :], LN_EPS)
                link(pool.memset(minus_half[:, :], -0.5))
                pool.wait_ge(w_loaded, 32)
                in_turns(pool, pair, NG // 2, PT, (0, -1, -2), link)
                affine(*last_pair)
                second(last_pair[0], last_pair[1] - 1)
                second(*last_pair)

            @block.vector
            def _(dve):
                def moments(st_, mv_, src, ready):
                    for t in range(2):
                        last = dve.bn_stats(st_[:, t, :], src[:, t, :])
                    link(last)
                    dve.memset(spacer[:, :], 0.0)
                    for t in range(2):
                        last = dve.bn_aggr(mv_[:, t, :], st_[:, t, :])
                    last.then_inc(ready, 1)

                def apply(out, src, mv_, rs):
                    for t in range(2):
                        last = dve.tensor_scalar(out[:, t, :], src[:, t, :], mv_[:, t, 0:1], rs[:, t:t + 1],
                                                 ALU.subtract, ALU.mult)
                    return last

                def x_of(k):
                    return xg[:, k // NP, 2 * (k % NP):2 * (k % NP) + 2, :]

                def scattered(j, k):
                    p = k % 2
                    if k % NP == 0:
                        dve.wait_ge(x_loaded[k // NP], 64 * j + 64)
                    if not (type(j) is int and PT * j + k < 2):
                        dve.wait_ge(z_ready, PT * j + (k - 1))
                    dve.wait_ge(y_made, PT * j + (k + 1))
                    link(dve.tensor_tensor(r[:, p], py[p][:, :, :], x_of(k), ALU.add))
                    dve.sem_inc(res_added, 1)
                    moments(stats[:, p], mv[:, p], r[:, p], var_ready)

                def first_norm(j, k):
                    p = k % 2
                    dve.wait_ge(rstd_ready, PT * j + (k + 1))
                    apply(z[:, p], r[:, p], mv[:, p], rstd[:, p]).then_inc(z_ready, 1)

                def residual(j, k):
                    p = k % 2
                    if not (type(j) is int and PT * j + k < 2):
                        dve.wait_ge(y_ready, PT * j + (k - 1))
                    dve.wait_ge(affine_done, PT * j + (k + 1))
                    link(dve.tensor_tensor(r2[:, p], z[:, p], x_of(k), ALU.add))
                    moments(stats2[:, p], mv2[:, p], r2[:, p], var2_ready)

                def finish(j, k):
                    p, q = k % 2, k // NP
                    dve.wait_ge(rstd2_ready, PT * j + (k + 1))
                    if k % NP == 0:
                        dve.wait_ge(y_stored[q], 64 * j + 64)
                    at = 2 * (k % NP)
                    apply(yg[:, q, at:at + 2], r2[:, p], mv2[:, p], rstd2[:, p]).then_inc(y_ready, 1)

                def pair(this, one_back, two_back, three_back):
                    scattered(*this)
                    if one_back is not None:
                        first_norm(*one_back)
                    if two_back is not None:
                        residual(*two_back)
                    if three_back is not None:
                        finish(*three_back)

                link = Chain(dve, chain, PT * 4)
                dve.sem_inc(res_added, 2)
                in_turns(dve, pair, NG // 2, PT, (0, -1, -2, -3), link)
                turn, k = last_pair
                first_norm(turn, k)
                residual(turn, k - 1)
                finish(turn, k - 2)
                residual(turn, k)
                finish(turn, k - 1)
                finish(turn, k)


def mamba(nc, x_in, x_out, ct_dram, g_d, win_d, wout_d, conv_d, wx_d, dtp_d, alog_d, ident_d):
    DI = wout_d.shape[0]
    IC = DI // P
    N = alog_d.shape[2]
    GB = 2
    NG = B // GB
    TT = GB * T
    GS = GB * S
    xf_in = x_in.rearrange("(g b) (t p) d -> g p (b t) d", b=GB, p=P)
    xf_out = x_out.rearrange("(g b) (t p) d -> g p (b t) d", b=GB, p=P)
    IT = IC // 2
    with Stage(nc, "ma") as st:
        sb, ps, sem = st.sb, st.ps, st.sem
        ident = sb("ident", [P, P])
        gain = sb("gain", [P, C])
        win = sb("win", [P, C, 2 * DI])
        wout = sb("wout", [P, IC, D])
        wx = sb("wx", [P, IC, 2 * N + 1])
        conv = sb("conv", [P, IC, 5])
        dtp = sb("dtp", [P, 3, IC])
        A = sb("A", [P, IC, N])
        k256 = sb("k256", [P, TT])
        eps6 = sb("eps6", [P, TT])
        eps5 = sb("eps5", [P, TT])
        minus_half = sb("minus_half", [P, TT])
        spacer = sb("spacer", [P, 1])
        x = sb("x", [P, TT, D])
        xr = sb("xr", [P, TT, D])
        ssq = sb("ssq", [P, TT])
        ms = sb("ms", [P, TT])
        rms = sb("rms", [P, TT])
        xn = sb("xn", [P, TT, D])
        square = xn
        xnT = sb("xnT", [P, C, GS])
        xc = sb("xc", [P, 2, IC, GS])
        sz = sb("sz", [P, 2, IC, GS])
        dt = sb("dt", [P, 2, IC, GS])
        b_t = sb("b_t", [P, 2, TT, N])
        ct = sb("ct", [P, GS])
        lrep = sb("lrep", [P, GS])
        av = sb("av", [P, IC, GS])
        ln1 = sb("ln1", [P, IC, GS])
        w1 = sb("w1", [P, IC, GS])
        uT = sb("uT", [P, 2, TT, IT * P])
        bu = sb("bu", [P, 2, TT, IT * P])
        ud = sb("ud", [P, 2, IC - IT, GS])
        bud = sb("bud", [P, 2, IC - IT, GS])
        a = sb("a", [P, 2, IC, GS])
        h = sb("h", [P, 2, IC, GS])
        bcrep = sb("bcrep", [P, 4, 2, GS])
        ch = sb("ch", [P, 2, IC, GS])
        yv = w1
        r = xr
        stats = sb("stats", [P, TT, 6])
        mv = sb("mv", [P, TT, 2])
        veps = sb("veps", [P, TT])
        rstd = sb("rstd", [P, TT])
        y = sb("y", [P, TT, D])
        u = av
        py = [ps(f"py{c}", [P, GS]) for c in range(IC)]
        pbu = [ps(f"pbu{k}", [P, GS]) for k in range(2)]
        pm = [ps(f"pm{k}", [P, GS]) for k in range(2)]

        w_loaded, x_loaded, xr_loaded, y_stored = sem("w_loaded"), sem("x_loaded"), sem("xr_loaded"), sem("y_stored")
        ct_stored, lrep_loaded = sem("ct_stored"), sem("lrep_loaded")
        bc_loaded = [sem(f"bc_loaded{k}") for k in range(4)]
        bud_ready, ud_ready = sem("bud_ready"), sem("ud_ready")
        setup_done, ssq_ready, rms_ready, xn_ready = sem("setup_done"), sem("ssq_ready"), sem("rms_ready"), sem("xn_ready")
        xT_made, xT_copied, in_made = sem("xT_made"), sem("xT_copied"), sem("in_made")
        sz_ready, w1_ready, loss_ready = sem("sz_ready"), sem("w1_ready"), sem("loss_ready")
        z_made, exp_ready = sem("z_made"), sem("exp_ready")
        conv_done, z_copied, silu_done = sem("conv_done"), sem("z_copied"), sem("silu_done")
        b_made, b_copied, ct_made, ct_copied = sem("b_made"), sem("b_copied"), sem("ct_made"), sem("ct_copied")
        ln_ready, dt_ready, u_ready, uT_made, uT_copied = sem("ln_ready"), sem("dt_ready"), sem("u_ready"), sem("uT_made"), sem("uT_copied")
        bu_ready, bu_turned, a_ready, scanned = sem("bu_ready"), sem("bu_turned"), sem("a_ready"), sem("scanned")
        multiplied, summed, gated, yv_ready = sem("multiplied"), sem("summed"), sem("gated"), sem("yv_ready")
        out_made, res_added, var_ready, rstd_ready, y_ready = sem("out_made"), sem("res_added"), sem("var_ready"), sem("rstd_ready"), sem("y_ready")
        act_chain, dve_chain, pool_chain = sem("act_chain"), sem("dve_chain"), sem("pool_chain")
        block = st.block()
        loads = [(ident[:, :], ident_d), (gain[:, :], g_d), (win[:, :, :], win_d.rearrange("(c p) f -> p c f", p=P)),
                 (wout[:, :, :], wout_d.rearrange("(c p) f -> p c f", p=P)),
                 (wx[:, :, :], wx_d.rearrange("(c p) f -> p c f", p=P)),
                 (conv[:, :, :], conv_d), (dtp[:, :, :], dtp_d), (A[:, :, :], alog_d)]

        def groups(eng, group, link=None, turns=NG // 2 - 1):
            if link:
                link.turn = None
            group(0, 0, True, False)
            if link:
                link.begin(0)
            with eng.Fori(0, turns) as j:
                if link:
                    link.turn = j
                group(2 * j + 1, 1, False, False)
                group(2 * j + 2, 0, False, False)
            if link:
                link.end(turns)
            for g in range(2 * turns + 1, NG):
                group(g, g % 2, False, g == NG - 1)

        @block.sync
        def _(sp):
            def load_x(g):
                sp.dma_start(x[:, :, :], xf_in[g]).then_inc(x_loaded, 16)

            def load_c(g, par, s):
                src = ct_dram[par, 0:2 * N].rearrange("(k n) f -> n k f", k=2)[s]
                sp.dma_start(bcrep[:, s % 4], src.partition_broadcast(P)).then_inc(bc_loaded[s % 4], 16)

            def spread(g, par):
                sp.wait_ge(ct_copied, g + 1)
                sp.dma_start(ct_dram[par], ct[0:2 * N + 1, :]).then_inc(ct_stored, 16)
                sp.wait_ge(ct_stored, 16 * g + 32)
                sp.dma_start(lrep[:, :], ct_dram[par, 2 * N, :].partition_broadcast(P)).then_inc(lrep_loaded, 16)

            def group(g, par, first, last):
                for s in range(N):
                    if s == 2 and not last:
                        if not (type(g) is int and g + 2 >= NG):
                            sp.wait_ge(xn_ready, g + 2)
                            load_x(g + 2)
                    if s == 14:
                        if not first:
                            sp.wait_ge(y_ready, g)
                            sp.dma_start(xf_out[g - 1], y[:, :, :]).then_inc(y_stored, 16)
                        sp.dma_start(xr[:, :, :], xf_in[g]).then_inc(xr_loaded, 16)
                    if s == 8 and not last:
                        spread(g + 1, 1 - par)
                    sp.wait_ge(multiplied, N * g + (s + 3))
                    if s + 4 < N:
                        load_c(g, par, s + 4)
                    elif not last:
                        load_c(g + 1, 1 - par, s + 4 - N)

            for dst, src in loads:
                sp.dma_start(dst, src).then_inc(w_loaded, 16)
            sp.sem_inc(y_stored, 16)
            sp.sem_inc(ct_stored, 16)
            load_x(0)
            sp.wait_ge(xn_ready, 1)
            load_x(1)
            spread(0, 0)
            for s in range(4):
                load_c(0, 0, s)
            groups(sp, group, turns=NG // 2 - 2)
            sp.wait_ge(y_ready, NG)
            sp.dma_start(xf_out[NG - 1], y[:, :, :]).then_inc(y_stored, 16)
            sp.wait_ge(y_stored, 16 * (NG + 1))

        @block.tensor
        def _(pe):
            def turn_x(n, c):
                if c == 0:
                    pe.wait_ge(xn_ready, n + 1)
                    if not (type(n) is int and n == 0):
                        pe.wait_ge(uT_copied, 2 * n)
                for t in range(TT):
                    last = pe.transpose(pm[c][:, t * P:(t + 1) * P], xn[:, t, c * P:(c + 1) * P], ident[:, :])
                last.then_inc(xT_made, 1)

            def project_in(n, f):
                if f == 0:
                    pe.wait_ge(xT_copied, 2 * n + 2)
                for half, copied, done in ((0, conv_done, in_made), (1, z_copied, z_made)):
                    if f > 0:
                        pe.wait_ge(copied, 4 * n + f)
                    for c in range(C):
                        last = pe.matmul(pm[half][:, :], win[:, c, half * DI + f * P:half * DI + (f + 1) * P], xnT[:, c, :],
                                         start=(c == 0), stop=(c == C - 1))
                    last.then_inc(done, 1)

            def parameters(n, par):
                pe.wait_ge(silu_done, n + 1)
                pe.wait_ge(z_copied, 4 * n + 4)
                for c in range(IC):
                    last = pe.matmul(pm[1][0:2 * N + 1, :], wx[:, c, :], xc[:, par, c, :],
                                     start=(c == 0), stop=(c == IC - 1))
                last.then_inc(ct_made, 1)

            def turn_b(n):
                pe.wait_ge(ct_copied, n + 1)
                for t in range(TT):
                    last = pe.transpose(pm[0][:, t * P:(t + 1) * P], ct[:, t * P:(t + 1) * P], ident[:, :])
                last.then_inc(b_made, 1)

            def turn_u(n, k, after_out):
                if k == 0:
                    pe.wait_ge(u_ready, IT * (n + 1))
                    pe.wait_ge(b_copied, n + 1)
                    pe.wait_ge(ct_copied, n + 1)
                    if after_out:
                        pe.wait_ge(res_added, 2 * n - 2)
                for t in range(2):
                    for c in range(IT):
                        last = pe.transpose(pm[k][:, (t * IT + c) * P:(t * IT + c + 1) * P],
                                            u[:, c, (2 * k + t) * P:(2 * k + t + 1) * P], ident[:, :])
                last.then_inc(uT_made, 1)

            def turn_state(g, s):
                pe.wait_ge(bu_ready, N * g + (s + 1))
                for c in range(IT):
                    pe.wait_ge(scanned, (N * IC) * g + (IC * s + c + 5))
                    for t in range(TT):
                        last = pe.transpose(pbu[c][:, t * P:(t + 1) * P], bu[:, s % 2, t, c * P:(c + 1) * P], ident[:, :])
                    last.then_inc(bu_turned, 1)

            def sum_state(g, s):
                pe.wait_ge(multiplied, N * g + (s + 3))
                for c in range(IC):
                    if s == 0:
                        pe.wait_ge(gated, IC * g + (c + 1))
                    last = pe.matmul(py[c][:, :], ident[:, :], ch[:, s % 2, c, :], start=(s == 0), stop=(s == N - 1))
                last.then_inc(summed, 1)

            def project_out(g, k, prep):
                if k == 0:
                    pe.wait_ge(yv_ready, g + 1)
                    if prep:
                        pe.wait_ge(b_copied, g + 3)
                    else:
                        pe.wait_ge(uT_copied, 2 * g + 4)
                for t in range(2):
                    for c in range(IC):
                        last = pe.matmul(pm[k][:, t * D:(t + 1) * D], yv[:, c, (2 * k + t) * P:(2 * k + t + 1) * P],
                                         wout[:, c, :], start=(c == 0), stop=(c == IC - 1))
                last.then_inc(out_made, 1)

            def group(g, par, first, last):
                n, prep = g + 1, not last
                for s in range(N):
                    turn_state(g, s)
                    if s == 2 and prep:
                        turn_x(n, 0)
                        turn_x(n, 1)
                    if 3 <= s < 3 + IC and prep:
                        project_in(n, s - 3)
                    if s == 8 and prep:
                        parameters(n, 1 - par)
                    if s == 9 and prep:
                        turn_b(n)
                    if s in (9, 10) and not first:
                        project_out(g - 1, s - 9, prep)
                    if s == 14 and prep:
                        turn_u(n, 0, not first)
                        turn_u(n, 1, not first)
                    if s >= 2:
                        sum_state(g, s - 2)
                    elif not first:
                        sum_state(g - 1, N + s - 2)

            pe.wait_ge(w_loaded, 16 * len(loads))
            turn_x(0, 0)
            turn_x(0, 1)
            for f in range(IC):
                project_in(0, f)
            parameters(0, 0)
            turn_b(0)
            for k in range(2):
                turn_u(0, k, False)
            groups(pe, group)
            for s in (N - 2, N - 1):
                sum_state(NG - 1, s)
            pe.wait_ge(yv_ready, NG)
            pe.wait_ge(res_added, 2 * NG - 2)
            for k in range(2):
                for t in range(2):
                    for c in range(IC):
                        last = pe.matmul(pm[k][:, t * D:(t + 1) * D], yv[:, c, (2 * k + t) * P:(2 * k + t + 1) * P],
                                         wout[:, c, :], start=(c == 0), stop=(c == IC - 1))
                last.then_inc(out_made, 1)

        @block.scalar
        def _(act):
            link = Chain(act, act_chain, 2 * 2)

            def squares(n):
                act.wait_ge(x_loaded, 16 * n + 16)
                for t in range(TT):
                    last = act.activation(square[:, t, :], x[:, t, :], ACT.Square, accum_out=ssq[:, t:t + 1])
                last.then_inc(ssq_ready, 1)

            def copy_xT(n, c):
                act.wait_ge(xT_made, 2 * n + (c + 1))
                act.activation(xnT[:, c, :], pm[c][:, :], ACT.Copy, scale=gain[:, c:c + 1]).then_inc(xT_copied, 1)

            def copy_z(n, par, f):
                if f == 0 and not (type(n) is int and n < 2):
                    act.wait_ge(yv_ready, n - 1)
                act.wait_ge(z_made, 4 * n + (f + 1))
                act.activation(sz[:, par, f, :], pm[1][:, :], ACT.Copy).then_inc(z_copied, 1)

            def silu(n, par):
                act.wait_ge(conv_done, 4 * n + 4)
                act.activation(xc[:, par], xc[:, par], ACT.Silu).then_inc(silu_done, 1)
                act.wait_ge(z_copied, 4 * n + 4)
                act.activation(sz[:, par], sz[:, par], ACT.Silu).then_inc(sz_ready, 1)

            def copy_parameters(n):
                act.wait_ge(ct_made, n + 1)
                act.wait_ge(ct_stored, 16 * n + 16)
                act.activation(ct[0:2 * N + 1, :], pm[1][0:2 * N + 1, :], ACT.Copy).then_inc(ct_copied, 1)

            def copy_b(n, par):
                act.wait_ge(b_made, n + 1)
                act.activation(b_t[:, par], pm[0][:, :].rearrange("p (t k) -> p t k", t=TT)[:, :, 0:N], ACT.Copy).then_inc(b_copied, 1)

            def step_size(n, par):
                act.wait_ge(lrep_loaded, 16 * n + 16)
                for c in range(IC):
                    act.activation(dt[:, par, c, :], lrep[:, :], ACT.Relu, bias=dtp[:, 1, c:c + 1], scale=dtp[:, 0, c:c + 1])
                    last = act.activation(av[:, c, :], lrep[:, :], ACT.Abs, bias=dtp[:, 1, c:c + 1], scale=dtp[:, 0, c:c + 1])
                link(last)

            def step_size_log(n):
                link(act.activation(av[:, :, :], av[:, :, :], ACT.Exp, scale=-1.0))
                act.sem_inc(exp_ready, 1)
                act.activation(ln1[:, :, :], av[:, :, :], ACT.Ln, bias=1.0).then_inc(ln_ready, 1)

            def copy_uT(n, par, k):
                act.wait_ge(uT_made, 2 * n + (k + 1))
                act.activation(uT[:, par, 2 * k:2 * k + 2, :], pm[k][:, :].rearrange("p (t f) -> p t f", t=2), ACT.Copy).then_inc(uT_copied, 1)

            def scale_b(g, par, s):
                if s == 0:
                    act.wait_ge(uT_copied, 2 * g + 2)
                    act.wait_ge(b_copied, g + 1)
                act.wait_ge(bu_turned, (N * IT) * g + (IT * s + 2))
                for t in range(TT):
                    last = act.activation(bu[:, s % 2, t, :], uT[:, par, t, :], ACT.Copy, scale=b_t[:, par, t, s:s + 1])
                last.then_inc(bu_ready, 1)

            def decay(g, par, s):
                if s == 0:
                    act.wait_ge(dt_ready, g + 1)
                for c in range(IC):
                    act.wait_ge(scanned, (N * IC) * g + (IC * s + c + 1))
                    act.activation(a[:, s % 2, c, :].rearrange("p (b t) -> p b t", b=GB)[:, :, 1:S],
                                   dt[:, par, c, :].rearrange("p (b t) -> p b t", b=GB)[:, :, 1:S],
                                   ACT.Exp, scale=A[:, c, s:s + 1]).then_inc(a_ready, 1)

            def group(g, par, first, last):
                n, prep, np_ = g + 1, not last, 1 - par
                for s in range(N):
                    if s != 8 or not prep:
                        decay(g, par, s)
                    if s + 1 < N:
                        scale_b(g, par, s + 1)
                    elif prep:
                        scale_b(n, np_, 0)
                    if s == 0 and prep:
                        squares(n)
                    if s == 2 and prep:
                        copy_xT(n, 0)
                        copy_xT(n, 1)
                    if 3 <= s < 3 + IC and prep:
                        copy_z(n, np_, s - 3)
                    if s == 7 and prep:
                        decay(g, par, 8)
                        silu(n, np_)
                    if s == 8 and prep:
                        copy_parameters(n)
                    if s == 9 and prep:
                        copy_b(n, np_)
                        step_size(n, np_)
                    if s == 10 and prep:
                        step_size_log(n)
                    if s == 14 and prep:
                        copy_uT(n, np_, 0)
                        copy_uT(n, np_, 1)

            act.wait_ge(w_loaded, 16 * len(loads))
            link(act.activation(A[:, :, :], A[:, :, :], ACT.Exp))
            link(act.activation(A[:, :, :], A[:, :, :], ACT.Copy, scale=-1.0))
            act.wait_ge(setup_done, 1)
            squares(0)
            copy_xT(0, 0)
            copy_xT(0, 1)
            for f in range(IC):
                copy_z(0, 0, f)
            silu(0, 0)
            copy_parameters(0)
            copy_b(0, 0)
            step_size(0, 0)
            step_size_log(0)
            for k in range(2):
                copy_uT(0, 0, k)
            scale_b(0, 0, 0)
            groups(act, group, link)

        @block.gpsimd
        def _(pool):
            link = Chain(pool, pool_chain, 2 * 3)

            def rms_scale(n):
                pool.wait_ge(ssq_ready, n + 1)
                link(pool.tensor_tensor(ms[:, :], ssq[:, :], k256[:, :], ALU.mult))
                link(pool.tensor_tensor(ms[:, :], ms[:, :], eps6[:, :], ALU.add))
                pool.tensor_tensor(rms[:, :], ms[:, :], minus_half[:, :], ALU.pow).then_inc(rms_ready, 1)

            def times_c(g, s):
                pool.wait_ge(scanned, (N * IC) * g + (IC * s + IC + 8))
                pool.wait_ge(bc_loaded[s % 4], (4 * 16) * g + 16 * (s // 4 + 1))
                pool.wait_ge(summed, N * g + (s + 1))
                pool.tensor_tensor(ch[:, s % 2], h[:, s % 2], bcrep[:, s % 4, 1, :].unsqueeze(1).broadcast_to([P, IC, GS]),
                                   ALU.mult).then_inc(multiplied, 1)

            def rounding_loss(n):
                pool.wait_ge(w1_ready, IC * (n + 1))
                pool.tensor_tensor(w1[:, :, :], av[:, :, :], w1[:, :, :], ALU.subtract).then_inc(loss_ready, 1)

            def scale_kept(n, par):
                pool.wait_ge(dt_ready, n + 1)
                pool.tensor_tensor(ud[:, par], dt[:, par, IT:IC], xc[:, par, IT:IC], ALU.mult).then_inc(ud_ready, 1)

            def rstd_of(g):
                pool.wait_ge(var_ready, g + 1)
                link(pool.tensor_tensor(veps[:, :], mv[:, :, 1], eps5[:, :], ALU.add))
                pool.tensor_tensor(rstd[:, :], veps[:, :], minus_half[:, :], ALU.pow).then_inc(rstd_ready, 1)

            def group(g, par, first, last):
                for s in range(N):
                    if s == 0 and not last:
                        rms_scale(g + 1)
                    if s == 12 and not first:
                        rstd_of(g - 1)
                    times_c(g, s)
                    if s == 10 and not last:
                        rounding_loss(g + 1)
                    if s == 13 and not last:
                        scale_kept(g + 1, 1 - par)

            pool.memset(k256[:, :], 1.0 / D)
            pool.memset(eps6[:, :], 1e-6)
            pool.memset(eps5[:, :], LN_EPS)
            link(pool.memset(minus_half[:, :], -0.5))
            pool.sem_inc(multiplied, 2)
            pool.sem_inc(summed, 2)
            rms_scale(0)
            rounding_loss(0)
            scale_kept(0, 0)
            groups(pool, group, link)
            rstd_of(NG - 1)

        @block.vector
        def _(dve):
            link = Chain(dve, dve_chain, 2 * (4 * 4 + 2 * IC + 1 + 1))

            def normalize(n):
                dve.wait_ge(rms_ready, n + 1)
                for t in range(TT):
                    last = dve.tensor_scalar(xn[:, t, :], x[:, t, :], rms[:, t:t + 1], None, ALU.mult)
                last.then_inc(xn_ready, 1)

            def convolve(n, par, f):
                dve.wait_ge(in_made, 4 * n + (f + 1))
                out = xc[:, par, f, :].rearrange("p (b t) -> p b t", b=GB)
                src = pm[0][:, :].rearrange("p (b t) -> p b t", b=GB)
                link(dve.tensor_scalar(out, src, conv[:, f, 3:4], conv[:, f, 4:5], ALU.mult, ALU.add))
                for k in range(1, 4):
                    link(dve.scalar_tensor_tensor(out=out[:, :, k:S], in0=src[:, :, 0:S - k], scalar=conv[:, f, 3 - k:4 - k],
                                                  in1=out[:, :, k:S], op0=ALU.mult, op1=ALU.add))
                dve.sem_inc(conv_done, 1)

            def step_size(n, par, op, c):
                if op == 0:
                    if c == 0:
                        dve.wait_ge(exp_ready, n + 1)
                    dve.tensor_scalar(w1[:, c, :], av[:, c, :], 1.0, 1.0, ALU.add, ALU.subtract).then_inc(w1_ready, 1)
                elif op == 1:
                    if c == 0:
                        dve.wait_ge(ln_ready, n + 1)
                    link(dve.tensor_tensor(dt[:, par, c, :], dt[:, par, c, :], ln1[:, c, :], ALU.add))
                elif op == 2:
                    if c == 0:
                        dve.wait_ge(loss_ready, n + 1)
                    link(dve.tensor_tensor(dt[:, par, c, :], dt[:, par, c, :], w1[:, c, :], ALU.add))
                    if c == IC - 1:
                        dve.sem_inc(dt_ready, 1)
                    if c < IT:
                        dve.tensor_tensor(u[:, c, :], dt[:, par, c, :], xc[:, par, c, :], ALU.mult).then_inc(u_ready, 1)

            def scans(g, par, s, before=None):
                dve.wait_ge(multiplied, N * g + (s + 1))
                dve.wait_ge(bc_loaded[s % 4], (4 * 16) * g + 16 * (s // 4 + 1))
                if s == 0:
                    dve.wait_ge(ud_ready, g + 1)
                for c in range(IC):
                    if before:
                        before(c)
                    if c < IC - IT:
                        dve.tensor_tensor(bud[:, s % 2, c, :], ud[:, par, c, :], bcrep[:, s % 4, 0, :], ALU.mult).then_inc(bud_ready, 1)
                    dve.wait_ge(a_ready, (N * IC) * g + (IC * s + c + 1))
                    if c < IT:
                        dve.wait_ge(bu_turned, (N * IT) * g + (IT * s + c + 5))
                        inp = pbu[c][:, :]
                    else:
                        dve.wait_ge(bud_ready, (N * (IC - IT)) * g + ((IC - IT) * s + c - IT + 1))
                        inp = bud[:, s % 2, c - IT, :]
                    dve.tensor_tensor_scan(out=h[:, s % 2, c, :], data0=a[:, s % 2, c, :], data1=inp,
                                           initial=0.0, op0=ALU.mult, op1=ALU.add).then_inc(scanned, 1)

            def gate(g, par, c):
                if c == 0:
                    dve.wait_ge(summed, N * g + (N + 2))
                last = dve.scalar_tensor_tensor(out=yv[:, c, :], in0=xc[:, par, c, :], scalar=dtp[:, 2, c:c + 1],
                                                in1=py[c][:, :], op0=ALU.mult, op1=ALU.add)
                if c < IC - 1:
                    last.then_inc(gated, 1)
                else:
                    link(last)
                    dve.sem_inc(gated, 1)

            def gate_end(g, par):
                dve.wait_ge(sz_ready, g + 1)
                dve.tensor_tensor(yv[:, :, :], yv[:, :, :], sz[:, par], ALU.mult).then_inc(yv_ready, 1)

            def residual(g, k):
                dve.wait_ge(out_made, 2 * g + (k + 1))
                if k == 0:
                    dve.wait_ge(xr_loaded, 16 * g + 16)
                dve.scalar_tensor_tensor(out=r[:, 2 * k:2 * k + 2, :], in0=xr[:, 2 * k:2 * k + 2, :], scalar=2.0,
                                         in1=pm[k][:, :].rearrange("p (t d) -> p t d", t=2),
                                         op0=ALU.mult, op1=ALU.add).then_inc(res_added, 1)
                if k == 1:
                    dve.wait_ge(res_added, 2 * g + 2)
                    for t in range(TT):
                        last = dve.bn_stats(stats[:, t, :], r[:, t, :])
                    link(last)
                    dve.memset(spacer[:, :], 0.0)
                    for t in range(TT):
                        last = dve.bn_aggr(mv[:, t, :], stats[:, t, :])
                    last.then_inc(var_ready, 1)

            def finish(g):
                dve.wait_ge(rstd_ready, g + 1)
                dve.wait_ge(y_stored, 16 * g + 16)
                for t in range(TT):
                    last = dve.tensor_scalar(y[:, t, :], r[:, t, :], mv[:, t, 0:1], rstd[:, t:t + 1], ALU.subtract, ALU.mult)
                last.then_inc(y_ready, 1)

            def group(g, par, first, last):
                n, prep, np_ = g + 1, not last, 1 - par
                for s in range(N):
                    before = None
                    if s == 2 and not first:
                        for c in range(IC):
                            gate(g - 1, np_, c)
                    if s in (12, 13) and prep:
                        before = lambda c: step_size(n, np_, s - 11, c)
                    scans(g, par, s, before)
                    if s == 2 and not first:
                        gate_end(g - 1, np_)
                    if s == 1 and prep:
                        normalize(n)
                    if 3 <= s < 3 + IC and prep:
                        convolve(n, np_, s - 3)
                    if s in (9, 10) and not first:
                        residual(g - 1, s - 9)
                    if s == 10 and prep:
                        for c in range(IC):
                            step_size(n, np_, 0, c)
                    if s == 13 and not first:
                        finish(g - 1)

            dve.memset(ct[:, :], 0.0)
            for p in range(2):
                dve.memset(a[:, p], 0.0)
            link(dve.memset(spacer[:, :], 0.0))
            dve.sem_inc(setup_done, 1)
            dve.sem_inc(bu_turned, 2 * IT)
            dve.sem_inc(scanned, 8)
            dve.sem_inc(gated, IC)
            dve.wait_ge(w_loaded, 16 * len(loads))
            normalize(0)
            for f in range(IC):
                convolve(0, 0, f)
            for op in range(3):
                for c in range(IC):
                    step_size(0, 0, op, c)
            groups(dve, group, link)
            for c in range(IC):
                gate(NG - 1, 1, c)
            gate_end(NG - 1, 1)
            residual(NG - 1, 0)
            residual(NG - 1, 1)
            finish(NG - 1)


def bit_ffn(nc, x_in, x_out, wgu_d, wd_d, ident_d):
    I = wd_d.shape[0]
    IC = I // P
    ROUND = 12582912.0
    FLOOR = 1e-5
    NT = 2 * B
    BT = 8
    with Stage(nc, "ff") as st:
        sb, ps, sem = st.sb, st.ps, st.sem
        ident = sb("ident", [P, P])
        identb = sb("identb", [P, P], bf16)
        ones = sb("ones", [P, P])
        wgu_f = sb("wgu_f", [P, 2, C, I])
        wd_f = sb("wd_f", [P, IC, D])
        wgu = sb("wgu", [P, 2, C, I], bf16)
        wd = sb("wd", [P, IC, D], bf16)
        wsum = sb("wsum", [P, 3])
        wmean = sb("wmean", [P, 3])
        wscale = sb("wscale", [P, 3])
        wm127 = sb("wm127", [P, 3])
        eps = sb("eps", [P, 1])
        minus_half = sb("minus_half", [P, 1])
        spacer = sb("spacer", [P, 1])
        x = sb("x", [P, 4, T, D])
        top = sb("top", [P, 2, 2])
        scale = sb("scale", [P, 2])
        fgu = sb("fgu", [P, 2, 2])
        xr = sb("xr", [P, D])
        xq = sb("xq", [P, 2, D], bf16)
        xT = sb("xT", [P, 2, C, P], bf16)
        g = sb("g", [P, I])
        h = sb("h", [P, I])
        fd = sb("fd", [P, 2])
        hr = sb("hr", [P, I])
        hq = sb("hq", [P, I], bf16)
        hT = sb("hT", [P, IC, P], bf16)
        r = sb("r", [P, 2, D])
        stats = sb("stats", [P, 2, 6])
        mv = sb("mv", [P, 2, 2])
        veps = sb("veps", [P, 1])
        rstd = sb("rstd", [P, 2])
        y = sb("y", [P, 2, T, D])
        pgate, pup = ps("pgate", [P, I]), ps("pup", [P, I])
        px, ph, pd = ps("px", [P, C, P], bf16), ps("ph", [P, IC, P], bf16), ps("pd", [P, 512])

        w_loaded, wsum_ready, wtotal_made, setup_done = sem("w_loaded"), sem("wsum_ready"), sem("wtotal_made"), sem("setup_done")
        x_loaded = [sem(f"x_loaded{b}") for b in range(4)]
        y_stored = [sem(f"y_stored{p}") for p in range(2)]
        xq_ready, xT_made, xT_copied = sem("xq_ready"), sem("xT_made"), sem("xT_copied")
        gate_made, up_made, g_ready, h_ready, hs_ready = sem("gate_made"), sem("up_made"), sem("g_ready"), sem("h_ready"), sem("hs_ready")
        hr_ready, hq_ready, hT_made, hT_copied = sem("hr_ready"), sem("hq_ready"), sem("hT_made"), sem("hT_copied")
        res_added = sem("res_added")
        down_made, var_ready, rstd_ready, y_ready = sem("down_made"), sem("var_ready"), sem("rstd_ready"), sem("y_ready")
        chain, pool_chain = sem("chain"), sem("pool_chain")
        block = st.block()

        def tiles(eng, tile, link=None):
            in_turns(eng, tile, NT // BT, BT, (-2, -1, 0, 1, 2), link)

        last_tile = (NT // BT - 1, BT - 1)

        @block.sync
        def _(sp):
            for dst, src in ((ident[:, :], ident_d), (wgu_f[:, 0], wgu_d[0].rearrange("(c p) i -> p c i", p=P)),
                             (wgu_f[:, 1], wgu_d[1].rearrange("(c p) i -> p c i", p=P)),
                             (wd_f[:, :, :], wd_d.rearrange("(c p) f -> p c f", p=P))):
                sp.dma_start(dst, src).then_inc(w_loaded, 16)
            for b in range(4):
                sp.dma_start(x[:, b], batch_tiles(x_in, b)).then_inc(x_loaded[b], 16)
            for p in range(2):
                sp.sem_inc(y_stored[p], 16)

            def store(j, b):
                sp.wait_ge(y_ready, BT * j + 2 * (b + 1))
                sp.dma_start(batch_tiles(x_out, 4 * j + b), y[:, b % 2]).then_inc(y_stored[b % 2], 16)

            with sp.Fori(0, B // 4 - 1) as j:
                for b in range(4):
                    store(j, b)
                    sp.dma_start(x[:, b], batch_tiles(x_in, 4 * j + (b + 4))).then_inc(x_loaded[b], 16)
            for b in range(4):
                store(B // 4 - 1, b)
            for p in range(2):
                sp.wait_ge(y_stored[p], 16 * (B // 2 + 1))

        @block.tensor
        def _(pe):
            def turn_x(j, k):
                pe.wait_ge(xq_ready, BT * j + (k + 1))
                for c in range(C):
                    last = pe.transpose(px[:, c, :], xq[:, k % 2, c * P:(c + 1) * P], identb[:, :])
                last.then_inc(xT_made, 1)

            def gate_up(j, k):
                pe.wait_ge(xT_copied, BT * j + (k + 1))
                pe.wait_ge(h_ready, BT * j + (k + 1))
                for m, out, done in ((0, pgate, gate_made), (1, pup, up_made)):
                    for half in range(2):
                        for c in range(C):
                            last = pe.matmul(out[:, half * 512:(half + 1) * 512], xT[:, k % 2, c, :],
                                             wgu[:, m, c, half * 512:(half + 1) * 512], start=(c == 0), stop=(c == C - 1))
                    last.then_inc(done, 1)

            def turn_h(j, k):
                pe.wait_ge(hq_ready, BT * j + (k + 1))
                for c in range(IC):
                    last = pe.transpose(ph[:, c, :], hq[:, c * P:(c + 1) * P], identb[:, :])
                last.then_inc(hT_made, 1)

            def down(j, k):
                pe.wait_ge(hT_copied, BT * j + (k + 1))
                pe.wait_ge(res_added, BT * j + (k + 1))
                for c in range(IC):
                    last = pe.matmul(pd[:, 0:D], hT[:, c, :], wd[:, c, :], start=(c == 0), stop=(c == IC - 1))
                last.then_inc(down_made, 1)

            pe.wait_ge(wsum_ready, 1)
            pe.matmul(pd[:, 0:3], ones[:, :], wsum[:, :], start=True, stop=True).then_inc(wtotal_made, 1)
            pe.wait_ge(setup_done, 1)
            turn_x(0, 0)
            gate_up(0, 0)
            turn_x(0, 1)

            def tile(two_before, before, this, nxt, after):
                if nxt is not None:
                    gate_up(*nxt)
                if before is not None:
                    down(*before)
                if after is not None:
                    turn_x(*after)
                turn_h(*this)

            tiles(pe, tile)
            down(*last_tile)

        @block.scalar
        def _(act):
            def copy_x(j, k):
                act.wait_ge(xT_made, BT * j + (k + 1))
                act.activation(xT[:, k % 2], px[:, :, :], ACT.Copy).then_inc(xT_copied, 1)

            def gate(j, k):
                act.wait_ge(gate_made, BT * j + (k + 1))
                act.activation(g[:, :], pgate[:, :], ACT.Silu, scale=fgu[:, k % 2, 0:1]).then_inc(g_ready, 1)

            def scale_h(j, k):
                act.wait_ge(hs_ready, BT * j + (k + 1))
                act.activation(hr[:, :], h[:, :], ACT.Copy, scale=scale[:, 0:1], bias=ROUND).then_inc(hr_ready, 1)

            def copy_h(j, k):
                act.wait_ge(hT_made, BT * j + (k + 1))
                act.activation(hT[:, :, :], ph[:, :, :], ACT.Copy).then_inc(hT_copied, 1)

            def tile(two_before, before, this, nxt, after):
                if nxt is not None:
                    gate(*nxt)
                scale_h(*this)
                if after is not None:
                    copy_x(*after)
                copy_h(*this)

            act.wait_ge(setup_done, 1)
            copy_x(0, 0)
            gate(0, 0)
            copy_x(0, 1)
            tiles(act, tile)

        @block.gpsimd
        def _(pool):
            link = Chain(pool, pool_chain, BT)
            pool.memset(eps[:, :], LN_EPS)
            link(pool.memset(minus_half[:, :], -0.5))
            link.begin(0)
            with pool.Fori(0, NT // BT) as j:
                link.turn = j
                for k in range(BT):
                    pool.wait_ge(var_ready, BT * j + (k + 1))
                    link(pool.tensor_tensor(veps[:, :], mv[:, k % 2, 1:2], eps[:, :], ALU.add))
                    pool.tensor_tensor(rstd[:, k % 2:k % 2 + 1], veps[:, :], minus_half[:, :], ALU.pow).then_inc(rstd_ready, 1)
            link.end(NT // BT)

        @block.vector
        def _(dve):
            def x_of(k):
                return x[:, k // 2, k % 2, :]

            def x_top(j, k):
                if k % 2 == 0:
                    dve.wait_ge(x_loaded[k // 2], 16 * j + 16)
                return dve.tensor_reduce(top[:, k % 2, 1:2], x_of(k), AX.X, ALU.max, apply_absolute_value=True)

            def scales(p, cols):
                link(dve.tensor_scalar(top[:, p, cols], top[:, p, cols], FLOOR, None, ALU.max))
                dve.tensor_scalar(fgu[:, p, :], wm127[:, 0:2], top[:, p, 1:2], None, ALU.mult)
                if cols.start == 0:
                    dve.tensor_tensor(fd[:, p:p + 1], wm127[:, 2:3], top[:, p, 0:1], ALU.mult)
                link(dve.reciprocal(scale[:, cols], top[:, p, cols]))
                link(dve.tensor_scalar(scale[:, cols], scale[:, cols], 127.0, None, ALU.mult))

            def quantize_x(j, k):
                link(dve.tensor_scalar(xr[:, :], x_of(k), scale[:, 1:2], ROUND, ALU.mult, ALU.add))
                dve.tensor_scalar(xq[:, k % 2, :], xr[:, :], ROUND, 127.0, ALU.subtract, ALU.min).then_inc(xq_ready, 1)

            def first_x(j, k):
                link(x_top(j, k))
                scales(k % 2, slice(1, 2))
                quantize_x(j, k)

            def hidden(this, after):
                j, k = this
                n, p = BT * j + (k + 1), k % 2
                dve.wait_ge(g_ready, n)
                dve.wait_ge(up_made, n)
                link(dve.scalar_tensor_tensor(out=h[:, :], in0=pup[:, :], scalar=fgu[:, p, 1:2], in1=g[:, :],
                                              op0=ALU.mult, op1=ALU.mult))
                dve.sem_inc(h_ready, 1)
                last = dve.tensor_reduce(top[:, p, 0:1], h[:, :], AX.X, ALU.max, apply_absolute_value=True)
                if after is not None:
                    last = x_top(*after)
                link(last)
                scales(p, slice(0, 2))
                dve.sem_inc(hs_ready, 1)

            def quantize_h(j, k):
                dve.wait_ge(hr_ready, BT * j + (k + 1))
                dve.tensor_scalar(hq[:, :], hr[:, :], ROUND, 127.0, ALU.subtract, ALU.min).then_inc(hq_ready, 1)

            def residual(j, k):
                p = k % 2
                dve.wait_ge(down_made, BT * j + (k + 1))
                link(dve.scalar_tensor_tensor(out=r[:, p, :], in0=pd[:, 0:D], scalar=fd[:, p:p + 1],
                                              in1=x[:, k // 2, k % 2, :], op0=ALU.mult, op1=ALU.add))
                dve.sem_inc(res_added, 1)
                link(dve.bn_stats(stats[:, p, :], r[:, p, :]))
                dve.memset(spacer[:, :], 0.0)
                dve.bn_aggr(mv[:, p, :], stats[:, p, :]).then_inc(var_ready, 1)

            def finish(j, k):
                p, b = k % 2, k // 2
                dve.wait_ge(rstd_ready, BT * j + (k + 1))
                if p == 0:
                    dve.wait_ge(y_stored[b % 2], 32 * j + 16 * (b // 2 + 1))
                dve.tensor_scalar(y[:, b % 2, p, :], r[:, p, :], mv[:, p, 0:1], rstd[:, p:p + 1],
                                  ALU.subtract, ALU.mult).then_inc(y_ready, 1)

            link = Chain(dve, chain, BT * (6 + 2))
            dve.memset(ones[:, :], 1.0)
            dve.wait_ge(w_loaded, 64)
            dve.tensor_copy(identb[:, :], ident[:, :])
            weights = ((wgu_f[:, 0].rearrange("p c i -> p (c i)"), wgu[:, 0].rearrange("p c i -> p (c i)")),
                       (wgu_f[:, 1].rearrange("p c i -> p (c i)"), wgu[:, 1].rearrange("p c i -> p (c i)")),
                       (wd_f[:, :, :].rearrange("p c i -> p (c i)"), wd[:, :, :].rearrange("p c i -> p (c i)")))
            for m, (w, _) in enumerate(weights):
                last = dve.tensor_reduce(wsum[:, m:m + 1], w, AX.X, ALU.add, apply_absolute_value=True)
            last.then_inc(wsum_ready, 1)
            dve.wait_ge(wtotal_made, 1)
            link(dve.tensor_scalar(wmean[:, :], pd[:, 0:3], 1.0 / (I * D), FLOOR, ALU.mult, ALU.max))
            dve.tensor_scalar(wm127[:, :], wmean[:, :], 1.0 / 127.0, None, ALU.mult)
            link(dve.reciprocal(wscale[:, :], wmean[:, :]))
            for m, (w, _) in enumerate(weights):
                last = dve.tensor_scalar(w, w, wscale[:, m:m + 1], ROUND, ALU.mult, ALU.add)
            link(last)
            for m, (w, _) in enumerate(weights):
                last = dve.tensor_scalar(w, w, ROUND, 1.0, ALU.subtract, ALU.min)
            link(last)
            for w, q in weights:
                last = dve.tensor_scalar(q, w, -1.0, None, ALU.max)
            link(last)
            dve.sem_inc(setup_done, 2)
            dve.sem_inc(h_ready, 1)
            dve.sem_inc(res_added, 1)
            first_x(0, 0)
            first_x(0, 1)

            def tile(two_before, before, this, nxt, after):
                hidden(this, after)
                if after is not None:
                    quantize_x(*after)
                if two_before is not None:
                    finish(*two_before)
                quantize_h(*this)
                if before is not None:
                    residual(*before)

            tiles(dve, tile, link)
            finish(last_tile[0], last_tile[1] - 1)
            residual(*last_tile)
            finish(*last_tile)


STAGES = 6


def decoder(nc, a, out):
    scratch = [nc.dram_tensor(f"act{n}", [B, S, D], fp32, kind="Internal").ap() for n in range(6)]
    acts = [a["x"], *scratch][:STAGES] + [out]
    linear_attention(nc, acts[0], acts[1], a["L0_attn_WqT"], a["L0_attn_bq"], a["L0_attn_WkvT"], a["L0_attn_bkv"],
                     a["L0_attn_WoT"], a["L0_attn_bo"], a["ident"], a["head_blocks"])
    if STAGES > 1:
        cross_attention(nc, "xa0", acts[1], acts[2], a["ctx"], a["L0_xattn_wq"], a["L0_xattn_wkv"], a["L0_xattn_wproj"],
                        a["L0_xattn_bproj"], a["ident"], a["head_columns"], mask_d=a["mask"],
                        norms_d=[a["L0_xattn_" + n] for n in ("g_x", "b_x", "g_kv", "b_kv")])
    if STAGES > 2:
        expert_attention(nc, acts[2], acts[3], a["L0_ffn_Wg"], a["L0_ffn_Wq"], a["L0_ffn_Wkv"], a["L0_ffn_Wo"], a["L0_ffn_bqkv"],
                         a["L0_ffn_bo"], a["L0_ffn_ln"], a["ident"], a["batch_iota"], a["position_mask"], a["sum4"], a["pick4"])
    if STAGES > 3:
        ct_dram = nc.dram_tensor("ma_ct_dram", [2, 33, 2 * S], fp32, kind="Internal").ap()
        mamba(nc, acts[3], acts[4], ct_dram, a["L1_attn_g"], a["L1_attn_WinT"], a["L1_attn_WoutT"], a["L1_attn_conv"],
              a["L1_attn_WxT"], a["L1_attn_dtp"], a["L1_attn_Alog"], a["ident"])
    if STAGES > 4:
        cross_attention(nc, "xa1", acts[4], acts[5], a["ctx"], a["L1_xattn_WqT"], a["L1_xattn_WkvT"], a["L1_xattn_WoT"],
                        a["L1_xattn_bo"], a["ident"], a["head_columns"],
                        bq_d=a["L1_xattn_bq"], bk_d=a["L1_xattn_bk"], bv_d=a["L1_xattn_bv"])
    if STAGES > 5:
        bit_ffn(nc, acts[5], acts[6], a["L1_ffn_wguT"], a["L1_ffn_wdT"], a["ident"])


def kernel(**inputs):
    import numpy as _np
    import concourse.bacc as _bacc
    from concourse import mybir as _mybir
    from concourse.bass_utils import run_bass_kernel_spmd as _run

    def columns(v):
        return v.reshape(-1, P).T

    src = {name: _np.asarray(a) for name, a in inputs.items()}
    lay = {"x": src["x"]}
    lay["L0_attn_WqT"] = src["L0_attn_Wq"].T
    lay["L0_attn_bq"] = columns(src["L0_attn_bq"])
    lay["L0_attn_WkvT"] = _np.concatenate([src["L0_attn_Wk"].T, src["L0_attn_Wv"].T], axis=1)
    lay["L0_attn_bkv"] = _np.concatenate([src["L0_attn_bk"], src["L0_attn_bv"]])
    lay["L0_attn_WoT"] = src["L0_attn_Wo"].T
    lay["L0_attn_bo"] = src["L0_attn_bo"]
    lay["ctx"] = src["ctx_1024"]
    lay["mask"] = src["mask_BxS2_ik0"]
    lay["L0_xattn_wq"], lay["L0_xattn_wkv"], lay["L0_xattn_wproj"] = src["L0_xattn_w_q"], src["L0_xattn_w_kv"], src["L0_xattn_w_proj"]
    lay["L0_xattn_bproj"] = src["L0_xattn_b_proj"]
    for n in ("g_x", "b_x", "g_kv", "b_kv"):
        lay["L0_xattn_" + n] = columns(src["L0_xattn_" + n])
    lay["L1_xattn_WqT"] = src["L1_xattn_Wq"].T
    lay["L1_xattn_WkvT"] = _np.concatenate([src["L1_xattn_Wk"].T, src["L1_xattn_Wv"].T], axis=1)
    lay["L1_xattn_WoT"] = src["L1_xattn_Wo"].T
    lay["L1_xattn_bq"], lay["L1_xattn_bk"] = columns(src["L1_xattn_bq"]), columns(src["L1_xattn_bk"])
    lay["L1_xattn_bv"], lay["L1_xattn_bo"] = src["L1_xattn_bv"], src["L1_xattn_bo"]
    for n in ("Wg", "Wq", "Wkv", "Wo"):
        lay["L0_ffn_" + n] = src["L0_ffn_" + n]
    bqkv = _np.zeros((H, P, 2), _np.float32)
    bqkv[:, :, 0] = src["L0_ffn_bkv"]
    bqkv[:, 0:64, 1] = src["L0_ffn_bq"]
    lay["L0_ffn_bqkv"] = bqkv
    lay["L0_ffn_bo"] = columns(src["L0_ffn_bo"])
    lay["L0_ffn_ln"] = _np.stack([src["L0_ffn_ln_g"], src["L0_ffn_ln_b"]])
    lay["L1_attn_g"] = columns(src["L1_attn_g"])
    lay["L1_attn_WinT"], lay["L1_attn_WoutT"], lay["L1_attn_WxT"] = src["L1_attn_W_in"].T, src["L1_attn_W_out"].T, src["L1_attn_W_x"].T
    lay["L1_attn_conv"] = _np.concatenate([src["L1_attn_conv_w"], src["L1_attn_conv_b"][:, None]], 1).reshape(-1, P, 5).transpose(1, 0, 2)
    lay["L1_attn_dtp"] = _np.stack([columns(v) for v in (src["L1_attn_W_dt"][:, 0], src["L1_attn_b_dt"], src["L1_attn_D"])], axis=1)
    lay["L1_attn_Alog"] = src["L1_attn_A_log"].reshape(-1, P, src["L1_attn_A_log"].shape[1]).transpose(1, 0, 2)
    lay["L1_ffn_wguT"] = _np.stack([src["L1_ffn_w_gate"].T, src["L1_ffn_w_up"].T])
    lay["L1_ffn_wdT"] = src["L1_ffn_w_down"].T
    lay["ident"] = _np.eye(P, dtype=_np.float32)
    lay["batch_iota"] = _np.tile(_np.arange(B, dtype=_np.float32), (P, 1))
    lay["position_mask"] = _np.kron(_np.eye(P // B), _np.ones((B, 1))).astype(_np.float32)
    lay["sum4"] = _np.tile(_np.eye(4, P, dtype=_np.float32), (64, 1, 1))
    lay["pick4"] = _np.repeat(_np.eye(4, dtype=_np.float32)[:, :, None], P, axis=2)
    lay["head_columns"] = _np.tile(_np.kron(_np.eye(P // 2 // DH), _np.ones((DH, 1))), (2, 1)).astype(_np.float32)
    lay["head_blocks"] = _np.kron(_np.eye(P // DH), _np.ones((DH, DH))).astype(_np.float32)

    nc = _bacc.Bacc("TRN2", target_bir_lowering=False, num_devices=1)
    arrays, args = {}, {}
    for name, a in lay.items():
        arrays[f"in_{name}"] = a = _np.ascontiguousarray(a)
        args[name] = nc.dram_tensor(f"in_{name}", a.shape, _mybir.dt.from_np(a.dtype), kind="ExternalInput").ap()
    out = nc.dram_tensor("out_0_dram", (B, S, D), _mybir.dt.float32, kind="ExternalOutput").ap()
    decoder(nc, args, out)
    r = _run(nc, [arrays], core_ids=[0])
    return r.results[0]["out_0_dram"]
```
